# Optimizing a Trainium2 kernel written in Bass

```python
import numpy as np
import jax
import jax.numpy as jnp

def _softmax(x, axis=-1):
    return jax.nn.softmax(x, axis=axis)

def _gelu(x):
    return jax.nn.gelu(x, approximate=True)

def _silu(x):
    return jax.nn.silu(x)

def _sigmoid(x):
    return jax.nn.sigmoid(x)

def _layernorm(x, axis=-1, eps=1e-05):
    m = jnp.mean(x, axis=axis, keepdims=True)
    v = jnp.var(x, axis=axis, keepdims=True)
    return (x - m) / jnp.sqrt(v + eps)

def _scatter_add(tgt, idx, src, axis=0):
    return tgt.at[idx].add(src)

def _segment_sum(src, seg, n):
    return jax.ops.segment_sum(src, seg, n)
kernel_name = 'mk_audio_tower_d2_tok_audfeat1024_r4_1aecbc'

def setup_inputs(seed: int=0):
    np.random.seed(seed)
    _w = jnp.asarray

    def _rec_inputs():
        import jax
        import jax.numpy as jnp
        _rk = jax.random.key(seed)
        x = -0.000125008 + 0.999885 * jax.random.normal(jax.random.fold_in(_rk, 1), (16, 256, 256), jnp.float32)
        return x
    x = _rec_inputs()

    def _L0_tok_setup():
        import jax, jax.numpy as jnp
        import numpy as np
        D_MODEL = 256
        STRIDE = 2
        KERNEL = 2
        INIT_STD = 0.02
        EPS = 1e-05
        key = jax.random.key(seed)
        k1, k2 = jax.random.split(key)
        hidden_states = jax.random.normal(k1, (4, 2048, D_MODEL), dtype=jnp.float32)
        conv_w = INIT_STD * jax.random.normal(k2, (D_MODEL, D_MODEL, KERNEL), dtype=jnp.float32)
        conv_b = jnp.zeros((D_MODEL,), dtype=jnp.float32)
        ln_gamma = jnp.ones((D_MODEL,), dtype=jnp.float32)
        ln_beta = jnp.zeros((D_MODEL,), dtype=jnp.float32)
        return {'hidden_states': hidden_states, 'conv_w': conv_w, 'conv_b': conv_b, 'ln_gamma': ln_gamma, 'ln_beta': ln_beta}
    _L0_tok_all = _L0_tok_setup()
    _L0_tok_in = {k: v for k, v in _L0_tok_all.items() if k in ('conv_w', 'conv_b', 'ln_gamma', 'ln_beta')}
    del _L0_tok_all

    def _L0_attn_setup():
        import jax, jax.numpy as jnp
        import numpy as np
        D_MODEL = 256
        NHEAD = 16
        HEAD_DIM = D_MODEL // NHEAD
        WINDOW = 64
        key = jax.random.key(seed)
        ks = jax.random.split(key, 5)
        B, S = (1, 1024)
        x = jax.random.normal(ks[0], (B, S, D_MODEL), dtype=jnp.float32)
        scale = 0.02
        Wq = jax.random.normal(ks[1], (D_MODEL, D_MODEL), dtype=jnp.float32) * scale
        Wk = jax.random.normal(ks[2], (D_MODEL, D_MODEL), dtype=jnp.float32) * scale
        Wv = jax.random.normal(ks[3], (D_MODEL, D_MODEL), dtype=jnp.float32) * scale
        Wo = jax.random.normal(ks[4], (D_MODEL, D_MODEL), dtype=jnp.float32) * scale
        return {'x': x, 'Wq': Wq, 'Wk': Wk, 'Wv': Wv, 'Wo': Wo}
    _L0_attn_all = _L0_attn_setup()
    _L0_attn_in = {k: v for k, v in _L0_attn_all.items() if k in ('Wq', 'Wk', 'Wv', 'Wo')}
    del _L0_attn_all

    def _L0_ffn_setup():
        import jax, jax.numpy as jnp
        import numpy as np
        B, S, D = (1, 512, 256)
        F = 352
        E = 16
        K = 2
        CAP_FACTOR = 1.25

        def _mlp(h, wg, wu, wd):
            return jax.nn.silu(h @ wg) * (h @ wu) @ wd
        key = jax.random.key(seed)
        ks = jax.random.split(key, 10)
        sd = 0.02
        return {'x': jax.random.normal(ks[0], (B, S, D), jnp.float32), 'router_w': jax.random.normal(ks[1], (D, E), jnp.float32) * sd, 'router_b': jnp.zeros((E,), jnp.float32), 'w_gate': jax.random.normal(ks[2], (E, D, F), jnp.float32) * sd, 'w_up': jax.random.normal(ks[3], (E, D, F), jnp.float32) * sd, 'w_down': jax.random.normal(ks[4], (E, F, D), jnp.float32) * sd, 'sw_gate': jax.random.normal(ks[5], (D, F), jnp.float32) * sd, 'sw_up': jax.random.normal(ks[6], (D, F), jnp.float32) * sd, 'sw_down': jax.random.normal(ks[7], (F, D), jnp.float32) * sd}
    _L0_ffn_all = _L0_ffn_setup()
    _L0_ffn_in = {k: v for k, v in _L0_ffn_all.items() if k in ('router_w', 'router_b', 'w_gate', 'w_up', 'w_down', 'sw_gate', 'sw_up', 'sw_down')}
    del _L0_ffn_all

    def _L1_attn_setup():
        import jax, jax.numpy as jnp
        import numpy as np
        HIDDEN = 256
        HEADS = 16
        CHUNK = 128
        NEG_INF = -10000000000.0
        key = jax.random.key(seed)
        k1, k2, k3 = jax.random.split(key, 3)
        B, S = (2, 1024)
        x = jax.random.normal(k1, (B, S, HIDDEN), dtype=jnp.float32)
        w_qkv = jax.random.normal(k2, (HIDDEN, 3 * HIDDEN), dtype=jnp.float32) / np.sqrt(HIDDEN).astype(np.float32)
        w_out = jax.random.normal(k3, (HIDDEN, HIDDEN), dtype=jnp.float32) / np.sqrt(HIDDEN).astype(np.float32)
        return {'x': x, 'w_qkv': w_qkv, 'w_out': w_out}
    _L1_attn_all = _L1_attn_setup()
    _L1_attn_in = {k: v for k, v in _L1_attn_all.items() if k in ('w_qkv', 'w_out')}
    del _L1_attn_all

    def _L1_ffn_setup():
        import jax, jax.numpy as jnp
        import numpy as np
        D = 256
        H = 1024
        E = 64
        K = 3
        B, S = (2, 512)
        C = 128
        key = jax.random.key(seed)
        ks = jax.random.split(key, 6)
        s = 0.02
        return {'x': jax.random.normal(ks[0], (B, S, D), jnp.float32), 'gate_w': jax.random.normal(ks[1], (D, E), jnp.float32) * s, 'gate_b': jnp.zeros((E,), jnp.float32), 'w1': jax.random.normal(ks[2], (E, D, H), jnp.float32) * s, 'b1': jnp.zeros((E, H), jnp.float32), 'w2': jax.random.normal(ks[3], (E, H, D), jnp.float32) * s, 'b2': jnp.zeros((E, D), jnp.float32)}
    _L1_ffn_all = _L1_ffn_setup()
    _L1_ffn_in = {k: v for k, v in _L1_ffn_all.items() if k in ('gate_w', 'gate_b', 'w1', 'b1', 'w2', 'b2')}
    del _L1_ffn_all
    return {'x': x, 'L0_tok_conv_w': _L0_tok_in['conv_w'], 'L0_tok_conv_b': _L0_tok_in['conv_b'], 'L0_tok_ln_gamma': _L0_tok_in['ln_gamma'], 'L0_tok_ln_beta': _L0_tok_in['ln_beta'], 'L0_attn_Wq': _L0_attn_in['Wq'], 'L0_attn_Wk': _L0_attn_in['Wk'], 'L0_attn_Wv': _L0_attn_in['Wv'], 'L0_attn_Wo': _L0_attn_in['Wo'], 'L0_ffn_router_w': _L0_ffn_in['router_w'], 'L0_ffn_router_b': _L0_ffn_in['router_b'], 'L0_ffn_w_gate': _L0_ffn_in['w_gate'], 'L0_ffn_w_up': _L0_ffn_in['w_up'], 'L0_ffn_w_down': _L0_ffn_in['w_down'], 'L0_ffn_sw_gate': _L0_ffn_in['sw_gate'], 'L0_ffn_sw_up': _L0_ffn_in['sw_up'], 'L0_ffn_sw_down': _L0_ffn_in['sw_down'], 'L1_attn_w_qkv': _L1_attn_in['w_qkv'], 'L1_attn_w_out': _L1_attn_in['w_out'], 'L1_ffn_gate_w': _L1_ffn_in['gate_w'], 'L1_ffn_gate_b': _L1_ffn_in['gate_b'], 'L1_ffn_w1': _L1_ffn_in['w1'], 'L1_ffn_b1': _L1_ffn_in['b1'], 'L1_ffn_w2': _L1_ffn_in['w2'], 'L1_ffn_b2': _L1_ffn_in['b2']}

def reference(x, L0_tok_conv_w, L0_tok_conv_b, L0_tok_ln_gamma, L0_tok_ln_beta, L0_attn_Wq, L0_attn_Wk, L0_attn_Wv, L0_attn_Wo, L0_ffn_router_w, L0_ffn_router_b, L0_ffn_w_gate, L0_ffn_w_up, L0_ffn_w_down, L0_ffn_sw_gate, L0_ffn_sw_up, L0_ffn_sw_down, L1_attn_w_qkv, L1_attn_w_out, L1_ffn_gate_w, L1_ffn_gate_b, L1_ffn_w1, L1_ffn_b1, L1_ffn_w2, L1_ffn_b2):
    import jax
    import jax.numpy as jnp

    def _L0_tok_ref(hidden_states, conv_w, conv_b, ln_gamma, ln_beta):
        import jax, jax.numpy as jnp
        import numpy as np
        D_MODEL = 256
        STRIDE = 2
        KERNEL = 2
        INIT_STD = 0.02
        EPS = 1e-05
        B, L, D = hidden_states.shape
        pad_len = -L % STRIDE
        if pad_len:
            hidden_states = jnp.pad(hidden_states, ((0, 0), (0, pad_len), (0, 0)))
            L = L + pad_len
        xb = hidden_states.reshape(B, L // STRIDE, STRIDE, D)
        x = jnp.einsum('btki,oik->bto', xb, conv_w) + conv_b
        x = x + xb.mean(axis=2)
        mu = x.mean(axis=-1, keepdims=True)
        var = jnp.mean(jnp.square(x - mu), axis=-1, keepdims=True)
        x = (x - mu) * jax.lax.rsqrt(var + EPS) * ln_gamma + ln_beta
        return x

    def _L0_attn_ref(x, Wq, Wk, Wv, Wo):
        import jax, jax.numpy as jnp
        import numpy as np
        D_MODEL = 256
        NHEAD = 16
        HEAD_DIM = D_MODEL // NHEAD
        WINDOW = 64
        B, S, D = x.shape
        H, hd, W = (NHEAD, HEAD_DIM, WINDOW)
        q = (x @ Wq.T).reshape(B, S, H, hd).transpose(0, 2, 1, 3)
        k = (x @ Wk.T).reshape(B, S, H, hd).transpose(0, 2, 1, 3)
        v = (x @ Wv.T).reshape(B, S, H, hd).transpose(0, 2, 1, 3)
        qpos = jnp.arange(S)
        offsets = jnp.arange(-W + 1, 1)
        key_idx = qpos[:, None] + offsets[None, :]
        valid = (key_idx >= 0) & (key_idx < S)
        key_idx = jnp.clip(key_idx, 0, S - 1)
        kw = jnp.take(k, key_idx, axis=2)
        vw = jnp.take(v, key_idx, axis=2)
        scores = jnp.einsum('bhsd,bhswd->bhsw', q, kw) / hd ** 0.5
        scores = jnp.where(valid[None, None, :, :], scores, -jnp.inf)
        attn = jax.nn.softmax(scores, axis=-1)
        out = jnp.einsum('bhsw,bhswd->bhsd', attn, vw)
        out = out.transpose(0, 2, 1, 3).reshape(B, S, D)
        return out @ Wo.T

    def _L0_ffn_ref(x, router_w, router_b, w_gate, w_up, w_down, sw_gate, sw_up, sw_down):
        import jax, jax.numpy as jnp
        import numpy as np
        B, S, D = (1, 512, 256)
        F = 352
        E = 16
        K = 2
        CAP_FACTOR = 1.25

        def _mlp(h, wg, wu, wd):
            return jax.nn.silu(h @ wg) * (h @ wu) @ wd
        b, s, d = x.shape
        N = b * s
        NK = N * K
        C = int(np.ceil(CAP_FACTOR * NK / E))
        x_tokens = x.reshape(N, d)
        logits = x_tokens @ router_w + router_b
        probs = jax.nn.softmax(logits, axis=-1)
        vals, idx = jax.lax.top_k(probs, K)
        vals = vals / (jnp.sum(vals, axis=-1, keepdims=True) + 1e-09)
        idx_flat = idx.reshape(NK)
        vals_flat = vals.reshape(NK)
        oh_e = jax.nn.one_hot(idx_flat, E, dtype=x.dtype)
        pos = (jnp.cumsum(oh_e, axis=0) * oh_e).sum(axis=1) - 1
        within = (pos < C).astype(x.dtype)
        pos_c = jnp.clip(pos, 0, C - 1).astype(jnp.int32)
        token_ids = jnp.arange(NK) // K
        x_pair = x_tokens[token_ids] * within[:, None]
        expert_inputs = jnp.zeros((E, C, d), x.dtype).at[idx_flat, pos_c].add(x_pair)
        expert_outputs = jax.vmap(_mlp)(expert_inputs, w_gate, w_up, w_down)
        gathered = expert_outputs[idx_flat, pos_c] * (vals_flat * within)[:, None]
        output_tokens = gathered.reshape(N, K, d).sum(axis=1)
        return x + _mlp(x, sw_gate, sw_up, sw_down) + output_tokens.reshape(b, s, d)

    def _L1_attn_ref(x, w_qkv, w_out):
        import jax, jax.numpy as jnp
        import numpy as np
        HIDDEN = 256
        HEADS = 16
        CHUNK = 128
        NEG_INF = -10000000000.0
        B, S, _ = x.shape
        H, D = (HEADS, HIDDEN // HEADS)
        qkv = (x @ w_qkv).reshape(B, S, 3, H, D)
        q, k, v = (qkv[:, :, 0], qkv[:, :, 1], qkv[:, :, 2])
        scale = jnp.sqrt(jnp.asarray(D, x.dtype))
        n_chunks = S // CHUNK
        q_chunks = q.reshape(B, n_chunks, CHUNK, H, D).transpose(1, 0, 2, 3, 4)
        starts = jnp.arange(n_chunks) * CHUNK

        def step(carry, inp):
            qc, start = inp
            scores = jnp.einsum('bqhd,bkhd->bhqk', qc, k) / scale
            causal = jnp.arange(CHUNK)[:, None] + start >= jnp.arange(S)[None, :]
            scores = jnp.where(causal[None, None], scores, NEG_INF)
            attn = jax.nn.softmax(scores, axis=-1)
            out_c = jnp.einsum('bhqk,bkhd->bqhd', attn, v).reshape(B, CHUNK, H * D)
            return (carry, out_c)
        _, outs = jax.lax.scan(step, None, (q_chunks, starts))
        out = outs.transpose(1, 0, 2, 3).reshape(B, S, H * D)
        return out @ w_out

    def _L1_ffn_ref(x, gate_w, gate_b, w1, b1, w2, b2):
        import jax, jax.numpy as jnp
        import numpy as np
        D = 256
        H = 1024
        E = 64
        K = 3
        B, S = (2, 512)
        C = 128
        xf = x.reshape(-1, D)
        T = xf.shape[0]
        logits = xf @ gate_w + gate_b
        top_l, top_i = jax.lax.top_k(logits, K)
        gates = jax.nn.softmax(top_l, axis=-1)
        fe = top_i.reshape(-1)
        fg = gates.reshape(-1)
        tok = jnp.repeat(jnp.arange(T), K)
        oh = jax.nn.one_hot(fe, E, dtype=jnp.int32)
        pos = (jnp.cumsum(oh, axis=0) * oh).sum(-1) - 1
        valid = pos < C
        buf = jnp.zeros((E, C, D), x.dtype).at[fe, pos].set(xf[tok], mode='drop')
        h = jax.nn.gelu(jnp.einsum('ecd,edh->ech', buf, w1) + b1[:, None, :], approximate=False)
        y = jnp.einsum('ech,ehd->ecd', h, w2) + b2[:, None, :]
        rows = y[fe, jnp.minimum(pos, C - 1)] * (fg * valid.astype(x.dtype))[:, None]
        out = jnp.zeros_like(xf).at[tok].add(rows)
        return out.reshape(x.shape)
    h = _L0_tok_ref(x, L0_tok_conv_w, L0_tok_conv_b, L0_tok_ln_gamma, L0_tok_ln_beta)
    h = h + _L0_attn_ref(_layernorm(h, axis=-1), L0_attn_Wq, L0_attn_Wk, L0_attn_Wv, L0_attn_Wo)
    h = h + _L0_ffn_ref(_layernorm(h, axis=-1), L0_ffn_router_w, L0_ffn_router_b, L0_ffn_w_gate, L0_ffn_w_up, L0_ffn_w_down, L0_ffn_sw_gate, L0_ffn_sw_up, L0_ffn_sw_down)
    h = h + _L1_attn_ref(_layernorm(h, axis=-1), L1_attn_w_qkv, L1_attn_w_out)
    h = h + _L1_ffn_ref(_layernorm(h, axis=-1), L1_ffn_gate_w, L1_ffn_gate_b, L1_ffn_w1, L1_ffn_b1, L1_ffn_w2, L1_ffn_b2)
    return h

_drawn_inputs = setup_inputs


def setup_inputs(seed=0):
    import zlib

    import numpy as np

    out = dict(_drawn_inputs(seed))
    spreads = {'L0_tok_conv_b': (0.0, 0.1),
     'L0_tok_ln_gamma': (1.0, 0.2),
     'L0_tok_ln_beta': (0.0, 0.1),
     'L0_ffn_router_b': (0.0, 0.8),
     'L1_ffn_gate_b': (0.0, 0.39),
     'L1_ffn_b1': (0.0, 2.0),
     'L1_ffn_b2': (0.0, 1.382)}
    factors = {'L0_attn_Wq': 8.0,
     'L0_attn_Wk': 8.0,
     'L0_ffn_router_w': 7.962,
     'L0_ffn_w_gate': 7.416,
     'L0_ffn_w_up': 7.585,
     'L0_ffn_w_down': 7.506,
     'L0_ffn_sw_gate': 5.247,
     'L0_ffn_sw_up': 5.261,
     'L0_ffn_sw_down': 5.252,
     'L1_ffn_w1': 7.4,
     'L1_ffn_w2': 2.789}
    for name, (base, spread) in spreads.items():
        noise = np.random.default_rng([zlib.crc32(name.encode()), seed]).standard_normal(out[name].shape)
        drawn = base * np.exp(spread * noise) if base else spread * noise
        out[name] = jnp.asarray(drawn.astype(out[name].dtype))
    for name, factor in factors.items():
        out[name] = (out[name] * factor).astype(out[name].dtype)
    return out
```

```python
from contextlib import ExitStack

import concourse.bass as bass
from concourse import mybir

F32 = mybir.dt.float32
BF16 = mybir.dt.bfloat16
I32 = mybir.dt.int32
U32 = mybir.dt.uint32
ALU = mybir.AluOpType
ACT = mybir.ActivationFunctionType
AX = mybir.AxisListType

P = 128
D = 256
DC = D // P
HEADS = 16
HD = D // HEADS
WINDOW = 64
EPS = 1e-5
BANK = 512
SCALE = HD ** -0.5
HEADS_PER_BANK = BANK // P
SBANKS = HEADS // HEADS_PER_BANK
MASKED = -1e30
SKIP = 1 << 20
GATHER_SUM_EPS = 1e-9


def wait(eng, sem, count):
    if not isinstance(count, int) or count > 0:
        eng.wait_ge(sem, count)


def settle(eng, i):
    if not isinstance(i, int):
        eng.nop(nofuse=True)


class Chain:

    def __init__(self, eng, sem, call, steps):
        self.eng, self.sem, self.base, self.steps, self.n = eng, sem, call * steps, steps, 0

    def link(self, instruction):
        instruction.then_inc(self.sem, 1)
        self.n += 1
        self.eng.wait_ge(self.sem, self.base + self.n)

    def end(self):
        assert self.n == self.steps, (self.n, self.steps)


def loop(eng, count, body):
    body(0, True, count == 1)
    if count > 2:
        with eng.Fori(1, count - 1) as i:
            body(i, False, False)
    if count > 1:
        body(count - 1, False, True)


def loop_from(eng, start, count, body):
    body(start, False, False)
    with eng.Fori(start + 1, count - 1) as i:
        body(i, False, False)
    body(count - 1, False, True)


def over(ap, axis, shape):
    return ap.unsqueeze(axis).to_broadcast(shape)


class Layer:

    def __init__(self, sem, n):
        self.n = n
        self.x_loaded = sem(f"x_loaded_{n}")
        self.x_summed = sem(f"x_summed_{n}")
        self.score_full = sem(f"score_full_{n}")
        self.max_done = sem(f"max_done_{n}")
        self.exp_done = sem(f"exp_done_{n}")
        self.turn_full = sem(f"turn_full_{n}")
        self.turned = sem(f"turned_{n}")
        self.pv_done = sem(f"pv_done_{n}")
        self.inv_done = sem(f"inv_done_{n}")
        self.mix_done = sem(f"mix_done_{n}")
        self.back_full = sem(f"back_full_{n}")
        self.back_free = sem(f"back_free_{n}")
        self.scattered = sem(f"scattered_{n}")
        self.tok_biased = sem(f"tok_biased_{n}")
        self.tok_steps = sem(f"tok_steps_{n}")
        self.tok_normed = sem(f"tok_normed_{n}")
        self.tok_scaled = sem(f"tok_scaled_{n}")
        self.h_ready = sem(f"h_ready_{n}")
        self.normed_ready = sem(f"normed_ready_{n}")
        self.ffn_ready = sem(f"ffn_ready_{n}")
        self.residual = sem(f"residual_{n}")
        self.to_exp = sem(f"to_exp_{n}")
        self.from_exp = sem(f"from_exp_{n}")
        self.route_steps = sem(f"route_steps_{n}")
        self.chosen_ready = sem(f"chosen_ready_{n}")
        self.slot_steps = sem(f"slot_steps_{n}")
        self.scatter_ready = sem(f"scatter_ready_{n}")
        self.gates_ready = sem(f"gates_ready_{n}")
        self.index_ready = sem(f"index_ready_{n}")
        self.gathered = sem(f"gathered_{n}")
        self.add_steps = sem(f"add_steps_{n}")
        self.running_zero = sem(f"running_zero_{n}")
        self.input_added = sem(f"input_added_{n}")
        self.stat_steps = [sem(f"stat_steps_{n}{w}") for w in range(3)]
        self.moments_ready = [sem(f"moments_ready_{n}{w}") for w in range(3)]
        self.eps_added = [sem(f"eps_added_{n}{w}") for w in range(3)]
        self.rstd_ready = [sem(f"rstd_ready_{n}{w}") for w in range(3)]
        self.front_full = [sem(f"front_full_{n}{b}") for b in range(2)]
        self.front_free = [sem(f"front_free_{n}{b}") for b in range(2)]


def build(nc, a, out):
    B, TOK, _ = a["x"].shape
    S = TOK // 2
    PAIRS = B // 2
    NE0, _, F0 = a["L0_ffn_w_gate"].shape
    NE1, _, F1 = a["L1_ffn_w1"].shape
    K0, K1 = 2, 3
    N = B * S
    C0 = -(-5 * N * K0 // (4 * NE0))
    C1 = 128
    FT = [(j * P, min(P, F0 - j * P)) for j in range(-(-F0 // P))]
    CT = [(j * P, min(P, C0 - j * P)) for j in range(-(-C0 // P))]
    NFT, NCT = len(FT), len(CT)
    J1 = F1 // P
    assert S == P and C1 == P and B % 2 == 0 and NFT == 3 and NCT == 3

    ctx = ExitStack()
    with ctx:
        def sb(name, shape, dt=F32):
            return ctx.enter_context(nc.sbuf_tensor(name, shape, dt))

        def sem(name):
            return ctx.enter_context(nc.semaphore(name))

        rows0 = nc.dram_tensor("rows0", [NE0 * C0, D], F32, kind="Internal").ap()
        y0 = nc.dram_tensor("y0", [NE0 * C0, D], F32, kind="Internal").ap()
        rows1 = nc.dram_tensor("rows1", [NE1 * C1, D], F32, kind="Internal").ap()
        y1 = nc.dram_tensor("y1", [NE1 * C1, D], F32, kind="Internal").ap()

        bank = [ctx.enter_context(nc.psum_tensor(f"bank{n}", [P, BANK], F32)) for n in range(8)]
        score_bank, turn_bank, mix_bank = bank[0:2], bank[2:4], bank[4]
        front_bank, back_bank = bank[5:7], bank[7]

        ident = sb("ident", [P, P])
        ones_f = sb("ones_f", [P, P])
        zeros = sb("zeros", [P, BANK])
        mask0 = sb("mask0", [P, P])
        mask1 = sb("mask1", [P, P])
        before = sb("before", [P, P], BF16)
        ones_b = sb("ones_b", [P, P], BF16)
        parity = sb("parity", [P, 2])
        row_id = sb("row_id", [P, 2], I32)
        row_f = sb("row_f", [P, 1])
        half_neg = sb("half_neg", [P, 2])
        iota_e = sb("iota_e", [P, NE1])
        conv_wT = sb("conv_wT", [P, 2 * DC, D])
        wT0 = sb("wT0", [P, 4, DC, D])
        w_qkv = sb("w_qkv", [P, DC, 3 * D])
        w_out = sb("w_out", [P, DC, D])
        router0 = sb("router0", [P, DC, NE0])
        router1 = sb("router1", [P, DC, NE1])
        sw_gate = sb("sw_gate", [P, DC, F0])
        sw_up = sb("sw_up", [P, DC, F0])
        sw_down = sb("sw_down", [P, NFT, D])
        conv_b = sb("conv_b", [P, D])
        gamma = sb("gamma", [P, D])
        beta = sb("beta", [P, D])
        rb0 = sb("rb0", [P, NE0])
        rb1 = sb("rb1", [P, NE1])
        b1T = sb("b1T", [P, J1, NE1])
        b2 = sb("b2", [NE1, D])
        h = sb("h", [P, B, D])
        x_in = sb("x_in", [P, 2, 2 * D])
        x_sum = sb("x_sum", [P, 2, D])
        xT = sb("xT", [P, 2, 2 * DC, P])
        tok = sb("tok", [P, 2, D])
        normed = sb("normed", [P, 2, D])
        normedT = sb("normedT", [P, DC, 2 * P])
        qT = sb("qT", [P, DC, 2, P])
        kT = sb("kT", [P, DC, 2, 2, P])
        v = sb("v", [P, 2, D])
        probs = sb("probs", [P, 2, HEADS, P])
        probsT = sb("probsT", [P, SBANKS, BANK])
        neg_max = sb("neg_max", [P, 2, HEADS])
        exp_sum = sb("exp_sum", [P, 2, HEADS])
        exp_inv = sb("exp_inv", [P, 2, HEADS])
        mixed = sb("mixed", [P, 2, D])
        mixedT = sb("mixedT", [P, DC, 2 * P])
        ffn_in = sb("ffn_in", [P, 2, D])
        ffn_inT = sb("ffn_inT", [P, DC, 2 * P])
        gathered = sb("gathered", [P, 2, K1, D])
        stats = sb("stats", [P, 3, 2, 6])
        moments = sb("moments", [P, 3, 2, 2])
        rstd = sb("rstd", [P, 3, 2])
        var_eps = sb("var_eps", [P, 3, 2])
        logits = sb("logits", [P, 2, NE1])
        shifted = sb("shifted", [P, 2, NE1])
        gate_p = sb("gate_p", [P, 2, NE1])
        top_v = sb("top_v", [P, 2, 8])
        top_m = sb("top_m", [P, 2, 8])
        top_i = sb("top_i", [P, 2, 8], U32)
        top_f = sb("top_f", [P, 2, 8])
        rsmall = sb("rsmall", [P, 8, 2])
        onehot = sb("onehot", [P, K1, 2, NE1])
        chosen = sb("chosen", [P, 2, NE1], BF16)
        earlier = sb("earlier", [P, 2, NE1], BF16)
        running = sb("running", [P, NE1], BF16)
        count_sb = sb("count_sb", [P, 2, NE1])
        product = sb("product", [P, K1, 2, NE1])
        gates_e = sb("gates_e", [P, 2, NE1])
        gates_eT = sb("gates_eT", [NE1, 2 * P])
        posf = sb("posf", [P, K1, 2])
        slotf = sb("slotf", [P, K1, 2])
        tmpf = sb("tmpf", [P, K1, 2])
        validf = sb("validf", [P, K1, 2])
        weight = sb("weight", [P, K1, 2])
        scatter_i = sb("scatter_i", [P, K1, 2], I32)
        all_w = [sb(f"all_w{n}", [P, K1, B]) for n in range(2)]
        all_i = [sb(f"all_i{n}", [P, K1, B], I32) for n in range(2)]
        pair_i = sb("pair_i", [P, K1, 2], I32)
        pair_w = sb("pair_w", [P, K1, 2])
        SLOT1 = 2 * F1 * DC
        RING1 = 4
        arena = sb("arena", [P, RING1 * SLOT1])
        at = [0]

        def part(n):
            at[0] += n
            assert at[0] <= RING1 * SLOT1
            return arena[:, at[0] - n:at[0]]

        all_inT = part(DC * N).rearrange("p (c n) -> p c n", c=DC)
        gate_w = [part(DC * F0).rearrange("p (c f) -> p c f", c=DC) for _ in range(2)]
        up_w = [part(DC * F0).rearrange("p (c f) -> p c f", c=DC) for _ in range(2)]
        down_w = [part(NFT * D).rearrange("p (j d) -> p j d", j=NFT) for _ in range(2)]
        erows = [gathered[:, u, :, :] for u in range(2)]
        erowsT = [part(DC * C0).rearrange("p (c n) -> p c n", c=DC) for _ in range(2)]
        hidden = part(2 * NFT * C0)
        hidT = [hidden[:, u * NFT * C0:(u + 1) * NFT * C0].rearrange("p (j n) -> p j n", j=NFT) for u in range(2)]
        silu = [part(BANK) for _ in range(3)]
        shT = hidden[:, 0:NFT * BANK].rearrange("p (j n) -> p j n", j=NFT)
        yrows = [part(NCT * D).rearrange("p (s d) -> p s d", s=NCT) for _ in range(2)]
        w1_sb = [arena[:, s * SLOT1:s * SLOT1 + DC * F1].rearrange("p (c f) -> p c f", c=DC) for s in range(RING1)]
        w2_sb = [arena[:, s * SLOT1 + DC * F1:(s + 1) * SLOT1].rearrange("p (j d) -> p j d", j=J1) for s in range(RING1)]
        dhidT = probs
        flat = probsT[:, :, :].rearrange("p b n -> p (b n)")
        drows = flat[:, 0:RING1 * D].rearrange("p (u d) -> p u d", u=RING1)
        drowsT = flat[:, RING1 * D:(RING1 + 2) * D].rearrange("p (u c n) -> p u c n", u=2, c=DC)
        dy = flat[:, (RING1 + 2) * D:(RING1 + 4) * D].rearrange("p (u d) -> p u d", u=2)
        stage = probs[:, :, :, :].rearrange("p a b c -> p (a b c)")
        conv_raw = stage[:, 0:2 * 2 * D].rearrange("p (m f) -> p m f", m=2)
        w_raw = stage[:, 4 * D:12 * D].rearrange("p (w m d) -> p w m d", w=4, m=2)
        b1_raw = stage[0:NE1, 12 * D:12 * D + F1]

        raw_in, dense_in, router_in, fill0, fill1 = (
            sem("raw_in"), sem("dense_in"), sem("router_in"), sem("fill0"), sem("fill1"))
        const_p, const_d, prep_full, prep_free = sem("const_p"), sem("const_d"), sem("prep_full"), sem("prep_free")

        layers = []
        for n in range(2):
            L = Layer(sem, n)
            L.NF = 8 if n == 0 else 4
            L.KF = L.NF - 4
            L.NB = 5 if n == 0 else 7
            L.E, L.K, L.C = (NE0, K0, C0) if n == 0 else (NE1, K1, C1)
            L.mask = mask0 if n == 0 else mask1
            L.rows, L.y = (rows0, y0) if n == 0 else (rows1, y1)
            L.rw, L.rb = (router0, rb0) if n == 0 else (router1, rb1)
            if n == 0:
                L.w = [lambda c, o, w=w: wT0[:, w, c, o] for w in range(4)]
            else:
                L.w = [lambda c, o, w=w: w_qkv[:, c, w * D + o.start:w * D + o.stop] for w in range(3)]
                L.w.append(lambda c, o: w_out[:, c, o])
            layers.append(L)
        L0, L1 = layers

        sh_gu, sh_silu, sh_hid, sh_y, sh_add = (sem(s) for s in ("sh_gu", "sh_silu", "sh_hid", "sh_y", "sh_add"))
        ew_in = [sem(f"ew_in{s}") for s in range(2)]
        er_in = [sem(f"er_in{s}") for s in range(2)]
        ey_out = [sem(f"ey_out{s}") for s in range(2)]
        ex_full, ex_free, e_gu, e_silu, e_hid, e_y, e_yfree = (
            sem(s) for s in ("ex_full", "ex_free", "e_gu", "e_silu", "e_hid", "e_y", "e_yfree"))
        dw_in = [sem(f"dw_in{s}") for s in range(RING1)]
        dr_in = [sem(f"dr_in{s}") for s in range(RING1)]
        dy_out = [sem(f"dy_out{s}") for s in range(2)]
        dx_full, dx_free, dh_full, dh_done, dy_full, dy_free = (
            sem(s) for s in ("dx_full", "dx_free", "dh_full", "dh_done", "dy_full", "dy_free"))
        out_ready, out_done = sem("out_ready"), [sem(f"out_done{t}") for t in range(2)]
        fin_index, fin_gathered, fin_steps = (
            [sem(f"fin_index{t}") for t in range(2)], [sem(f"fin_gathered{t}") for t in range(2)], sem("fin_steps"))
        FILLS = (NE0 * C0 * D // (P * 2048), NE1 * C1 * D // (P * 2048))

        def front(L, i, k):
            return k % 2, i * (L.NF // 2) + k // 2

        L0.fill, L1.fill = fill0, fill1
        GU = (2, 4, 0)
        ROUTER_LOADS = 9 + NFT
        ROUTE_STEPS, SLOT_STEPS = (14, 10), (5, 8)

        def head(b, j):
            return 8 * (j // 2) + 2 * b + j % 2

        def later(i, u):
            return (i + 1, u - RING1) if u >= RING1 else (i, u)

        block = ctx.enter_context(nc.Block())

        @block.sync
        def _(sp):
            x_rows = a["x"].rearrange("b (t k) d -> b t (k d)", k=2)

            def load_x(i, first):
                if not first:
                    for k in range(2):
                        b, n = front(L0, i - 1, k)
                        wait(sp, L0.front_full[b], n + 1)
                    wait(sp, L0.x_summed, i)
                sp.dma_start(x_in[:, :, :], x_rows[bass.ts(i, 2)].rearrange("b t f -> t b f")).then_inc(L0.x_loaded, 16)

            sp.dma_start(conv_raw, a["L0_tok_conv_w"].rearrange("(m o) i k -> o m (i k)", m=2)).then_inc(raw_in, 16)
            load_x(0, True)
            for w, name in enumerate(("Wq", "Wk", "Wv", "Wo")):
                sp.dma_start(w_raw[:, w], a[f"L0_attn_{name}"].rearrange("(m o) d -> o m d", m=2)).then_inc(raw_in, 16)
            sp.dma_start(b1_raw, a["L1_ffn_b1"]).then_inc(raw_in, 16)

            def shared_row(dst, src):
                sp.dma_start(dst, src.rearrange("(a n) -> a n", a=1).to_broadcast([P, src.shape[0]])).then_inc(dense_in, 16)

            shared_row(conv_b[:, :], a["L0_tok_conv_b"])
            shared_row(gamma[:, :], a["L0_tok_ln_gamma"])
            shared_row(beta[:, :], a["L0_tok_ln_beta"])
            def whole(dst, src):
                sp.dma_start(dst, src).then_inc(router_in, 16)

            whole(router0[:, :, :], a["L0_ffn_router_w"].rearrange("(c p) e -> p c e", p=P))
            whole(rb0[:, :], a["L0_ffn_router_b"].rearrange("(a n) -> a n", a=1).to_broadcast([P, NE0]))
            whole(router1[:, :, :], a["L1_ffn_gate_w"].rearrange("(c p) e -> p c e", p=P))
            whole(rb1[:, :], a["L1_ffn_gate_b"].rearrange("(a n) -> a n", a=1).to_broadcast([P, NE1]))
            whole(w_qkv[:, :, :], a["L1_attn_w_qkv"].rearrange("(c p) e -> p c e", p=P))
            whole(w_out[:, :, :], a["L1_attn_w_out"].rearrange("(c p) e -> p c e", p=P))
            whole(sw_gate[:, :, :], a["L0_ffn_sw_gate"].rearrange("(c p) e -> p c e", p=P))
            whole(sw_up[:, :, :], a["L0_ffn_sw_up"].rearrange("(c p) e -> p c e", p=P))
            for j, (f, m) in enumerate(FT):
                whole(sw_down[0:m, j, :], a["L0_ffn_sw_down"][f:f + m, :])
            whole(b2[:, :], a["L1_ffn_b2"])

            def load_weights(e, u, first):
                if not first:
                    wait(sp, e_y, (e - 2) * NCT + NCT)
                s = ew_in[u % 2]
                sp.dma_start(gate_w[u % 2], a["L0_ffn_w_gate"][bass.ds(e, 1)].rearrange("a (p c) f -> p (a c) f", c=DC)).then_inc(s, 16)
                sp.dma_start(up_w[u % 2], a["L0_ffn_w_up"][bass.ds(e, 1)].rearrange("a (p c) f -> p (a c) f", c=DC)).then_inc(s, 16)
                full = sum(m == P for _, m in FT)
                sp.dma_start(down_w[u % 2][:, 0:full, :],
                             a["L0_ffn_w_down"][bass.ds(e, 1), 0:full * P].rearrange("a (j p) d -> p (a j) d", p=P)).then_inc(s, 16)
                sp.dma_start(down_w[u % 2][0:F0 - full * P, full:full + 1, :],
                             a["L0_ffn_w_down"][bass.ds(e, 1), full * P:F0].rearrange("a p d -> p a d")).then_inc(s, 16)

            full = sum(m == P for _, m in CT)

            def load_rows(e, u, first):
                if not first:
                    wait(sp, ex_full, e - 1)
                s = er_in[u % 2]
                sp.dma_start(erows[u % 2][:, 0:full, :], rows0[bass.ds(e * C0, full * P)].rearrange("(s p) d -> p s d", p=P)).then_inc(s, 16)
                sp.dma_start(erows[u % 2][0:C0 - full * P, full, :], rows0[bass.ds(e * C0 + full * P, C0 - full * P)]).then_inc(s, 16)

            def store_y(e, u):
                wait(sp, e_yfree, (e + 1) * NCT)
                s = ey_out[u % 2]
                sp.dma_start(y0[bass.ds(e * C0, full * P)].rearrange("(s p) d -> p s d", p=P), yrows[u % 2][:, 0:full, :]).then_inc(s, 16)
                sp.dma_start(y0[bass.ds(e * C0 + full * P, C0 - full * P)], yrows[u % 2][0:C0 - full * P, full, :]).then_inc(s, 16)

            load_weights(0, 0, True)
            load_weights(1, 1, True)
            loop(sp, PAIRS, lambda i, first, last: None if first else load_x(i, False))

            sp.wait_ge(L0.scattered, 16 * 2 * K0 * PAIRS)
            load_rows(0, 0, True)
            load_rows(1, 1, True)

            def experts_b(i, first, last):
                for u in range(2):
                    e = 2 * i + u
                    if not last:
                        load_rows(e + 2, u, False)
                        load_weights(e + 2, u, False)
                    store_y(e, u)

            loop(sp, NE0 // 2, experts_b)
            for u in range(2):
                sp.wait_ge(ey_out[u], 16 * 2 * (NE0 // 2))

            def load_dw(e, u, first):
                if not first:
                    wait(sp, dy_full, e - RING1 + 1)
                sp.dma_start(w1_sb[u], a["L1_ffn_w1"][bass.ds(e, 1)].rearrange("a (p c) f -> p (a c) f", c=DC)).then_inc(dw_in[u], 16)
                sp.dma_start(w2_sb[u], a["L1_ffn_w2"][bass.ds(e, 1)].rearrange("a (p j) d -> p (a j) d", j=J1)).then_inc(dw_in[u], 16)

            def load_dr(e, u, first):
                if not first:
                    wait(sp, dx_full, e - RING1 + 1)
                sp.dma_start(drows[:, u, :], rows1[bass.ds(e * C1, C1)]).then_inc(dr_in[u], 16)

            for u in range(RING1):
                load_dw(u, u, True)
            sp.wait_ge(L1.scattered, 16 * 2 * K1 * PAIRS)
            for u in range(RING1):
                load_dr(u, u, True)

            def experts_d(i, first, last):
                for u in range(RING1):
                    e = RING1 * i + u
                    wait(sp, dy_free, e + 1)
                    sp.dma_start(y1[bass.ds(e * C1, C1)], dy[:, u % 2, :]).then_inc(dy_out[u % 2], 16)
                    if not last:
                        load_dr(e + RING1, u, False)
                        load_dw(e + RING1, u, False)

            loop(sp, NE1 // RING1, experts_d)

            def result(i, first, last):
                for t in range(2):
                    wait(sp, out_ready, 2 * i + t + 1)
                    sp.dma_start(out[bass.ds(2 * i + t, 1)].rearrange("b p d -> p b d"), h[:, bass.ds(2 * i + t, 1), :]).then_inc(out_done[t], 16)

            loop(sp, PAIRS, result)
            for t in range(2):
                sp.wait_ge(out_done[t], 16 * PAIRS)

        @block.gpsimd
        def _(pool):
            g = nc.gpsimd
            g.memset(zeros[:, :], 0.0).then_inc(const_p, 1)
            g.memset(ident[:, :], 0.0).then_inc(const_p, 1)
            g.memset(ones_f[:, :], 1.0).then_inc(const_p, 1)
            g.memset(half_neg[:, :], -0.5).then_inc(const_p, 1)
            g.memset(mask0[:, :], 0.0).then_inc(const_p, 1)
            g.memset(mask1[:, :], 0.0).then_inc(const_p, 1)
            g.iota(row_id[:, 0:1], [[0, 1]], base=0, channel_multiplier=1).then_inc(const_p, 1)
            g.iota(iota_e[:, :], [[1, NE1]], base=0, channel_multiplier=0, allow_small_or_imprecise_dtypes=True).then_inc(const_p, 1)
            pool.wait_ge(const_p, 8)
            g.affine_select(out=ident[:, :], in_=ident[:, :], compare_op=ALU.not_equal, fill=1.0, base=0,
                            pattern=[[-1, P]], channel_multiplier=1).then_inc(const_p, 1)
            g.affine_select(out=mask0[:, :], in_=mask0[:, :], compare_op=ALU.is_ge, fill=MASKED, base=0,
                            pattern=[[-1, P]], channel_multiplier=1).then_inc(const_p, 1)
            g.affine_select(out=mask1[:, :], in_=mask1[:, :], compare_op=ALU.is_ge, fill=MASKED, base=0,
                            pattern=[[-1, P]], channel_multiplier=1).then_inc(const_p, 1)
            g.affine_select(out=before[:, :], in_=ones_f[:, :], compare_op=ALU.is_gt, fill=0.0, base=0,
                            pattern=[[1, P]], channel_multiplier=-1).then_inc(const_p, 1)
            pool.wait_ge(const_p, 12)
            g.affine_select(out=mask0[:, :], in_=mask0[:, :], compare_op=ALU.is_gt, fill=MASKED, base=WINDOW,
                            pattern=[[1, P]], channel_multiplier=-1).then_inc(const_p, 1)
            pool.wait_ge(const_p, 13)

            def ln_scale(L, w, i):
                wait(pool, L.moments_ready[w], i + 1)
                settle(pool, i)
                g.tensor_scalar(var_eps[:, w, :], moments[:, w, :, 1], EPS, None, ALU.add).then_inc(L.eps_added[w], 1)
                pool.wait_ge(L.eps_added[w], i + 1)
                g.tensor_tensor(rstd[:, w, :], var_eps[:, w, :], half_neg[:, :], ALU.pow).then_inc(L.rstd_ready[w], 1)

            def sum_x(i):
                wait(pool, L0.x_loaded, 16 * (i + 1))
                wait(pool, L0.tok_biased, 2 * i)
                g.tensor_tensor(x_sum[:, :, :], x_in[:, :, 0:D], x_in[:, :, D:2 * D], ALU.add).then_inc(L0.x_summed, 1)

            def affine(i, first):
                wait(pool, L0.tok_normed, i + 1)
                if first:
                    pool.wait_ge(dense_in, 48)
                g.tensor_tensor(tok[:, :, :], tok[:, :, :], over(gamma[:, :], 1, [P, 2, D]), ALU.mult).then_inc(L0.tok_scaled, 1)
                wait(pool, L0.tok_scaled, i + 1)
                settle(pool, i)
                g.tensor_tensor(h[:, bass.ts(i, 2), :], tok[:, :, :], over(beta[:, :], 1, [P, 2, D]), ALU.add).then_inc(L0.h_ready, 1)

            def scatter(L, i, first):
                wait(pool, L.scatter_ready, i + 1)
                if first:
                    pool.wait_ge(L.fill, 16 * FILLS[L.n])
                settle(pool, i)
                for t in range(2):
                    for k in range(L.K):
                        g.indirect_dma_start(L.rows, bass.IndirectOffsetOnAxis(ap=scatter_i[:, k, t:t + 1], axis=0),
                                             ffn_in[:, t, :], None, bounds_check=L.E * L.C - 1,
                                             oob_is_err=False).then_inc(L.scattered, 16)

            def gather(i):
                wait(pool, L1.index_ready, i + 1)
                settle(pool, i)
                for t in range(2):
                    for k in range(K0):
                        g.indirect_dma_start(gathered[:, t, k, :], None, y0,
                                             bass.IndirectOffsetOnAxis(ap=pair_i[:, k, t:t + 1], axis=0)).then_inc(L1.gathered, 16)

            def add_input(i):
                wait(pool, L0.ffn_ready, i + 1)
                hp = h[:, bass.ts(i, 2), :]
                g.tensor_tensor(hp, hp, ffn_in[:, :, :], ALU.add).then_inc(L0.input_added, 1)

            def front0(i, first):
                sum_x(i)
                ln_scale(L0, 2, i)
                affine(i, first)
                ln_scale(L0, 0, i)

            def phase_a(i, first, last):
                if not first:
                    scatter(L0, i - 1, isinstance(i, int) and i == 1)
                if not last:
                    front0(i + 1, False)
                ln_scale(L0, 1, i)
                add_input(i)

            front0(0, True)
            phase_a(0, True, False)
            loop_from(pool, 1, PAIRS, phase_a)
            scatter(L0, PAIRS - 1, False)

            for u in range(2):
                pool.wait_ge(ey_out[u], 16 * 2 * (NE0 // 2))

            def phase_c(i, first, last):
                if not first:
                    scatter(L1, i - 1, isinstance(i, int) and i == 1)
                if not last:
                    gather(i + 1)
                    ln_scale(L1, 0, i + 1)
                ln_scale(L1, 1, i)

            gather(0)
            ln_scale(L1, 0, 0)
            phase_c(0, True, False)
            loop_from(pool, 1, PAIRS, phase_c)
            scatter(L1, PAIRS - 1, False)

            for u in range(2):
                pool.wait_ge(dy_out[u], 16 * (NE1 // 2))

            def final_gather(i, first, last):
                for t in range(2):
                    wait(pool, fin_index[t], i + 1)
                    settle(pool, i)
                    for k in range(K1):
                        g.indirect_dma_start(gathered[:, t, k, :], None, y1,
                                             bass.IndirectOffsetOnAxis(ap=pair_i[:, k, t:t + 1], axis=0)).then_inc(fin_gathered[t], 16)

            loop(pool, PAIRS, final_gather)

        @block.tensor
        def _(pe):
            pe.wait_ge(const_p, 13)
            pe.wait_ge(raw_in, 16 * 6)
            prep = [0]

            def prep_job(turns):
                n = prep[0]
                wait(pe, prep_free, n - 1)
                for out_ap, in_ap, k in turns:
                    last = pe.transpose(out_ap, in_ap, ident[0:k, 0:k])
                last.then_inc(prep_full, 1)
                prep[0] += 1

            def prep_out(col, n=P):
                return front_bank[prep[0] % 2][:, col:col + n]

            for k in range(2):
                prep_job([(prep_out((c * 2 + m) * P), conv_raw[:, m, c * 2 * P + k:(c + 1) * 2 * P:2], P)
                          for c in range(DC) for m in range(2)])
            for w in range(4):
                prep_job([(prep_out((c * 2 + m) * P), w_raw[:, w, m, c * P:(c + 1) * P], P)
                          for c in range(DC) for m in range(2)])
            prep_job([(prep_out(j * NE1, NE1), b1_raw[:, j:F1:J1], NE1) for j in range(J1)])
            pe.wait_ge(prep_free, prep[0])

            def front_job(L, i, k):
                b, n = front(L, i, k)
                wait(pe, L.front_free[b], n)
                return front_bank[b], L.front_full[b]

            def turn_x(i):
                wait(pe, L0.x_loaded, 16 * (i + 1))
                for t in range(2):
                    bk, full = front_job(L0, i, t)
                    for c in range(2 * DC):
                        last = pe.transpose(bk[:, c * P:(c + 1) * P], x_in[:, t, c * P:(c + 1) * P], ident[:, :])
                    last.then_inc(full, 1)

            def conv(i):
                for t in range(2):
                    wait(pe, L0.front_free[t], i * (L0.NF // 2) + 1)
                    bk, full = front_job(L0, i, 2 + t)
                    for c in range(2 * DC):
                        last = pe.matmul(bk[:, 0:D], xT[:, t, c, :], conv_wT[:, c, :], start=c == 0, stop=c == 2 * DC - 1)
                    last.then_inc(full, 1)

            def turn_normed(L, i):
                wait(pe, L.normed_ready, i + 1)
                bk, full = front_job(L, i, L.KF)
                for c in range(DC):
                    for t in range(2):
                        last = pe.transpose(bk[:, (2 * c + t) * P:(2 * c + t + 1) * P], normed[:, t, c * P:(c + 1) * P], ident[:, :])
                last.then_inc(full, 1)

            def project(L, i):
                b, n = front(L, i, L.KF)
                wait(pe, L.front_free[b], n + 1)
                for w in range(2):
                    bk, full = front_job(L, i, L.KF + 1 + w)
                    for m in range(DC):
                        for c in range(DC):
                            last = pe.matmul(bk[:, m * D:(m + 1) * D], L.w[w](c, slice(m * P, (m + 1) * P)),
                                             normedT[:, c, :], start=c == 0, stop=c == DC - 1)
                    last.then_inc(full, 1)
                bk, full = front_job(L, i, L.KF + 3)
                for t in range(2):
                    for c in range(DC):
                        last = pe.matmul(bk[:, t * D:(t + 1) * D], normedT[:, c, t * P:(t + 1) * P],
                                         L.w[2](c, slice(0, D)), start=c == 0, stop=c == DC - 1)
                last.then_inc(full, 1)

            def scores(L, i, t):
                if t == 0:
                    for k in (1, 2):
                        b, n = front(L, i, L.KF + k)
                        wait(pe, L.front_free[b], n + 1)
                for b in range(SBANKS):
                    wait(pe, L.max_done, 8 * i + 4 * t + b - 1)
                    row = 32 * b
                    for m in range(DC):
                        last = pe.matmul(score_bank[b % 2][:, 2 * m * P:2 * (m + 1) * P], qT[row:row + 32, m, t, :],
                                         kT[row:row + 32, m, t, :, :], start=True, stop=True)
                    last.then_inc(L.score_full, 1)

            def attend(L, i, t):
                def values(b):
                    n = 8 * i + 4 * t + b
                    wait(pe, L.turned, n + 1)
                    if b == 0:
                        fb, fn = front(L, i, L.KF + 3)
                        wait(pe, L.front_free[fb], fn + 1)
                        wait(pe, L.mix_done, 2 * i + t - 1)
                    for j in range(HEADS_PER_BANK):
                        hd = head(b, j)
                        last = pe.matmul(mix_bank[:, t * D + hd * HD:t * D + (hd + 1) * HD],
                                         probsT[:, b, j * P:(j + 1) * P], v[:, t, hd * HD:(hd + 1) * HD],
                                         start=True, stop=True)
                    last.then_inc(L.pv_done, 1)

                for b in range(SBANKS):
                    n = 8 * i + 4 * t + b
                    wait(pe, L.exp_done, n + 1)
                    wait(pe, L.turned, n - 1)
                    for j in range(HEADS_PER_BANK):
                        last = pe.transpose(turn_bank[b % 2][:, j * P:(j + 1) * P], probs[:, t, head(b, j), :], ident[:, :])
                    last.then_inc(L.turn_full, 1)
                    if b >= 1:
                        values(b - 1)
                values(SBANKS - 1)

            def back_job(L, i, k):
                wait(pe, L.back_free, i * L.NB + k)

            def turn_mixed(L, i):
                wait(pe, L.mix_done, 2 * i + 2)
                back_job(L, i, 0)
                for c in range(DC):
                    for t in range(2):
                        last = pe.transpose(back_bank[:, (2 * c + t) * P:(2 * c + t + 1) * P], mixed[:, t, c * P:(c + 1) * P], ident[:, :])
                last.then_inc(L.back_full, 1)

            def project_out(L, i):
                back_job(L, i, 1)
                for t in range(2):
                    for c in range(DC):
                        last = pe.matmul(back_bank[:, t * D:(t + 1) * D], mixedT[:, c, t * P:(t + 1) * P],
                                         L.w[3](c, slice(0, D)), start=c == 0, stop=c == DC - 1)
                last.then_inc(L.back_full, 1)

            def route(L, i, first):
                wait(pe, L.ffn_ready, i + 1)
                back_job(L, i, 2)
                for c in range(DC):
                    for t in range(2):
                        last = pe.transpose(back_bank[:, (2 * c + t) * P:(2 * c + t + 1) * P], ffn_in[:, t, c * P:(c + 1) * P], ident[:, :])
                last.then_inc(L.back_full, 1)
                back_job(L, i, 3)
                for t in range(2):
                    for c in range(DC):
                        last = pe.matmul(back_bank[:, t * L.E:(t + 1) * L.E], ffn_inT[:, c, t * P:(t + 1) * P],
                                         L.rw[:, c, :], start=c == 0, stop=c == DC - 1)
                last.then_inc(L.back_full, 1)

            def count(L, i):
                wait(pe, L.chosen_ready, i + 1)
                back_job(L, i, 4)
                for t in range(2):
                    col = back_bank[:, t * L.E:(t + 1) * L.E]
                    pe.matmul(col, before[:, :], chosen[:, t, 0:L.E], start=True, stop=False)
                    last = pe.matmul(col, ones_b[:, :], earlier[:, t, 0:L.E], start=False, stop=True)
                last.then_inc(L.back_full, 1)

            def turn_gates(i):
                wait(pe, L1.gates_ready, i + 1)
                back_job(L1, i, 5)
                settle(pe, i)
                for t in range(2):
                    last = pe.transpose(back_bank[0:NE1, t * P:(t + 1) * P], gates_e[:, t, :], ident[:, :])
                last.then_inc(L1.back_full, 1)

            def gated_b2(i):
                back_job(L1, i, 6)
                for t in range(2):
                    last = pe.matmul(back_bank[:, t * D:(t + 1) * D], gates_eT[:, t * P:(t + 1) * P], b2[:, :], start=True, stop=True)
                last.then_inc(L1.back_full, 1)

            def pairs(L):
                def body(i, first, last):
                    scores(L, i, 0)
                    if not first:
                        route(L, i - 1, False)
                    scores(L, i, 1)
                    if not first:
                        count(L, i - 1)
                    if not last and L is L0:
                        turn_x(i + 1)
                        conv(i + 1)
                    attend(L, i, 0)
                    if not first and L is L1:
                        turn_gates(i - 1)
                    attend(L, i, 1)
                    if not first and L is L1:
                        gated_b2(i - 1)
                    turn_mixed(L, i)
                    if not last:
                        turn_normed(L, i + 1)
                    project_out(L, i)
                    if not last:
                        project(L, i + 1)
                if L is L0:
                    turn_x(0)
                    conv(0)
                turn_normed(L, 0)
                project(L, 0)
                loop(pe, PAIRS, body)
                route(L, PAIRS - 1, False)
                count(L, PAIRS - 1)
                if L is L1:
                    turn_gates(PAIRS - 1)
                    gated_b2(PAIRS - 1)

            def banks_empty(L):
                pe.wait_ge(L.max_done, SBANKS * B)
                pe.wait_ge(L.turned, SBANKS * B)
                pe.wait_ge(L.mix_done, B)
                for b in range(2):
                    pe.wait_ge(L.front_free[b], PAIRS * L.NF // 2)
                pe.wait_ge(L.back_free, PAIRS * L.NB)

            pe.wait_ge(router_in, 16 * ROUTER_LOADS)
            pairs(L0)
            banks_empty(L0)

            def shared_mlp(q, first, last):
                for j, (f, m) in enumerate(FT):
                    gate_bank, up_bank = bank[GU[j]], bank[GU[j] + 1]
                    wait(pe, sh_hid, 3 * q + j - 2)
                    for w, dst in ((sw_gate, gate_bank), (sw_up, up_bank)):
                        for c in range(DC):
                            mm = pe.matmul(dst[0:m, :], w[:, c, f:f + m], all_inT[:, c, bass.ts(q, BANK)],
                                           start=c == 0, stop=c == DC - 1)
                    mm.then_inc(sh_gu, 1)
                wait(pe, sh_hid, 3 * q + 3)
                for half in range(2):
                    wait(pe, sh_add, 2 * q - 1 + half)
                    for t in range(2):
                        col = (2 * half + t) * P
                        for j, (f, m) in enumerate(FT):
                            mm = pe.matmul(bank[6 + half][:, t * D:(t + 1) * D], shT[0:m, j, col:col + P],
                                           sw_down[0:m, j, :], start=j == 0, stop=j == NFT - 1)
                    mm.then_inc(sh_y, 1)

            loop(pe, N // BANK, shared_mlp)
            pe.wait_ge(sh_hid, NFT * (N // BANK))
            pe.wait_ge(sh_add, 2 * (N // BANK))

            def turn_rows_b(i, u):
                e = 2 * i + u
                wait(pe, er_in[u], 32 * (i + 1))
                wait(pe, ex_free, e)
                for c in range(DC):
                    for s, (r, m) in enumerate(CT):
                        mm = pe.transpose(bank[c][:, r:r + m], erows[u][0:m, s, c:D:DC], ident[0:m, 0:m])
                mm.then_inc(ex_full, 1)

            def gate_up(i, u):
                e = 2 * i + u
                wait(pe, ex_free, e + 1)
                wait(pe, ew_in[u], 64 * (i + 1))
                for j, (f, m) in enumerate(FT):
                    s = (NFT * u + j) % 2
                    wait(pe, e_hid, NFT * e + j - 1)
                    for w, dst in ((gate_w[u], bank[2 + 2 * s]), (up_w[u], bank[3 + 2 * s])):
                        for c in range(DC):
                            mm = pe.matmul(dst[0:m, 0:C0], w[:, c, f:f + m], erowsT[u][:, c, :],
                                           start=c == 0, stop=c == DC - 1)
                    mm.then_inc(e_gu, 1)

            def down(i, u):
                e = 2 * i + u
                wait(pe, e_hid, NFT * (e + 1))
                for s, (r, m) in enumerate(CT):
                    wait(pe, e_yfree, NCT * e + s - 1)
                    for j, (f, fm) in enumerate(FT):
                        mm = pe.matmul(bank[6 + (NCT * u + s) % 2][0:m, 0:D], hidT[u][0:fm, j, r:r + m],
                                       down_w[u][0:fm, j, :], start=j == 0, stop=j == NFT - 1)
                    mm.then_inc(e_y, 1)

            def experts_b(i, first, last):
                for u in range(2):
                    if not last:
                        turn_rows_b(i + 1, u)
                    if u == 0:
                        gate_up(i, 1)
                    elif not last:
                        gate_up(i + 1, 0)
                    down(i, u)

            turn_rows_b(0, 0)
            turn_rows_b(0, 1)
            gate_up(0, 0)
            loop(pe, NE0 // 2, experts_b)
            pe.wait_ge(e_hid, NFT * NE0)
            pe.wait_ge(e_yfree, NCT * NE0)

            pairs(L1)
            banks_empty(L1)

            def turn_rows_d(i, v_):
                i, u = later(i, v_)
                e = RING1 * i + u
                wait(pe, dr_in[u], 16 * (i + 1))
                wait(pe, dx_free, e - 1)
                for c in range(DC):
                    mm = pe.transpose(bank[u % 2][:, c * P:(c + 1) * P], drows[:, u, c:D:DC], ident[:, :])
                mm.then_inc(dx_full, 1)

            def first_product(i, v_):
                i, u = later(i, v_)
                e = RING1 * i + u
                wait(pe, dx_free, e + 1)
                wait(pe, dw_in[u], 32 * (i + 1))
                for half in range(2):
                    wait(pe, dh_done, 2 * e - 3 + half)
                    for jj in range(J1 // 2):
                        j = half * (J1 // 2) + jj
                        for c in range(DC):
                            mm = pe.matmul(bank[2 + 2 * (u % 2) + half][:, jj * P:(jj + 1) * P], w1_sb[u][:, c, j:F1:J1],
                                           drowsT[:, u % 2, c, :], start=c == 0, stop=c == DC - 1)
                    mm.then_inc(dh_full, 1)

            def second_product(i, u):
                e = RING1 * i + u
                wait(pe, dh_done, 2 * e + 2)
                wait(pe, dy_free, e - 1)
                for j in range(J1):
                    mm = pe.matmul(bank[6 + u % 2][:, 0:D], dhidT[:, u % 2, j, :], w2_sb[u][:, j, :], start=j == 0, stop=j == J1 - 1)
                mm.then_inc(dy_full, 1)

            def experts_d(i, first, last):
                for u in range(RING1):
                    if not (last and u + 2 >= RING1):
                        turn_rows_d(i, u + 2)
                    if not (last and u + 1 >= RING1):
                        first_product(i, u + 1)
                    second_product(i, u)

            turn_rows_d(0, 0)
            turn_rows_d(0, 1)
            first_product(0, 0)
            loop(pe, NE1 // RING1, experts_d)

        @block.scalar
        def _(act):
            act.wait_ge(const_p, 1)
            for rows, fill, n in ((rows0, fill0, FILLS[0]), (rows1, fill1, FILLS[1])):
                flat = rows.rearrange("(n p r) d -> n p (r d)", p=P, r=2048 // D)
                for k in range(n):
                    act.dma_start(flat[k].rearrange("p (r n) -> p r n", n=BANK), over(zeros[:, :], 1, [P, 2048 // BANK, BANK])).then_inc(fill, 16)

            def from_front(L, i, k):
                b, n = front(L, i, k)
                wait(act, L.front_full[b], n + 1)
                return front_bank[b], L.front_free[b]

            def keep_xT(i):
                for t in range(2):
                    wait(act, L0.front_full[t], (i - 1) * (L0.NF // 2) + 2)
                for t in range(2):
                    bk, free = from_front(L0, i, t)
                    act.activation(xT[:, t, :, :], bk[:, :].rearrange("p (c n) -> p c n", n=P), ACT.Copy).then_inc(free, 1)

            def keep_normedT(L, i):
                b, n = front(L, i - 1, L.KF + 3)
                wait(act, L.front_full[b], n + 1)
                bk, free = from_front(L, i, L.KF)
                act.activation(normedT[:, :, :], bk[:, :].rearrange("p (c n) -> p c n", c=DC), ACT.Copy).then_inc(free, 1)

            def keep_qkv(L, i):
                wait(act, L.score_full, 8 * i)
                bk, free = from_front(L, i, L.KF + 1)
                act.activation(qT[:, :, :, :], bk[:, :].rearrange("p (m t n) -> p m t n", m=DC, t=2), ACT.Copy).then_inc(free, 1)
                bk, free = from_front(L, i, L.KF + 2)
                for r in range(2):
                    last = act.activation(kT[:, :, :, r, :], bk[:, :].rearrange("p (m t n) -> p m t n", m=DC, t=2),
                                          ACT.Copy, scale=parity[:, r:r + 1])
                last.then_inc(free, 1)
                wait(act, L.pv_done, 8 * i)
                bk, free = from_front(L, i, L.KF + 3)
                act.activation(v[:, :, :], bk[:, :].rearrange("p (t n) -> p t n", t=2), ACT.Copy).then_inc(free, 1)

            def exponentials(L, i, t):
                wait(act, L.mix_done, 2 * i + t - 1)
                for b in range(SBANKS):
                    wait(act, L.max_done, 8 * i + 4 * t + b + 1)
                    for j in range(HEADS_PER_BANK):
                        hd = head(b, j)
                        last = act.activation(probs[:, t, hd, :], probs[:, t, hd, :], ACT.Exp, scale=-1.0,
                                              bias=neg_max[:, t, hd:hd + 1], accum_out=exp_sum[:, t, hd:hd + 1])
                    last.then_inc(L.exp_done, 1)

            def from_back(L, i, k):
                wait(act, L.back_full, i * L.NB + k + 1)

            def keep_mixedT(L, i):
                from_back(L, i, 0)
                act.activation(mixedT[:, :, :], back_bank[:, :].rearrange("p (c n) -> p c n", c=DC), ACT.Copy).then_inc(L.back_free, 1)

            def keep_ffn_inT(L, i):
                from_back(L, i, 2)
                src = back_bank[:, :].rearrange("p (c n) -> p c n", c=DC)
                if L is L0:
                    act.activation(all_inT[:, :, bass.ts(i, 2 * P)], src, ACT.Copy)
                act.activation(ffn_inT[:, :, :], src, ACT.Copy).then_inc(L.back_free, 1)

            def router_exp(L, i):
                wait(act, L.to_exp, i + 1)
                n = L.E if L is L0 else L.K
                act.activation(gate_p[:, :, 0:n], shifted[:, :, 0:n], ACT.Exp).then_inc(L.from_exp, 1)

            def keep_gatesT(i):
                from_back(L1, i, 5)
                act.activation(gates_eT[:, :], back_bank[0:NE1, 0:2 * P], ACT.Copy).then_inc(L1.back_free, 1)

            def pairs(L):
                def body(i, first, last):
                    exponentials(L, i, 0)
                    if not first:
                        keep_ffn_inT(L, i - 1)
                        router_exp(L, i - 1)
                    exponentials(L, i, 1)
                    if not last and L is L0:
                        keep_xT(i + 1)
                    if not first and L is L1:
                        keep_gatesT(i - 1)
                    keep_mixedT(L, i)
                    if not last:
                        keep_normedT(L, i + 1)
                        keep_qkv(L, i + 1)
                if L is L0:
                    keep_xT(0)
                keep_normedT(L, 0)
                keep_qkv(L, 0)
                loop(act, PAIRS, body)
                keep_ffn_inT(L, PAIRS - 1)
                router_exp(L, PAIRS - 1)
                if L is L1:
                    keep_gatesT(PAIRS - 1)

            act.wait_ge(const_d, 3)
            pairs(L0)

            def shared_silu(q, first, last):
                for j, (f, m) in enumerate(FT):
                    wait(act, sh_gu, 3 * q + j + 1)
                    wait(act, sh_hid, 3 * q + j - 2)
                    act.activation(silu[j][0:m, :], bank[GU[j]][0:m, :], ACT.Silu).then_inc(sh_silu, 1)

            loop(act, N // BANK, shared_silu)

            def experts_b(i, first, last):
                for u in range(2):
                    e = 2 * i + u
                    for j, (f, m) in enumerate(FT):
                        s = (NFT * u + j) % 2
                        wait(act, e_gu, NFT * e + j + 1)
                        wait(act, e_hid, NFT * e + j - 1)
                        act.activation(silu[s][0:m, 0:C0], bank[2 + 2 * s][0:m, 0:C0], ACT.Silu).then_inc(e_silu, 1)

            loop(act, NE0 // 2, experts_b)

            pairs(L1)

            def experts_d(i, first, last):
                for u in range(RING1):
                    e = RING1 * i + u
                    wait(act, dy_full, e - 1)
                    for half in range(2):
                        wait(act, dh_full, 2 * e + half + 1)
                        for jj in range(J1 // 2):
                            j = half * (J1 // 2) + jj
                            last_ = act.activation(dhidT[:, u % 2, j, :], bank[2 + 2 * (u % 2) + half][:, jj * P:(jj + 1) * P],
                                                   ACT.Gelu, bias=b1T[:, j, bass.ds(e, 1)])
                        last_.then_inc(dh_done, 1)

            loop(act, NE1 // RING1, experts_d)

        @block.vector
        def _(dve):
            dve.wait_ge(const_p, 8)
            dve.memset(ones_b[:, :], 1.0)
            dve.tensor_scalar(row_id[:, 1:2], row_id[:, 0:1], HD.bit_length() - 1, 1, ALU.logical_shift_right,
                              ALU.bitwise_and).then_inc(const_d, 1)
            dve.wait_ge(const_d, 1)
            dve.tensor_copy(row_f[:, :], row_id[:, 1:2]).then_inc(const_d, 1)
            dve.wait_ge(const_d, 2)
            dve.tensor_scalar(parity[:, 0:1], row_f[:, :], -SCALE, SCALE, ALU.mult, ALU.add)
            dve.tensor_scalar(parity[:, 1:2], row_f[:, :], SCALE, None, ALU.mult).then_inc(const_d, 1)
            places = [conv_wT[:, 2 * k:2 * k + 2, :] for k in range(2)] + [wT0[:, w, :, :] for w in range(4)] + [b1T[:, :, :]]
            for n, place in enumerate(places):
                dve.wait_ge(prep_full, n + 1)
                dve.tensor_copy(place, front_bank[n % 2][:, :].rearrange("p (a b) -> p a b", a=place.shape[1])).then_inc(prep_free, 1)

            def ln_stats(L, w, i, src):
                settle(dve, i)
                for t in range(2):
                    last = dve.bn_stats(stats[:, w, t, :], src(t))
                last.then_inc(L.stat_steps[w], 1)
                wait(dve, L.stat_steps[w], i + 1)
                settle(dve, i)
                for t in range(2):
                    last = dve.bn_aggr(moments[:, w, t, :], stats[:, w, t, :])
                last.then_inc(L.moments_ready[w], 1)

            def ln_apply(L, w, i, src, dst, done):
                wait(dve, L.rstd_ready[w], i + 1)
                wait(dve, L.moments_ready[w], i + 1)
                for t in range(2):
                    last = dve.tensor_scalar(dst(t), src(t), moments[:, w, t, 0:1], rstd[:, w, t:t + 1],
                                             ALU.subtract, ALU.mult)
                last.then_inc(done, 1)

            def h_tile(i):
                return lambda t: h[:, bass.ds(2 * i + t, 1), :].rearrange("p a d -> p (a d)")

            def mix_tokens(i, first):
                wait(dve, L0.x_summed, i + 1)
                if first:
                    dve.wait_ge(dense_in, 48)
                for t in range(2):
                    b, n = front(L0, i, 2 + t)
                    wait(dve, L0.front_full[b], n + 1)
                    dve.scalar_tensor_tensor(out=tok[:, t, :], in0=x_sum[:, t, :], scalar=0.5, in1=front_bank[b][:, 0:D],
                                             op0=ALU.mult, op1=ALU.add).then_inc(L0.front_free[b], 1)
                for t in range(2):
                    b, n = front(L0, i, 2 + t)
                    wait(dve, L0.front_free[b], n + 1)
                    dve.tensor_tensor(tok[:, t, :], tok[:, t, :], conv_b[:, :], ALU.add).then_inc(L0.tok_biased, 1)
                wait(dve, L0.tok_biased, 2 * i + 2)
                ln_stats(L0, 2, i, lambda t: tok[:, t, :])

            def add_gathered(i):
                wait(dve, L1.gathered, 16 * 2 * K0 * (i + 1))
                for k in range(K0):
                    for t in range(2):
                        ht = h_tile(i)(t)
                        last = dve.scalar_tensor_tensor(out=ht, in0=gathered[:, t, k, :], scalar=pair_w[:, k, t:t + 1],
                                                        in1=ht, op0=ALU.mult, op1=ALU.add)
                    last.then_inc(L1.add_steps, 1)
                    wait(dve, L1.add_steps, K0 * i + k + 1)

            def pair_indices(i):
                dve.tensor_copy(pair_w[:, 0:K0, :], all_w[0][:, 0:K0, bass.ts(i, 2)])
                dve.tensor_copy(pair_i[:, 0:K0, :], all_i[0][:, 0:K0, bass.ts(i, 2)]).then_inc(L1.index_ready, 1)
                wait(dve, L1.index_ready, i + 1)

            def front_a(L, i, first):
                if L is L0:
                    mix_tokens(i, first)
                else:
                    add_gathered(i)
                    ln_stats(L1, 0, i, h_tile(i))

            def front_b(L, i, last):
                if L is L0:
                    ln_apply(L0, 2, i, lambda t: tok[:, t, :], lambda t: tok[:, t, :], L0.tok_normed)
                elif not last:
                    pair_indices(i + 1)

            def front_c(L, i):
                if L is L0:
                    wait(dve, L0.h_ready, i + 1)
                    ln_stats(L0, 0, i, h_tile(i))

            def front_d(L, i):
                b, n = front(L, i - 1, L.KF)
                wait(dve, L.front_full[b], n + 1)
                ln_apply(L, 0, i, h_tile(i), lambda t: normed[:, t, :], L.normed_ready)

            def greatest(L, i, t):
                wait(dve, L.turn_full, 8 * i + 4 * t - 4)
                for b in range(SBANKS):
                    wait(dve, L.score_full, 8 * i + 4 * t + b + 1)
                    settle(dve, i)
                    for j in range(HEADS_PER_BANK):
                        hd = head(b, j)
                        last = dve.tensor_tensor_reduce(probs[:, t, hd, :], score_bank[b % 2][:, j * P:(j + 1) * P],
                                                        L.mask[:, :], -1.0, 3e38, ALU.add, ALU.min,
                                                        neg_max[:, t, hd:hd + 1])
                    last.then_inc(L.max_done, 1)

            def keep_turned(L, i, t):
                for b in range(SBANKS):
                    n = 8 * i + 4 * t + b
                    wait(dve, L.turn_full, n + 1)
                    wait(dve, L.pv_done, n - 3)
                    dve.tensor_copy(probsT[:, b, :], turn_bank[b % 2][:, :]).then_inc(L.turned, 1)

            def normalise(L, i, t):
                if t == 0:
                    wait(dve, L.back_full, (i - 1) * L.NB + 1)
                wait(dve, L.pv_done, 8 * i + 4 * t + 4)
                dve.reciprocal(exp_inv[:, t, :], exp_sum[:, t, :]).then_inc(L.inv_done, 1)
                wait(dve, L.inv_done, 2 * i + t + 1)
                dve.tensor_tensor(mixed[:, t, :].rearrange("p (h d) -> p h d", h=HEADS),
                                  mix_bank[:, t * D:(t + 1) * D].rearrange("p (h d) -> p h d", h=HEADS),
                                  over(exp_inv[:, t, :], 2, [P, HEADS, HD]), ALU.mult).then_inc(L.mix_done, 1)

            def residual(L, i):
                wait(dve, L.back_full, i * L.NB + 2)
                hp = h[:, bass.ts(i, 2), :]
                dve.tensor_tensor(hp, hp, back_bank[:, :].rearrange("p (t d) -> p t d", t=2), ALU.add).then_inc(L.back_free, 1)
                wait(dve, L.back_free, i * L.NB + 2)
                ln_stats(L, 1, i, h_tile(i))

            def expert_input(L, i):
                wait(dve, L.scattered, 16 * 2 * L.K * i)
                if L is L0:
                    wait(dve, L.input_added, i)
                ln_apply(L, 1, i, h_tile(i), lambda t: ffn_in[:, t, :], L.ffn_ready)

            def choose(L, i):
                E, K = L.E, L.K
                chain = Chain(dve, L.route_steps, i, ROUTE_STEPS[L.n])
                wait(dve, L.back_full, i * L.NB + 4)
                lg = logits[:, :, 0:E]
                dve.tensor_tensor(lg, back_bank[:, 0:2 * E].rearrange("p (t e) -> p t e", t=2),
                                  over(L.rb[:, 0:E], 1, [P, 2, E]), ALU.add).then_inc(L.back_free, 1)
                wait(dve, L.back_free, i * L.NB + 4)
                if L is L0:
                    chain.link(dve.tensor_reduce(rsmall[:, 0, :], lg, AX.X, ALU.max))
                    dve.tensor_tensor(shifted[:, :, 0:E], lg, over(rsmall[:, 0, :], 2, [P, 2, E]), ALU.subtract).then_inc(L.to_exp, 1)
                    wait(dve, L.from_exp, i + 1)
                    chain.link(dve.tensor_reduce(rsmall[:, 1, :], gate_p[:, :, 0:E], AX.X, ALU.add))
                    chain.link(dve.reciprocal(rsmall[:, 2, :], rsmall[:, 1, :]))
                    chain.link(dve.tensor_tensor(lg, gate_p[:, :, 0:E], over(rsmall[:, 2, :], 2, [P, 2, E]), ALU.mult))
                settle(dve, i)
                for t in range(2):
                    last = dve.max(top_v[:, t, :], logits[:, t, 0:E])
                chain.link(last)
                settle(dve, i)
                for t in range(2):
                    last = dve.max_index(top_i[:, t, :], top_v[:, t, :], logits[:, t, 0:E])
                chain.link(last)
                chain.link(dve.tensor_copy(top_f[:, :, :], top_i[:, :, :]))
                for k in range(K):
                    last = dve.tensor_tensor(onehot[:, k, :, 0:E], over(iota_e[:, 0:E], 1, [P, 2, E]),
                                             top_f[:, :, k:k + 1].to_broadcast([P, 2, E]), ALU.is_equal)
                chain.link(last)
                ch = chosen[:, :, 0:E]
                if K == 2:
                    chain.link(dve.tensor_tensor(ch, onehot[:, 0, :, 0:E], onehot[:, 1, :, 0:E], ALU.add))
                else:
                    chain.link(dve.tensor_tensor(product[:, 0, :, 0:E], onehot[:, 0, :, 0:E], onehot[:, 1, :, 0:E], ALU.add))
                    chain.link(dve.tensor_tensor(ch, product[:, 0, :, 0:E], onehot[:, 2, :, 0:E], ALU.add))
                dve.tensor_copy(earlier[:, 0, 0:E], running[:, 0:E])
                chain.link(dve.tensor_tensor(earlier[:, 1, 0:E], running[:, 0:E], chosen[:, 0, 0:E], ALU.add))
                dve.tensor_tensor(running[:, 0:E], earlier[:, 1, 0:E], chosen[:, 1, 0:E], ALU.add).then_inc(L.chosen_ready, 1)
                wait(dve, L.chosen_ready, i + 1)
                vals = top_v[:, :, 0:K]
                if L is L0:
                    chain.link(dve.tensor_tensor(rsmall[:, 3, :], top_v[:, :, 0], top_v[:, :, 1], ALU.add))
                    chain.link(dve.tensor_scalar(rsmall[:, 4, :], rsmall[:, 3, :], GATHER_SUM_EPS, None, ALU.add))
                else:
                    dve.tensor_tensor(shifted[:, :, 0:K], vals, top_v[:, :, 0:1].to_broadcast([P, 2, K]), ALU.subtract).then_inc(L.to_exp, 1)
                    wait(dve, L.from_exp, i + 1)
                    vals = gate_p[:, :, 0:K]
                    chain.link(dve.tensor_reduce(rsmall[:, 4, :], vals, AX.X, ALU.add))
                chain.link(dve.reciprocal(rsmall[:, 5, :], rsmall[:, 4, :]))
                chain.link(dve.tensor_tensor(weight[:, 0:K, :], vals.rearrange("p t k -> p k t"),
                                             over(rsmall[:, 5, :], 1, [P, K, 2]), ALU.mult))
                chain.end()

            def place(L, i):
                E, K, C = L.E, L.K, L.C
                chain = Chain(dve, L.slot_steps, i, SLOT_STEPS[L.n])
                wait(dve, L.back_full, i * L.NB + 5)
                dve.tensor_copy(count_sb[:, :, 0:E], back_bank[:, 0:2 * E].rearrange("p (t e) -> p t e", t=2)).then_inc(L.back_free, 1)
                wait(dve, L.back_free, i * L.NB + 5)
                for k in range(K):
                    last = dve.tensor_tensor(product[:, k, :, 0:E], onehot[:, k, :, 0:E], count_sb[:, :, 0:E], ALU.mult)
                chain.link(last)
                chain.link(dve.tensor_reduce(posf[:, 0:K, :], product[:, 0:K, :, 0:E], AX.X, ALU.add))
                dve.tensor_scalar(validf[:, 0:K, :], posf[:, 0:K, :], float(C), None, ALU.is_lt)
                chain.link(dve.tensor_scalar(tmpf[:, 0:K, :], posf[:, 0:K, :], float(C - 1), None, ALU.min))
                chain.link(dve.scalar_tensor_tensor(out=slotf[:, 0:K, :], in0=top_f[:, :, 0:K].rearrange("p t k -> p k t"),
                                                    scalar=float(C), in1=tmpf[:, 0:K, :], op0=ALU.mult, op1=ALU.add))
                chain.link(dve.tensor_scalar(tmpf[:, 0:K, :], validf[:, 0:K, :], -float(SKIP), float(SKIP), ALU.mult, ALU.add))
                dve.tensor_copy(all_i[L.n][:, 0:K, bass.ts(i, 2)], slotf[:, 0:K, :])
                dve.tensor_tensor(all_w[L.n][:, 0:K, bass.ts(i, 2)], weight[:, 0:K, :], validf[:, 0:K, :], ALU.mult)
                dve.tensor_tensor(scatter_i[:, 0:K, :], slotf[:, 0:K, :], tmpf[:, 0:K, :], ALU.add).then_inc(L.scatter_ready, 1)
                if L is L1:
                    chain.link(dve.tensor_tensor(weight[:, 0:K, :], weight[:, 0:K, :], validf[:, 0:K, :], ALU.mult))
                    for k in range(K):
                        last = dve.tensor_tensor(product[:, k, :, :], onehot[:, k, :, :], over(weight[:, k, :], 2, [P, 2, E]), ALU.mult)
                    chain.link(last)
                    chain.link(dve.tensor_tensor(product[:, 0, :, :], product[:, 0, :, :], product[:, 1, :, :], ALU.add))
                    dve.tensor_tensor(gates_e[:, :, :], product[:, 0, :, :], product[:, 2, :, :], ALU.add).then_inc(L.gates_ready, 1)
                chain.end()

            def add_b2(i):
                wait(dve, L1.back_full, i * L1.NB + 7)
                hp = h[:, bass.ts(i, 2), :]
                dve.tensor_tensor(hp, hp, back_bank[:, :].rearrange("p (t d) -> p t d", t=2), ALU.add).then_inc(L1.back_free, 1)

            def pairs(L):
                def body(i, first, last):
                    greatest(L, i, 0)
                    if not first:
                        choose(L, i - 1)
                    greatest(L, i, 1)
                    if not first:
                        place(L, i - 1)
                    if not last:
                        front_a(L, i + 1, False)
                    keep_turned(L, i, 0)
                    if not last:
                        front_b(L, i + 1, isinstance(i, int) and i + 2 == PAIRS)
                    normalise(L, i, 0)
                    keep_turned(L, i, 1)
                    if not last:
                        front_c(L, i + 1)
                    if not first and L is L1:
                        add_b2(i - 1)
                    normalise(L, i, 1)
                    if not last:
                        front_d(L, i + 1)
                    residual(L, i)
                    expert_input(L, i)

                dve.memset(running[:, :], 0.0).then_inc(L.running_zero, 1)
                dve.wait_ge(L.running_zero, 1)
                if L is L1:
                    pair_indices(0)
                front_a(L, 0, True)
                front_b(L, 0, False)
                front_c(L, 0)
                front_d(L, 0)
                body(0, True, False)
                with dve.Fori(1, PAIRS - 2) as i:
                    body(i, False, False)
                body(PAIRS - 2, False, False)
                body(PAIRS - 1, False, True)
                choose(L, PAIRS - 1)
                place(L, PAIRS - 1)
                if L is L1:
                    add_b2(PAIRS - 1)

            dve.wait_ge(router_in, 16 * ROUTER_LOADS)
            pairs(L0)

            dve.wait_ge(L0.input_added, PAIRS)

            def shared_mlp(q, first, last):
                for j, (f, m) in enumerate(FT):
                    wait(dve, sh_silu, 3 * q + j + 1)
                    wait(dve, sh_y, 2 * q)
                    dve.tensor_tensor(shT[0:m, j, :], silu[j][0:m, :], bank[GU[j] + 1][0:m, :], ALU.mult).then_inc(sh_hid, 1)
                for half in range(2):
                    wait(dve, sh_y, 2 * q + half + 1)
                    hp = h[:, bass.ds(4 * q + 2 * half, 2), :]
                    dve.tensor_tensor(hp, hp, bank[6 + half][:, :].rearrange("p (t d) -> p t d", t=2), ALU.add).then_inc(sh_add, 1)

            loop(dve, N // BANK, shared_mlp)

            def keep_rows_b(i, u):
                e = 2 * i + u
                wait(dve, ex_full, e + 1)
                wait(dve, e_gu, NFT * (e - 1))
                for c in range(DC):
                    last = dve.tensor_copy(erowsT[u][:, c, :], bank[c][:, 0:C0])
                last.then_inc(ex_free, 1)

            def hidden_b(i, u):
                e = 2 * i + u
                for j, (f, m) in enumerate(FT):
                    s = (NFT * u + j) % 2
                    wait(dve, e_silu, NFT * e + j + 1)
                    wait(dve, e_y, NCT * (e - 1))
                    dve.tensor_tensor(hidT[u][0:m, j, :], silu[s][0:m, 0:C0], bank[3 + 2 * s][0:m, 0:C0], ALU.mult).then_inc(e_hid, 1)

            def result_b(i, u):
                e = 2 * i + u
                wait(dve, ey_out[u], 32 * i)
                for s, (r, m) in enumerate(CT):
                    wait(dve, e_y, NCT * e + s + 1)
                    dve.tensor_copy(yrows[u][0:m, s, :], bank[6 + (NCT * u + s) % 2][0:m, 0:D]).then_inc(e_yfree, 1)

            def experts_b(i, first, last):
                for u in range(2):
                    if not last:
                        keep_rows_b(i + 1, u)
                    if u == 0:
                        hidden_b(i, 1)
                    elif not last:
                        hidden_b(i + 1, 0)
                    result_b(i, u)

            keep_rows_b(0, 0)
            keep_rows_b(0, 1)
            hidden_b(0, 0)
            loop(dve, NE0 // 2, experts_b)

            pairs(L1)

            def keep_rows_d(i, v_):
                i, u = later(i, v_)
                e = RING1 * i + u
                wait(dve, dx_full, e + 1)
                wait(dve, dh_full, 2 * e - 2)
                dve.tensor_copy(drowsT[:, u % 2, :, :], bank[u % 2][:, 0:D].rearrange("p (c n) -> p c n", c=DC)).then_inc(dx_free, 1)

            def experts_d(i, first, last):
                for u in range(RING1):
                    e = RING1 * i + u
                    if not (last and u + 2 >= RING1):
                        keep_rows_d(i, u + 2)
                    wait(dve, dy_full, e + 1)
                    wait(dve, dy_out[u % 2], 16 * ((RING1 // 2) * i + u // 2))
                    dve.tensor_copy(dy[:, u % 2, :], bank[6 + u % 2][:, 0:D]).then_inc(dy_free, 1)

            keep_rows_d(0, 0)
            keep_rows_d(0, 1)
            loop(dve, NE1 // RING1, experts_d)

            def tile_indices(i, t):
                dve.tensor_copy(pair_w[:, :, t:t + 1], all_w[1][:, :, bass.ds(2 * i + t, 1)])
                dve.tensor_copy(pair_i[:, :, t:t + 1], all_i[1][:, :, bass.ds(2 * i + t, 1)]).then_inc(fin_index[t], 1)
                wait(dve, fin_index[t], i + 1)

            def final_sum(i, first, last):
                for t in range(2):
                    wait(dve, fin_gathered[t], 16 * K1 * (i + 1))
                    ht = h_tile(i)(t)
                    for k in range(K1):
                        add = dve.scalar_tensor_tensor(out=ht, in0=gathered[:, t, k, :], scalar=pair_w[:, k, t:t + 1],
                                                       in1=ht, op0=ALU.mult, op1=ALU.add)
                        if k < K1 - 1:
                            add.then_inc(fin_steps, 1)
                            wait(dve, fin_steps, (K1 - 1) * (2 * i + t) + k + 1)
                    add.then_inc(out_ready, 1)
                    wait(dve, out_ready, 2 * i + t + 1)
                    if not last:
                        tile_indices(i + 1, t)

            tile_indices(0, 0)
            tile_indices(0, 1)
            loop(dve, PAIRS, final_sum)


NAMES = ["x", "L0_tok_conv_w", "L0_tok_conv_b", "L0_tok_ln_gamma", "L0_tok_ln_beta", "L0_attn_Wq", "L0_attn_Wk",
         "L0_attn_Wv", "L0_attn_Wo", "L0_ffn_router_w", "L0_ffn_router_b", "L0_ffn_w_gate", "L0_ffn_w_up",
         "L0_ffn_w_down", "L0_ffn_sw_gate", "L0_ffn_sw_up", "L0_ffn_sw_down", "L1_attn_w_qkv", "L1_attn_w_out",
         "L1_ffn_gate_w", "L1_ffn_gate_b", "L1_ffn_w1", "L1_ffn_b1", "L1_ffn_w2", "L1_ffn_b2"]


def kernel(**inputs):
    import numpy as np
    from concourse import bacc
    from concourse.bass_utils import run_bass_kernel_spmd

    nc = bacc.Bacc("TRN2", target_bir_lowering=False, num_devices=1)
    arrays = {name: np.ascontiguousarray(inputs[name]) for name in NAMES}
    a = {name: nc.dram_tensor(name, arrays[name].shape, F32, kind="ExternalInput").ap() for name in NAMES}
    b, tokens, d = arrays["x"].shape
    out = nc.dram_tensor("out", [b, tokens // 2, d], F32, kind="ExternalOutput").ap()
    build(nc, a, out)
    return run_bass_kernel_spmd(nc, [arrays], core_ids=[0]).results[0]["out"]
```

```python
from contextlib import ExitStack

import concourse.bass as bass
from concourse import mybir

F32 = mybir.dt.float32
F32R = mybir.dt.float32r
BF16 = mybir.dt.bfloat16
I32 = mybir.dt.int32
U32 = mybir.dt.uint32
ALU = mybir.AluOpType
ACT = mybir.ActivationFunctionType
AX = mybir.AxisListType

P = 128
D = 256
DC = D // P
HEADS = 16
HD = D // HEADS
WINDOW = 64
EPS = 1e-5
BANK = 512
SCALE = HD ** -0.5
HEADS_PER_BANK = BANK // P
SBANKS = HEADS // HEADS_PER_BANK
MASKED = -1e30
SKIP = 1 << 20
GATE_SUM_EPS = 1e-9


def wait(eng, sem, count):
    if not isinstance(count, int) or count > 0:
        eng.wait_ge(sem, count)


def settle(eng, i):
    if not isinstance(i, int):
        eng.nop(nofuse=True)


class Chain:

    def __init__(self, eng, sem, call, steps):
        self.eng, self.sem, self.base, self.steps, self.n = eng, sem, call * steps, steps, 0

    def link(self, instruction):
        instruction.then_inc(self.sem, 1)
        self.n += 1
        self.eng.wait_ge(self.sem, self.base + self.n)

    def end(self):
        assert self.n == self.steps, (self.n, self.steps)


def loop(eng, count, body):
    body(0, True, count == 1)
    if count > 2:
        with eng.Fori(1, count - 1) as i:
            body(i, False, False)
    if count > 1:
        body(count - 1, False, True)


def skewed_loop(eng, count, lead, body):
    for i in range(lead):
        body(i)
    with eng.Fori(lead, count - 1) as i:
        body(i)
    for i in range(count - 1, count + lead):
        body(i)


def there(j, count):
    return not isinstance(j, int) or 0 <= j < count


def split(eng, high, low, value):
    return eng.tensor_tensor(low, value, high.bitcast(F32), ALU.subtract)


def over(ap, axis, shape):
    return ap.unsqueeze(axis).to_broadcast(shape)


class Layer:

    def __init__(self, sem, n):
        self.n = n
        self.x_loaded = sem(f"x_loaded_{n}")
        self.x_summed = sem(f"x_summed_{n}")
        self.score_full = sem(f"score_full_{n}")
        self.max_done = sem(f"max_done_{n}")
        self.exp_done = sem(f"exp_done_{n}")
        self.turn_full = sem(f"turn_full_{n}")
        self.turned = sem(f"turned_{n}")
        self.pv_done = sem(f"pv_done_{n}")
        self.inv_done = sem(f"inv_done_{n}")
        self.mix_done = sem(f"mix_done_{n}")
        self.back_full = sem(f"back_full_{n}")
        self.back_free = sem(f"back_free_{n}")
        self.scattered = sem(f"scattered_{n}")
        self.tok_biased = sem(f"tok_biased_{n}")
        self.tok_normed = sem(f"tok_normed_{n}")
        self.tok_scaled = sem(f"tok_scaled_{n}")
        self.h_ready = sem(f"h_ready_{n}")
        self.normed_ready = sem(f"normed_ready_{n}")
        self.ffn_ready = sem(f"ffn_ready_{n}")
        self.to_exp = sem(f"to_exp_{n}")
        self.from_exp = sem(f"from_exp_{n}")
        self.route_steps = sem(f"route_steps_{n}")
        self.chosen_ready = sem(f"chosen_ready_{n}")
        self.slot_steps = sem(f"slot_steps_{n}")
        self.scatter_ready = sem(f"scatter_ready_{n}")
        self.running_zero = sem(f"running_zero_{n}")
        self.input_added = sem(f"input_added_{n}")
        self.stat_steps = [sem(f"stat_steps_{n}{w}") for w in range(3)]
        self.moments_ready = [sem(f"moments_ready_{n}{w}") for w in range(3)]
        self.eps_added = [sem(f"eps_added_{n}{w}") for w in range(3)]
        self.rstd_ready = [sem(f"rstd_ready_{n}{w}") for w in range(3)]
        self.front_full = [sem(f"front_full_{n}{b}") for b in range(2)]
        self.front_free = [sem(f"front_free_{n}{b}") for b in range(2)]


def build(nc, a, out):
    B, TOK, _ = a["x"].shape
    S = TOK // 2
    PAIRS = B // 2
    NE0, _, F0 = a["L0_ffn_w_gate"].shape
    NE1, _, F1 = a["L1_ffn_w1"].shape
    K0, K1 = 2, 3
    N = B * S
    C0 = -(-5 * N * K0 // (4 * NE0))
    C1 = 128
    FT = [(j * P, min(P, F0 - j * P)) for j in range(-(-F0 // P))]
    CT = [(j * P, min(P, C0 - j * P)) for j in range(-(-C0 // P))]
    NFT, NCT = len(FT), len(CT)
    J1 = F1 // P
    RING1 = 4
    assert S == P and C1 == P and B % 2 == 0 and NFT == 3 and NCT == 3

    ctx = ExitStack()
    with ctx:
        def sb(name, shape, dt=F32):
            return ctx.enter_context(nc.sbuf_tensor(name, shape, dt))

        def sem(name):
            return ctx.enter_context(nc.semaphore(name))

        CODE, EXPERT, WEIGHT, ROW = D, D + 1, D + 1 + K1, D + 8
        rows0 = nc.dram_tensor("rows0", [NE0 * C0, ROW], F32, kind="Internal").ap()
        rows1 = nc.dram_tensor("rows1", [NE1 * C1, ROW], F32, kind="Internal").ap()
        stream = nc.dram_tensor("stream", [N + NCT * P, D], F32, kind="Internal").ap()

        bank = [ctx.enter_context(nc.psum_tensor(f"bank{n}", [P, BANK], F32)) for n in range(8)]
        score_bank, turn_bank, mix_bank = bank[0:2], bank[2:4], bank[4]
        front_bank, back_bank = bank[5:7], bank[7]

        ident = sb("ident", [P, P])
        ones_f = sb("ones_f", [P, P])
        zeros = sb("zeros", [P, BANK])
        mask0 = sb("mask0", [P, P])
        mask1 = sb("mask1", [P, P])
        before = sb("before", [P, P], BF16)
        ones_b = sb("ones_b", [P, P], BF16)
        parity = sb("parity", [P, 2])
        row_id = sb("row_id", [P, 2], I32)
        row_f = sb("row_f", [P, 1])
        half_neg = sb("half_neg", [P, 2])
        iota_e = sb("iota_e", [P, NE1])
        router0 = sb("router0", [P, DC, NE0])
        router1 = sb("router1", [P, DC, NE1])
        conv_b = sb("conv_b", [P, D])
        gamma = sb("gamma", [P, D])
        beta = sb("beta", [P, D])
        rb0 = sb("rb0", [P, NE0])
        rb1 = sb("rb1", [P, NE1])
        b1T = sb("b1T", [P, J1, NE1])
        normed = sb("normed", [P, 2, D])
        normedT = sb("normedT", [P, DC, 2 * P])
        qT = sb("qT", [P, DC, 2, P])
        kT = sb("kT", [P, DC, 2, 2, P])
        HALF = (P // HD) * (P + HD)
        v_wide = sb("v_wide", [P, 2 * DC, HALF])
        probsT = sb("probsT", [P, SBANKS, BANK])
        neg_max = sb("neg_max", [P, 2, HEADS])
        exp_sum = sb("exp_sum", [P, 2, HEADS])
        exp_inv = sb("exp_inv", [P, 2, HEADS])
        own_rows = sb("own_rows", [HEADS, D])
        exp_invT = sb("exp_invT", [HEADS, 2 * P])
        inv_rows = sb("inv_rows", [P, DC, 2 * P])
        mixedT = sb("mixedT", [P, DC, 2 * P])
        ffn_in = sb("ffn_in", [P, 2, ROW])
        ffn_inT = sb("ffn_inT", [P, DC, 2 * P])
        slot_match = sb("slot_match", [P, RING1, NCT, K1])
        slot_gate = sb("slot_gate", [P, RING1, NCT])
        slot_empty = sb("slot_empty", [P, RING1, NCT])
        slot_token = sb("slot_token", [P, RING1, NCT], I32)
        empty_row = sb("empty_row", [P, NCT])
        stats = sb("stats", [P, 3, 2, 6])
        moments = sb("moments", [P, 3, 2, 2])
        rstd = sb("rstd", [P, 3, 2])
        var_eps = sb("var_eps", [P, 3, 2])
        logits = sb("logits", [P, 2, NE1])
        shifted = sb("shifted", [P, 2, NE1])
        gate_p = sb("gate_p", [P, 2, NE1])
        top_v = sb("top_v", [P, 2, 8])
        top_m = sb("top_m", [P, 2, 8])
        top_i = sb("top_i", [P, 2, 8], U32)
        top_f = sb("top_f", [P, 2, 8])
        rsmall = sb("rsmall", [P, 8, 2])
        onehot = sb("onehot", [P, K1, 2, NE1])
        chosen = sb("chosen", [P, 2, NE1], BF16)
        earlier = sb("earlier", [P, 2, NE1], BF16)
        running = sb("running", [P, NE1], BF16)
        count_sb = sb("count_sb", [P, 2, NE1])
        product = sb("product", [P, K1, 2, NE1])
        posf = sb("posf", [P, K1, 2])
        slotf = sb("slotf", [P, K1, 2])
        tmpf = sb("tmpf", [P, K1, 2])
        validf = sb("validf", [P, K1, 2])
        weight = sb("weight", [P, K1, 2])
        scatter_i = sb("scatter_i", [P, K1, 2], I32)
        code = sb("code", [P, B])
        SLOT1 = 2 * F1 * DC
        arena = sb("arena", [P, RING1 * SLOT1])
        at = [0]

        def part(n):
            at[0] += n
            assert at[0] <= RING1 * SLOT1
            return arena[:, at[0] - n:at[0]]

        all_inT = part(DC * N).rearrange("p (c n) -> p c n", c=DC)
        gate_w = [part(DC * F0).rearrange("p (c f) -> p c f", c=DC) for _ in range(2)]
        up_w = [part(DC * F0).rearrange("p (c f) -> p c f", c=DC) for _ in range(2)]
        down_w = [part(NFT * D).rearrange("p (j d) -> p j d", j=NFT) for _ in range(2)]
        erowsT = [part(DC * C0).rearrange("p (c n) -> p c n", c=DC) for _ in range(2)]
        hidden = part(2 * NFT * C0)
        hidT = [hidden[:, u * NFT * C0:(u + 1) * NFT * C0].rearrange("p (j n) -> p j n", j=NFT) for u in range(2)]
        silu = [part(BANK) for _ in range(3)]
        shT = hidden[:, 0:NFT * BANK].rearrange("p (j n) -> p j n", j=NFT)
        yrows = [part(NCT * D).rearrange("p (s d) -> p s d", s=NCT) for _ in range(2)]
        w1_sb = [arena[:, s * SLOT1:s * SLOT1 + DC * F1].rearrange("p (c f) -> p c f", c=DC) for s in range(RING1)]
        w2_sb = [arena[:, s * SLOT1 + DC * F1:(s + 1) * SLOT1].rearrange("p (j d) -> p j d", j=J1) for s in range(RING1)]
        flat = probsT[:, :, :].rearrange("p b n -> p (b n)")
        drows = sb("drows", [P, RING1, ROW])
        drowsT = flat[:, 0:2 * D].rearrange("p (u c n) -> p u c n", u=2, c=DC)
        dy = flat[:, 2 * D:4 * D].rearrange("p (u d) -> p u d", u=2)
        b2_raw = flat[0:NE1, 4 * D:5 * D]
        ctx_abc = ExitStack()

        def sb_abc(name, shape):
            return ctx_abc.enter_context(nc.sbuf_tensor(name, shape, F32))

        probs = sb_abc("probs", [P, 2, HEADS, P])
        conv_wT = sb_abc("conv_wT", [P, 2 * DC, D])
        wT0 = sb_abc("wT0", [P, 4, DC, D])
        w_qkv = sb_abc("w_qkv", [P, DC, 3 * D])
        w_out = sb_abc("w_out", [P, DC, D])
        sw_gate = sb_abc("sw_gate", [P, DC, F0])
        sw_up = sb_abc("sw_up", [P, DC, F0])
        sw_down = sb_abc("sw_down", [P, NFT, D])
        early = sb_abc("early", [P, 12 * D])
        h = sb_abc("h", [P, B, D])
        x_in = early[:, 0:4 * D].rearrange("p (t d) -> p t d", t=2)
        x_sum = early[:, 4 * D:6 * D].rearrange("p (t d) -> p t d", t=2)
        tok = early[:, 6 * D:8 * D].rearrange("p (t d) -> p t d", t=2)
        xT = early[:, 8 * D:12 * D].rearrange("p (t c n) -> p t c n", t=2, c=2 * DC)
        erows = early[:, 0:2 * NCT * ROW].rearrange("p (u s d) -> p u s d", u=2, s=NCT)
        stage = probs[:, :, :, :].rearrange("p a b c -> p (a b c)")
        conv_raw = stage[:, 0:2 * 2 * D].rearrange("p (m f) -> p m f", m=2)
        w_raw = stage[:, 4 * D:12 * D].rearrange("p (w m d) -> p w m d", w=4, m=2)
        b1_raw = stage[0:NE1, 12 * D:12 * D + F1]
        ctx_abc.close()
        hidden_high = sb("hidden_high", [P, 2, J1, P], F32R)
        hidden_low = sb("hidden_low", [P, 2, J1, P], F32R)
        w2_high = sb("w2_high", [P, 2, J1, D], F32R)
        w2_low = sb("w2_low", [P, 2, J1, D], F32R)
        dhidT = sb("dhidT", [P, 2, J1, P])
        b2_high = sb("b2_high", [NE1, D], F32R)
        b2_low = sb("b2_low", [NE1, D], F32R)
        chooser = sb("chooser", [NE1, 2, P], F32R)

        raw_in, dense_in, router_in, fill0, fill1, fill_stream = (
            sem("raw_in"), sem("dense_in"), sem("router_in"), sem("fill0"), sem("fill1"), sem("fill_stream"))
        const_p, const_d, prep_full, prep_free = sem("const_p"), sem("const_d"), sem("prep_full"), sem("prep_free")

        layers = []
        for n in range(2):
            L = Layer(sem, n)
            L.NF = 8 if n == 0 else 4
            L.KF = L.NF - 4
            L.NB = 6
            L.E, L.K, L.C = (NE0, K0, C0) if n == 0 else (NE1, K1, C1)
            L.mask = mask0 if n == 0 else mask1
            L.rows = rows0 if n == 0 else rows1
            L.rw, L.rb = (router0, rb0) if n == 0 else (router1, rb1)
            if n == 0:
                L.w = [lambda c, o, w=w: wT0[:, w, c, o] for w in range(4)]
            else:
                L.w = [lambda c, o, w=w: w_qkv[:, c, w * D + o.start:w * D + o.stop] for w in range(3)]
                L.w.append(lambda c, o: w_out[:, c, o])
            layers.append(L)
        L0, L1 = layers

        sh_gu, sh_silu, sh_hid, sh_y, sh_add = (sem(s) for s in ("sh_gu", "sh_silu", "sh_hid", "sh_y", "sh_add"))
        ew_in = [sem(f"ew_in{s}") for s in range(2)]
        ed_in = [sem(f"ed_in{s}") for s in range(2)]
        er_in = [sem(f"er_in{s}") for s in range(2)]
        slot_steps = sem("slot_steps")
        e_slots, e_added, h_stored, h_loaded, h_loaded_rest = (
            sem(s) for s in ("e_slots", "e_added", "h_stored", "h_loaded", "h_loaded_rest"))
        ex_full, ex_free, e_gu, e_silu, e_hid, e_y, e_yfree = (
            sem(s) for s in ("ex_full", "ex_free", "e_gu", "e_silu", "e_hid", "e_y", "e_yfree"))
        dw1_in = [sem(f"dw1_in{s}") for s in range(RING1)]
        dw2_in = [sem(f"dw2_in{s}") for s in range(RING1)]
        dr_in = [sem(f"dr_in{s}") for s in range(RING1)]
        d_slots, d_steps, d_added, h_final = (sem(s) for s in ("d_slots", "d_steps", "d_added", "h_final"))
        dx_full, dx_free, dh_full, dh_done, dy_full, dy_free = (
            sem(s) for s in ("dx_full", "dx_free", "dh_full", "dh_done", "dy_full", "dy_free"))
        out_done, b2_in, b2_rounded, b2_split, chooser_ready = (
            sem(s) for s in ("out_done", "b2_in", "b2_rounded", "b2_split", "chooser_ready"))
        w2_rounded, hid_rounded, hid_split, w2_split_dve, w2_split_pool = (
            sem(s) for s in ("w2_rounded", "hid_rounded", "hid_split", "w2_split_dve", "w2_split_pool"))
        FILL = 4 * BANK
        FILLS = [-(-r.shape[0] * r.shape[1] // (P * FILL)) for r in (rows0, rows1)]

        def front(L, i, k):
            return k % 2, i * (L.NF // 2) + k // 2

        L0.fill, L1.fill = fill0, fill1
        GU = (2, 4, 0)
        ROUTER_LOADS = 8 + NFT
        ROUTE_STEPS, SLOT_STEPS = (14, 10), (5, 5)

        def head(b, j):
            return 8 * (j // 2) + 2 * b + j % 2

        W2_DVE = J1 - 2

        def later(i, u):
            return (i + 1, u - RING1) if u >= RING1 else (i, u)

        block = ctx.enter_context(nc.Block())

        @block.sync
        def _(sp):
            x_rows = a["x"].rearrange("b (t k) d -> b t (k d)", k=2)

            def load_x(i, first):
                if not first:
                    for k in range(2):
                        b, n = front(L0, i - 1, k)
                        wait(sp, L0.front_full[b], n + 1)
                    wait(sp, L0.x_summed, i)
                sp.dma_start(x_in[:, :, :], x_rows[bass.ts(i, 2)].rearrange("b t f -> t b f")).then_inc(L0.x_loaded, 16)

            sp.dma_start(conv_raw, a["L0_tok_conv_w"].rearrange("(m o) i k -> o m (i k)", m=2)).then_inc(raw_in, 16)
            load_x(0, True)
            for w, name in enumerate(("Wq", "Wk", "Wv", "Wo")):
                sp.dma_start(w_raw[:, w], a[f"L0_attn_{name}"].rearrange("(m o) d -> o m d", m=2)).then_inc(raw_in, 16)
            sp.dma_start(b1_raw, a["L1_ffn_b1"]).then_inc(raw_in, 16)

            def shared_row(dst, src):
                sp.dma_start(dst, src.rearrange("(a n) -> a n", a=1).to_broadcast([P, src.shape[0]])).then_inc(dense_in, 16)

            shared_row(conv_b[:, :], a["L0_tok_conv_b"])
            shared_row(gamma[:, :], a["L0_tok_ln_gamma"])
            shared_row(beta[:, :], a["L0_tok_ln_beta"])
            def whole(dst, src):
                sp.dma_start(dst, src).then_inc(router_in, 16)

            whole(router0[:, :, :], a["L0_ffn_router_w"].rearrange("(c p) e -> p c e", p=P))
            whole(rb0[:, :], a["L0_ffn_router_b"].rearrange("(a n) -> a n", a=1).to_broadcast([P, NE0]))
            whole(router1[:, :, :], a["L1_ffn_gate_w"].rearrange("(c p) e -> p c e", p=P))
            whole(rb1[:, :], a["L1_ffn_gate_b"].rearrange("(a n) -> a n", a=1).to_broadcast([P, NE1]))
            whole(w_qkv[:, :, :], a["L1_attn_w_qkv"].rearrange("(c p) e -> p c e", p=P))
            whole(w_out[:, :, :], a["L1_attn_w_out"].rearrange("(c p) e -> p c e", p=P))
            whole(sw_gate[:, :, :], a["L0_ffn_sw_gate"].rearrange("(c p) e -> p c e", p=P))
            whole(sw_up[:, :, :], a["L0_ffn_sw_up"].rearrange("(c p) e -> p c e", p=P))
            for j, (f, m) in enumerate(FT):
                whole(sw_down[0:m, j, :], a["L0_ffn_sw_down"][f:f + m, :])

            def load_gate_up(e, u, first):
                if not first:
                    wait(sp, e_gu, (e - 1) * NFT)
                s = ew_in[u % 2]
                sp.dma_start(gate_w[u % 2], a["L0_ffn_w_gate"][bass.ds(e, 1)].rearrange("a (p c) f -> p (a c) f", c=DC)).then_inc(s, 16)
                sp.dma_start(up_w[u % 2], a["L0_ffn_w_up"][bass.ds(e, 1)].rearrange("a (p c) f -> p (a c) f", c=DC)).then_inc(s, 16)

            def load_down(e, u, first):
                if not first:
                    wait(sp, e_y, (e - 1) * NCT)
                s = ed_in[u % 2]
                full = sum(m == P for _, m in FT)
                sp.dma_start(down_w[u % 2][:, 0:full, :],
                             a["L0_ffn_w_down"][bass.ds(e, 1), 0:full * P].rearrange("a (j p) d -> p (a j) d", p=P)).then_inc(s, 16)
                sp.dma_start(down_w[u % 2][0:F0 - full * P, full:full + 1, :],
                             a["L0_ffn_w_down"][bass.ds(e, 1), full * P:F0].rearrange("a p d -> p a d")).then_inc(s, 16)

            full = sum(m == P for _, m in CT)

            def load_rows(e, u, first):
                if not first:
                    wait(sp, ex_full, e - 1)
                    wait(sp, e_slots, e - 1)
                s = er_in[u % 2]
                sp.dma_start(erows[:, u % 2, 0:full, :], rows0[bass.ds(e * C0, full * P)].rearrange("(s p) d -> p s d", p=P)).then_inc(s, 16)
                sp.dma_start(erows[0:C0 - full * P, u % 2, full, :], rows0[bass.ds(e * C0 + full * P, C0 - full * P)]).then_inc(s, 16)

            for u in range(2):
                load_gate_up(u, u, True)
                load_down(u, u, True)
            def fill_zeros():
                for rows, fill in ((rows0, fill0), (rows1, fill1)):
                    flat = rows.rearrange("r d -> (r d)")
                    for at in range(0, flat.shape[0], P * FILL):
                        n = min(P * FILL, flat.shape[0] - at) // P
                        w = min(n, BANK)
                        sp.dma_start(flat[at:at + n * P].rearrange("(p r n) -> p r n", p=P, n=w),
                                      over(zeros[:, 0:w], 1, [P, n // w, w])).then_inc(fill, 16)
                sp.dma_start(stream[N:].rearrange("(s p) d -> p s d", p=P), over(zeros[:, 0:D], 1, [P, NCT, D])).then_inc(fill_stream, 16)

            load_x(1, False)
            sp.wait_ge(const_p, 1)
            fill_zeros()
            with sp.Fori(2, PAIRS) as i:
                load_x(i, False)

            sp.wait_ge(L0.scattered, 16 * 2 * K0 * PAIRS)
            load_rows(0, 0, True)
            load_rows(1, 1, True)

            def experts_b(i):
                for u in range(2):
                    e = 2 * i + u
                    if not (isinstance(i, int) and e + 3 >= NE0):
                        load_rows(e + 3, u + 3, False)
                        load_gate_up(e + 3, u + 3, False)
                    load_down(e + 2, u, False)

            stream_rows = stream[0:N].rearrange("(b p) d -> p b d", p=P)
            sp.wait_ge(sh_add, 2 * (N // BANK))
            sp.dma_start(stream_rows, h[:, :, :]).then_inc(h_stored, 16)
            load_rows(2, 2, False)
            load_gate_up(2, 2, False)
            experts_b(0)
            with sp.Fori(1, NE0 // 2 - 2) as i:
                experts_b(i)
            experts_b(NE0 // 2 - 2)
            sp.wait_ge(e_added, 16 * NCT * NE0)
            sp.dma_start(h[:, 0:2, :], stream_rows[:, 0:2, :]).then_inc(h_loaded, 16)
            sp.dma_start(h[:, 2:B, :], stream_rows[:, 2:B, :]).then_inc(h_loaded_rest, 16)

            def load_w1(e, u, first):
                if not first:
                    wait(sp, dh_full, 2 * (e - RING1) + 2)
                sp.dma_start(w1_sb[u], a["L1_ffn_w1"][bass.ds(e, 1)].rearrange("a (p c) f -> p (a c) f", c=DC)).then_inc(dw1_in[u], 16)

            def load_w2(e, u, first):
                if not first:
                    wait(sp, w2_split_dve, 2 * (e - RING1) + 2)
                    wait(sp, w2_split_pool, e - RING1 + 1)
                sp.dma_start(w2_sb[u], a["L1_ffn_w2"][bass.ds(e, 1)].rearrange("a (p j) d -> p (a j) d", j=J1)).then_inc(dw2_in[u], 16)

            def load_dr(e, u, first):
                if not first:
                    wait(sp, dx_full, e - RING1 + 1)
                    wait(sp, d_slots, e - RING1 + 1)
                sp.dma_start(drows[:, u, :], rows1[bass.ds(e * C1, C1)]).then_inc(dr_in[u], 16)

            for u in range(RING1):
                load_w1(u, u, True)
                load_w2(u, u, True)
            sp.wait_ge(L1.back_free, (PAIRS - 1) * L1.NB + 3)
            sp.dma_start(stream_rows, h[:, :, :]).then_inc(h_final, 16)
            sp.wait_ge(L1.scattered, 16 * 2 * K1 * PAIRS)
            for u in range(RING1):
                load_dr(u, u, True)
            sp.dma_start(b2_raw, a["L1_ffn_b2"]).then_inc(b2_in, 16)

            def experts_d(i, first, last):
                for u in range(RING1):
                    e = RING1 * i + u
                    load_w1(e + RING1, u, False)
                    load_dr(e + RING1, u, False)
                    load_w2(e + RING1, u, False)

            loop(sp, NE1 // RING1 - 1, experts_d)

            sp.wait_ge(d_added, 16 * NE1)
            sp.dma_start(out.rearrange("b p d -> (b p) d"), stream[0:N]).then_inc(out_done, 16)
            sp.wait_ge(out_done, 16)

        @block.gpsimd
        def _(pool):
            g = nc.gpsimd
            g.memset(zeros[:, :], 0.0).then_inc(const_p, 1)
            g.memset(ident[:, :], 0.0).then_inc(const_p, 1)
            g.memset(ones_f[:, :], 1.0).then_inc(const_p, 1)
            g.memset(half_neg[:, :], -0.5).then_inc(const_p, 1)
            g.memset(mask0[:, :], 0.0).then_inc(const_p, 1)
            g.memset(mask1[:, :], 0.0).then_inc(const_p, 1)
            g.iota(code[:, :], [[P, B]], base=1, channel_multiplier=1, allow_small_or_imprecise_dtypes=True).then_inc(const_p, 1)
            g.iota(empty_row[:, :], [[P, NCT]], base=N + 1, channel_multiplier=1, allow_small_or_imprecise_dtypes=True).then_inc(const_p, 1)
            g.memset(ffn_in[:, :, D:ROW], 0.0).then_inc(const_p, 1)
            g.memset(v_wide[:, :, :], 0.0).then_inc(const_p, 1)
            g.memset(own_rows[:, :], 1.0).then_inc(const_p, 1)
            g.iota(row_id[:, 0:1], [[0, 1]], base=0, channel_multiplier=1).then_inc(const_p, 1)
            g.iota(iota_e[:, :], [[1, NE1]], base=0, channel_multiplier=0, allow_small_or_imprecise_dtypes=True).then_inc(const_p, 1)
            pool.wait_ge(const_p, 13)
            g.affine_select(out=ident[:, :], in_=ident[:, :], compare_op=ALU.not_equal, fill=1.0, base=0,
                            pattern=[[-1, P]], channel_multiplier=1).then_inc(const_p, 1)
            g.affine_select(out=mask0[:, :], in_=mask0[:, :], compare_op=ALU.is_ge, fill=MASKED, base=0,
                            pattern=[[-1, P]], channel_multiplier=1).then_inc(const_p, 1)
            g.affine_select(out=mask1[:, :], in_=mask1[:, :], compare_op=ALU.is_ge, fill=MASKED, base=0,
                            pattern=[[-1, P]], channel_multiplier=1).then_inc(const_p, 1)
            g.affine_select(out=before[:, :], in_=ones_f[:, :], compare_op=ALU.is_gt, fill=0.0, base=0,
                            pattern=[[1, P]], channel_multiplier=-1).then_inc(const_p, 1)
            g.affine_select(out=own_rows[:, :], in_=own_rows[:, :], compare_op=ALU.is_ge, fill=0.0, base=0,
                            pattern=[[1, D]], channel_multiplier=-HD).then_inc(const_p, 1)
            pool.wait_ge(const_p, 18)
            g.affine_select(out=own_rows[:, :], in_=own_rows[:, :], compare_op=ALU.is_ge, fill=0.0, base=HD - 1,
                            pattern=[[-1, D]], channel_multiplier=HD).then_inc(const_p, 1)
            g.affine_select(out=mask0[:, :], in_=mask0[:, :], compare_op=ALU.is_gt, fill=MASKED, base=WINDOW,
                            pattern=[[1, P]], channel_multiplier=-1).then_inc(const_p, 1)
            pool.wait_ge(const_p, 20)

            def ln_scale(L, w, i):
                wait(pool, L.moments_ready[w], i + 1)
                settle(pool, i)
                g.tensor_scalar(var_eps[:, w, :], moments[:, w, :, 1], EPS, None, ALU.add).then_inc(L.eps_added[w], 1)
                pool.wait_ge(L.eps_added[w], i + 1)
                g.tensor_tensor(rstd[:, w, :], var_eps[:, w, :], half_neg[:, :], ALU.pow).then_inc(L.rstd_ready[w], 1)

            def sum_x(i):
                wait(pool, L0.x_loaded, 16 * (i + 1))
                wait(pool, L0.tok_biased, 2 * i)
                g.tensor_tensor(x_sum[:, :, :], x_in[:, :, 0:D], x_in[:, :, D:2 * D], ALU.add).then_inc(L0.x_summed, 1)

            def affine(i, first):
                wait(pool, L0.tok_normed, i + 1)
                if first:
                    pool.wait_ge(dense_in, 48)
                g.tensor_tensor(tok[:, :, :], tok[:, :, :], over(gamma[:, :], 1, [P, 2, D]), ALU.mult).then_inc(L0.tok_scaled, 1)
                wait(pool, L0.tok_scaled, i + 1)
                settle(pool, i)
                g.tensor_tensor(h[:, bass.ts(i, 2), :], tok[:, :, :], over(beta[:, :], 1, [P, 2, D]), ALU.add).then_inc(L0.h_ready, 1)

            def scatter(L, i):
                wait(pool, L.scatter_ready, i + 1)
                settle(pool, i)
                for t in range(2):
                    for k in range(L.K):
                        g.indirect_dma_start(L.rows, bass.IndirectOffsetOnAxis(ap=scatter_i[:, k, t:t + 1], axis=0),
                                             ffn_in[:, t, :], None, bounds_check=L.E * L.C - 1,
                                             oob_is_err=False).then_inc(L.scattered, 16)

            def add_input(i):
                wait(pool, L0.ffn_ready, i + 1)
                hp = h[:, bass.ts(i, 2), :]
                g.tensor_tensor(hp, hp, ffn_in[:, :, 0:D], ALU.add).then_inc(L0.input_added, 1)

            sum_x(0)
            ln_scale(L0, 2, 0)
            affine(0, True)
            ln_scale(L0, 0, 0)

            def phase_a(i):
                before_, next_ = there(i - 1, PAIRS), there(i + 1, PAIRS)
                if next_:
                    sum_x(i + 1)
                if there(i - 2, PAIRS):
                    scatter(L0, i - 2)
                if next_:
                    ln_scale(L0, 2, i + 1)
                if before_:
                    ln_scale(L0, 1, i - 1)
                if next_:
                    affine(i + 1, False)
                if before_:
                    add_input(i - 1)
                if next_:
                    ln_scale(L0, 0, i + 1)
                if isinstance(i, int) and i == 1:
                    pool.wait_ge(L0.fill, 16 * FILLS[0])

            skewed_loop(pool, PAIRS, 2, phase_a)

            def add_b(i, first, last):
                for u in range(2):
                    e = 2 * i + u
                    wait(pool, e_added, 16 * NCT * e)
                    wait(pool, e_yfree, NCT * (e + 1))
                    settle(pool, i)
                    for s, (r, m) in enumerate(CT):
                        g.indirect_dma_start(stream, bass.IndirectOffsetOnAxis(ap=slot_token[0:m, u, s:s + 1], axis=0),
                                             yrows[u][0:m, s, :], None, bounds_check=N + NCT * P - 1,
                                             compute_op=ALU.add).then_inc(e_added, 16)

            pool.wait_ge(h_stored, 16)
            pool.wait_ge(fill_stream, 16)
            loop(pool, NE0 // 2, add_b)

            pool.wait_ge(L1.fill, 16 * FILLS[1])
            ln_scale(L1, 0, 0)

            def phase_c(i):
                if there(i + 1, PAIRS):
                    ln_scale(L1, 0, i + 1)
                if there(i - 2, PAIRS):
                    scatter(L1, i - 2)
                if there(i - 1, PAIRS):
                    ln_scale(L1, 1, i - 1)

            skewed_loop(pool, PAIRS, 2, phase_c)

            def split_w2_pool(i, u):
                e = RING1 * i + u
                wait(pool, w2_rounded, 2 * e + 2)
                split(g, w2_high[:, u % 2, W2_DVE:J1, :], w2_low[:, u % 2, W2_DVE:J1, :], w2_sb[u][:, W2_DVE:J1, :]).then_inc(w2_split_pool, 1)

            def add_d(i, first, last):
                for u in range(RING1):
                    e = RING1 * i + u
                    split_w2_pool(i, u)
                    wait(pool, d_added, 16 * e)
                    wait(pool, dy_free, e + 1)
                    settle(pool, i)
                    g.indirect_dma_start(stream, bass.IndirectOffsetOnAxis(ap=slot_token[:, u, 0:1], axis=0),
                                         dy[:, u % 2, :], None, bounds_check=N + NCT * P - 1,
                                         compute_op=ALU.add).then_inc(d_added, 16)

            pool.wait_ge(h_final, 16)
            loop(pool, NE1 // RING1, add_d)

        @block.tensor
        def _(pe):
            pe.wait_ge(const_p, 20)
            pe.wait_ge(raw_in, 16 * 6)
            prep = [0]

            def prep_job(turns):
                n = prep[0]
                wait(pe, prep_free, n - 1)
                for out_ap, in_ap, k in turns:
                    last = pe.transpose(out_ap, in_ap, ident[0:k, 0:k])
                last.then_inc(prep_full, 1)
                prep[0] += 1

            def prep_out(col, n=P):
                return front_bank[prep[0] % 2][:, col:col + n]

            for k in range(2):
                prep_job([(prep_out((c * 2 + m) * P), conv_raw[:, m, c * 2 * P + k:(c + 1) * 2 * P:2], P)
                          for c in range(DC) for m in range(2)])
            for w in range(4):
                prep_job([(prep_out((c * 2 + m) * P), w_raw[:, w, m, c * P:(c + 1) * P], P)
                          for c in range(DC) for m in range(2)])
            prep_job([(prep_out(j * NE1, NE1), b1_raw[:, j:F1:J1], NE1) for j in range(J1)])
            pe.wait_ge(prep_free, prep[0])

            def front_job(L, i, k):
                b, n = front(L, i, k)
                wait(pe, L.front_free[b], n)
                return front_bank[b], L.front_full[b]

            def turn_x(i):
                wait(pe, L0.x_loaded, 16 * (i + 1))
                for t in range(2):
                    bk, full = front_job(L0, i, t)
                    for c in range(2 * DC):
                        last = pe.transpose(bk[:, c * P:(c + 1) * P], x_in[:, t, c * P:(c + 1) * P], ident[:, :])
                    last.then_inc(full, 1)

            def conv(i):
                for t in range(2):
                    wait(pe, L0.front_free[t], i * (L0.NF // 2) + 1)
                    bk, full = front_job(L0, i, 2 + t)
                    for c in range(2 * DC):
                        last = pe.matmul(bk[:, 0:D], xT[:, t, c, :], conv_wT[:, c, :], start=c == 0, stop=c == 2 * DC - 1)
                    last.then_inc(full, 1)

            def turn_normed(L, i):
                wait(pe, L.normed_ready, i + 1)
                bk, full = front_job(L, i, L.KF)
                for c in range(DC):
                    for t in range(2):
                        last = pe.transpose(bk[:, (2 * c + t) * P:(2 * c + t + 1) * P], normed[:, t, c * P:(c + 1) * P], ident[:, :])
                last.then_inc(full, 1)

            def project_qk(L, i):
                b, n = front(L, i, L.KF)
                wait(pe, L.front_free[b], n + 1)
                for w in range(2):
                    bk, full = front_job(L, i, L.KF + 1 + w)
                    for m in range(DC):
                        for c in range(DC):
                            last = pe.matmul(bk[:, m * D:(m + 1) * D], L.w[w](c, slice(m * P, (m + 1) * P)),
                                             normedT[:, c, :], start=c == 0, stop=c == DC - 1)
                    last.then_inc(full, 1)

            def project_v(L, i):
                bk, full = front_job(L, i, L.KF + 3)
                for t in range(2):
                    for c in range(DC):
                        last = pe.matmul(bk[:, t * D:(t + 1) * D], normedT[:, c, t * P:(t + 1) * P],
                                         L.w[2](c, slice(0, D)), start=c == 0, stop=c == DC - 1)
                last.then_inc(full, 1)

            def scores(L, i, t, b):
                if t == 0 and b == 0:
                    for k in (1, 2):
                        fb, n = front(L, i, L.KF + k)
                        wait(pe, L.front_free[fb], n + 1)
                wait(pe, L.max_done, 8 * i + 4 * t + b - 1)
                row = 32 * b
                for m in range(DC):
                    last = pe.matmul(score_bank[b % 2][:, 2 * m * P:2 * (m + 1) * P], qT[row:row + 32, m, t, :],
                                     kT[row:row + 32, m, t, :, :], start=True, stop=True)
                last.then_inc(L.score_full, 1)

            def turn_probs(L, i, t, b):
                n = 8 * i + 4 * t + b
                wait(pe, L.exp_done, n + 1)
                wait(pe, L.turned, n - 1)
                for j in range(HEADS_PER_BANK):
                    last = pe.transpose(turn_bank[b % 2][:, j * P:(j + 1) * P], probs[:, t, head(b, j), :], ident[:, :])
                last.then_inc(L.turn_full, 1)

            def values(L, i, t, b):
                wait(pe, L.turned, 8 * i + 4 * t + b + 1)
                if b == 0:
                    fb, fn = front(L, i, L.KF + 3)
                    wait(pe, L.front_free[fb], fn + 1)
                    wait(pe, L.mix_done, i)
                for j in range(HEADS_PER_BANK):
                    m, own = divmod(head(b, j), P // HD)
                    col = (2 * m + t) * P
                    last = pe.matmul(mix_bank[:, col:col + P], v_wide[:, DC * t + m, own * P:(own + 1) * P],
                                     probsT[:, b, j * P:(j + 1) * P], start=b == 0 and j == 0,
                                     stop=b == SBANKS - 1 and j % 2 == 1, skip_group_check=True)
                last.then_inc(L.pv_done, 1)

            def step(L, s, a):
                for b in range(SBANKS):
                    if s:
                        scores(L, *s, b)
                    if a:
                        turn_probs(L, *a, b)
                        if b >= 1:
                            values(L, *a, b - 1)
                if a:
                    values(L, *a, SBANKS - 1)

            def back_job(L, i, k):
                wait(pe, L.back_free, i * L.NB + k)

            def turn_inverse(L, i):
                wait(pe, L.inv_done, 2 * i + 2)
                back_job(L, i, 0)
                for t in range(2):
                    last = pe.transpose(back_bank[0:HEADS, t * P:(t + 1) * P], exp_inv[:, t, :], ident[:, :])
                last.then_inc(L.back_full, 1)

            def spread_inverse(L, i):
                back_job(L, i, 1)
                for m in range(DC):
                    last = pe.matmul(back_bank[:, m * D:(m + 1) * D], own_rows[:, m * P:(m + 1) * P], exp_invT[:, :],
                                     start=True, stop=True)
                last.then_inc(L.back_full, 1)

            def project_out(L, i):
                wait(pe, L.mix_done, i + 1)
                back_job(L, i, 2)
                for t in range(2):
                    for c in range(DC):
                        last = pe.matmul(back_bank[:, t * D:(t + 1) * D], mixedT[:, c, t * P:(t + 1) * P],
                                         L.w[3](c, slice(0, D)), start=c == 0, stop=c == DC - 1)
                last.then_inc(L.back_full, 1)

            def turn_ffn_in(L, i):
                wait(pe, L.ffn_ready, i + 1)
                back_job(L, i, 3)
                for c in range(DC):
                    for t in range(2):
                        last = pe.transpose(back_bank[:, (2 * c + t) * P:(2 * c + t + 1) * P], ffn_in[:, t, c * P:(c + 1) * P], ident[:, :])
                last.then_inc(L.back_full, 1)

            def route(L, i):
                back_job(L, i, 4)
                for t in range(2):
                    for c in range(DC):
                        last = pe.matmul(back_bank[:, t * L.E:(t + 1) * L.E], ffn_inT[:, c, t * P:(t + 1) * P],
                                         L.rw[:, c, :], start=c == 0, stop=c == DC - 1)
                last.then_inc(L.back_full, 1)

            def count(L, i):
                wait(pe, L.chosen_ready, i + 1)
                back_job(L, i, 5)
                for t in range(2):
                    col = back_bank[:, t * L.E:(t + 1) * L.E]
                    pe.matmul(col, before[:, :], chosen[:, t, 0:L.E], start=True, stop=False)
                    last = pe.matmul(col, ones_b[:, :], earlier[:, t, 0:L.E], start=False, stop=True)
                last.then_inc(L.back_full, 1)

            def pairs(L):
                def body(i):
                    now, before_, next_ = there(i, PAIRS), there(i - 1, PAIRS), there(i + 1, PAIRS)
                    step(L, (i, 0) if now else None, (i - 1, 1) if before_ else None)
                    if there(i - 2, PAIRS):
                        count(L, i - 2)
                    if before_:
                        turn_inverse(L, i - 1)
                    if next_ and L is L0:
                        turn_x(i + 1)
                    if next_ and L is L1:
                        turn_normed(L1, i + 1)
                    if before_:
                        spread_inverse(L, i - 1)
                    if next_ and L is L0:
                        conv(i + 1)
                    if next_ and L is L1:
                        project_qk(L1, i + 1)
                    if before_:
                        project_out(L, i - 1)
                    if now:
                        step(L, (i, 1), (i, 0))
                    if before_:
                        turn_ffn_in(L, i - 1)
                    if next_ and L is L0:
                        turn_normed(L0, i + 1)
                    if before_:
                        route(L, i - 1)
                    if next_ and L is L0:
                        project_qk(L0, i + 1)
                    if next_:
                        project_v(L, i + 1)

                if L is L0:
                    turn_x(0)
                    conv(0)
                turn_normed(L, 0)
                project_qk(L, 0)
                project_v(L, 0)
                skewed_loop(pe, PAIRS, 2, body)

            def banks_empty(L):
                pe.wait_ge(L.max_done, SBANKS * B)
                pe.wait_ge(L.turned, SBANKS * B)
                for b in range(2):
                    pe.wait_ge(L.front_free[b], PAIRS * L.NF // 2)
                pe.wait_ge(L.back_free, PAIRS * L.NB)
                pe.wait_ge(L.mix_done, PAIRS)

            pe.wait_ge(router_in, 16 * ROUTER_LOADS)
            pairs(L0)
            banks_empty(L0)

            def shared_mlp(q, first, last):
                for j, (f, m) in enumerate(FT):
                    gate_bank, up_bank = bank[GU[j]], bank[GU[j] + 1]
                    wait(pe, sh_hid, 3 * q + j - 2)
                    for w, dst in ((sw_gate, gate_bank), (sw_up, up_bank)):
                        for c in range(DC):
                            mm = pe.matmul(dst[0:m, :], w[:, c, f:f + m], all_inT[:, c, bass.ts(q, BANK)],
                                           start=c == 0, stop=c == DC - 1)
                    mm.then_inc(sh_gu, 1)
                wait(pe, sh_hid, 3 * q + 3)
                for half in range(2):
                    wait(pe, sh_add, 2 * q - 1 + half)
                    for t in range(2):
                        col = (2 * half + t) * P
                        for j, (f, m) in enumerate(FT):
                            mm = pe.matmul(bank[6 + half][:, t * D:(t + 1) * D], shT[0:m, j, col:col + P],
                                           sw_down[0:m, j, :], start=j == 0, stop=j == NFT - 1)
                    mm.then_inc(sh_y, 1)

            loop(pe, N // BANK, shared_mlp)
            pe.wait_ge(sh_hid, NFT * (N // BANK))
            pe.wait_ge(sh_add, 2 * (N // BANK))

            def turn_rows_b(i, u):
                e = 2 * i + u
                wait(pe, er_in[u], 32 * (i + 1))
                wait(pe, ex_free, e)
                for c in range(DC):
                    for s, (r, m) in enumerate(CT):
                        mm = pe.transpose(bank[c][:, r:r + m], erows[0:m, u, s, c:D:DC], ident[0:m, 0:m])
                mm.then_inc(ex_full, 1)

            def gate_up(i, u):
                e = 2 * i + u
                wait(pe, ex_free, e + 1)
                wait(pe, ew_in[u], 32 * (i + 1))
                for j, (f, m) in enumerate(FT):
                    s = (NFT * u + j) % 2
                    wait(pe, e_hid, NFT * e + j - 1)
                    for w, dst in ((gate_w[u], bank[2 + 2 * s]), (up_w[u], bank[3 + 2 * s])):
                        for c in range(DC):
                            mm = pe.matmul(dst[0:m, 0:C0], w[:, c, f:f + m], erowsT[u][:, c, :],
                                           start=c == 0, stop=c == DC - 1)
                    mm.then_inc(e_gu, 1)

            def down(i, u):
                e = 2 * i + u
                wait(pe, e_hid, NFT * (e + 1))
                wait(pe, ed_in[u], 32 * (i + 1))
                for s, (r, m) in enumerate(CT):
                    wait(pe, e_yfree, NCT * e + s - 1)
                    for j, (f, fm) in enumerate(FT):
                        mm = pe.matmul(bank[6 + (NCT * u + s) % 2][0:m, 0:D], hidT[u][0:fm, j, r:r + m],
                                       down_w[u][0:fm, j, :], start=j == 0, stop=j == NFT - 1)
                    mm.then_inc(e_y, 1)

            def experts_b(i, first, last):
                for u in range(2):
                    if not last:
                        turn_rows_b(i + 1, u)
                    if u == 0:
                        gate_up(i, 1)
                    elif not last:
                        gate_up(i + 1, 0)
                    down(i, u)

            turn_rows_b(0, 0)
            turn_rows_b(0, 1)
            gate_up(0, 0)
            loop(pe, NE0 // 2, experts_b)
            pe.wait_ge(e_hid, NFT * NE0)
            pe.wait_ge(e_yfree, NCT * NE0)

            pairs(L1)
            banks_empty(L1)

            def turn_rows_d(i, v_):
                i, u = later(i, v_)
                e = RING1 * i + u
                wait(pe, dr_in[u], 16 * (i + 1))
                wait(pe, dx_free, e - 1)
                for c in range(DC):
                    mm = pe.transpose(bank[u % 2][:, c * P:(c + 1) * P], drows[:, u, c:D:DC], ident[:, :])
                mm.then_inc(dx_full, 1)

            def first_product(i, v_):
                i, u = later(i, v_)
                e = RING1 * i + u
                wait(pe, dx_free, e + 1)
                wait(pe, dw1_in[u], 16 * (i + 1))
                for half in range(2):
                    wait(pe, dh_done, 2 * e - 3 + half)
                    for jj in range(J1 // 2):
                        j = half * (J1 // 2) + jj
                        for c in range(DC):
                            mm = pe.matmul(bank[2 + 2 * (u % 2) + half][:, jj * P:(jj + 1) * P], w1_sb[u][:, c, j:F1:J1],
                                           drowsT[:, u % 2, c, :], start=c == 0, stop=c == DC - 1)
                    mm.then_inc(dh_full, 1)

            def second_product(i, u):
                e = RING1 * i + u
                wait(pe, hid_split, 2 * e + 2)
                wait(pe, w2_split_dve, 2 * e + 2)
                wait(pe, w2_split_pool, e + 1)
                wait(pe, dy_free, e - 1)
                for j in range(J1):
                    high, low = hidden_high[:, u % 2, j, :], hidden_low[:, u % 2, j, :]
                    w_high, w_low = w2_high[:, u % 2, j, :], w2_low[:, u % 2, j, :]
                    for n, (hid, w) in enumerate(((high, w_high), (high, w_low), (low, w_high))):
                        pe.matmul(bank[6 + u % 2][:, 0:D], hid, w, start=j == 0 and n == 0, stop=False)
                wait(pe, chooser_ready, e + 1)
                for n, b2 in enumerate((b2_high, b2_low)):
                    mm = pe.matmul(bank[6 + u % 2][:, 0:D], chooser[:, u % 2, :], b2[:, :], start=False, stop=n == 1)
                mm.then_inc(dy_full, 1)

            def experts_d(i, first, last):
                for u in range(RING1):
                    if not (last and u + 2 >= RING1):
                        turn_rows_d(i, u + 2)
                    if not (last and u + 1 >= RING1):
                        first_product(i, u + 1)
                    second_product(i, u)

            turn_rows_d(0, 0)
            turn_rows_d(0, 1)
            first_product(0, 0)
            pe.wait_ge(b2_split, 1)
            loop(pe, NE1 // RING1, experts_d)

        @block.scalar
        def _(act):
            def from_front(L, i, k):
                b, n = front(L, i, k)
                wait(act, L.front_full[b], n + 1)
                return front_bank[b], L.front_free[b]

            def keep_xT(i):
                for t in range(2):
                    wait(act, L0.front_full[t], (i - 1) * (L0.NF // 2) + 2)
                for t in range(2):
                    bk, free = from_front(L0, i, t)
                    act.activation(xT[:, t, :, :], bk[:, :].rearrange("p (c n) -> p c n", n=P), ACT.Copy).then_inc(free, 1)

            def keep_normedT(L, i):
                b, n = front(L, i - 1, L.KF + 3)
                wait(act, L.front_full[b], n + 1)
                bk, free = from_front(L, i, L.KF)
                act.activation(normedT[:, :, :], bk[:, :].rearrange("p (c n) -> p c n", c=DC), ACT.Copy).then_inc(free, 1)

            def keep_qk(L, i):
                wait(act, L.score_full, 8 * i)
                bk, free = from_front(L, i, L.KF + 1)
                act.activation(qT[:, :, :, :], bk[:, :].rearrange("p (m t n) -> p m t n", m=DC, t=2), ACT.Copy).then_inc(free, 1)
                bk, free = from_front(L, i, L.KF + 2)
                for r in range(2):
                    last = act.activation(kT[:, :, :, r, :], bk[:, :].rearrange("p (m t n) -> p m t n", m=DC, t=2),
                                          ACT.Copy, scale=parity[:, r:r + 1])
                last.then_inc(free, 1)

            def keep_v(L, i):
                wait(act, L.pv_done, 8 * i)
                bk, free = from_front(L, i, L.KF + 3)
                act.activation(v_wide[:, :, :].rearrange("p g (j n) -> p g j n", n=P + HD)[:, :, :, 0:HD],
                               bk[:, :].rearrange("p (g j d) -> p g j d", g=2 * DC, d=HD), ACT.Copy).then_inc(free, 1)

            def exponentials(L, i, t, b):
                if b == 0:
                    wait(act, L.inv_done, 2 * i + t - 1)
                wait(act, L.max_done, 8 * i + 4 * t + b + 1)
                for j in range(HEADS_PER_BANK):
                    hd = head(b, j)
                    last = act.activation(probs[:, t, hd, :], probs[:, t, hd, :], ACT.Exp, scale=-1.0,
                                          bias=neg_max[:, t, hd:hd + 1], accum_out=exp_sum[:, t, hd:hd + 1])
                last.then_inc(L.exp_done, 1)

            def keep_turned(L, i, t, b):
                n = 8 * i + 4 * t + b
                wait(act, L.turn_full, n + 1)
                wait(act, L.pv_done, n - 3)
                act.activation(probsT[:, b, :], turn_bank[b % 2][:, :], ACT.Copy).then_inc(L.turned, 1)

            def step(L, s, a):
                for b in range(SBANKS):
                    if a:
                        keep_turned(L, *a, b)
                    if s:
                        exponentials(L, *s, b)

            def from_back(L, i, k):
                wait(act, L.back_full, i * L.NB + k + 1)

            def keep_inverse(L, i):
                from_back(L, i, 0)
                act.activation(exp_invT[:, :], back_bank[0:HEADS, 0:2 * P], ACT.Copy).then_inc(L.back_free, 1)

            def keep_spread(L, i):
                from_back(L, i, 1)
                wait(act, L.mix_done, i)
                act.activation(inv_rows[:, :, :], back_bank[:, :].rearrange("p (c n) -> p c n", c=DC), ACT.Copy).then_inc(L.back_free, 1)

            def keep_ffn_inT(L, i):
                from_back(L, i, 3)
                src = back_bank[:, :].rearrange("p (c n) -> p c n", c=DC)
                if L is L0:
                    act.activation(all_inT[:, :, bass.ts(i, 2 * P)], src, ACT.Copy)
                act.activation(ffn_inT[:, :, :], src, ACT.Copy).then_inc(L.back_free, 1)

            def router_exp(L, i):
                wait(act, L.to_exp, i + 1)
                n = L.E if L is L0 else L.K
                act.activation(gate_p[:, :, 0:n], shifted[:, :, 0:n], ACT.Exp).then_inc(L.from_exp, 1)

            def pairs(L):
                def body(i):
                    now, before_, next_ = there(i, PAIRS), there(i - 1, PAIRS), there(i + 1, PAIRS)
                    step(L, (i, 0) if now else None, (i - 1, 1) if before_ else None)
                    if now:
                        keep_v(L, i)
                    if before_:
                        keep_inverse(L, i - 1)
                    if next_ and L is L0:
                        keep_xT(i + 1)
                    if next_ and L is L1:
                        keep_normedT(L1, i + 1)
                    if before_:
                        keep_spread(L, i - 1)
                    if now:
                        step(L, (i, 1), (i, 0))
                    if before_:
                        keep_ffn_inT(L, i - 1)
                    if next_ and L is L0:
                        keep_normedT(L0, i + 1)
                    if before_ and L is L0:
                        router_exp(L, i - 1)
                    if next_:
                        keep_qk(L, i + 1)
                    if before_ and L is L1:
                        router_exp(L, i - 1)

                if L is L0:
                    keep_xT(0)
                keep_normedT(L, 0)
                keep_qk(L, 0)
                skewed_loop(act, PAIRS, 2, body)

            act.wait_ge(const_d, 3)
            pairs(L0)

            def shared_silu(q, first, last):
                for j, (f, m) in enumerate(FT):
                    wait(act, sh_gu, 3 * q + j + 1)
                    wait(act, sh_hid, 3 * q + j - 2)
                    act.activation(silu[j][0:m, :], bank[GU[j]][0:m, :], ACT.Silu).then_inc(sh_silu, 1)

            loop(act, N // BANK, shared_silu)

            def experts_b(i, first, last):
                for u in range(2):
                    e = 2 * i + u
                    for j, (f, m) in enumerate(FT):
                        s = (NFT * u + j) % 2
                        wait(act, e_gu, NFT * e + j + 1)
                        wait(act, e_hid, NFT * e + j - 1)
                        act.activation(silu[s][0:m, 0:C0], bank[2 + 2 * s][0:m, 0:C0], ACT.Silu).then_inc(e_silu, 1)

            loop(act, NE0 // 2, experts_b)

            pairs(L1)
            def experts_d(i, first, last):
                for u in range(RING1):
                    e = RING1 * i + u
                    wait(act, dy_full, e - 1)
                    wait(act, dw2_in[u], 16 * (i + 1))
                    for half in range(2):
                        wait(act, dh_full, 2 * e + half + 1)
                        for jj in range(J1 // 2):
                            j = half * (J1 // 2) + jj
                            last_ = act.activation(dhidT[:, u % 2, j, :], bank[2 + 2 * (u % 2) + half][:, jj * P:(jj + 1) * P],
                                                   ACT.Gelu, bias=b1T[:, j, bass.ds(e, 1)])
                        last_.then_inc(dh_done, 1)
                        rows = slice(half * (J1 // 2), (half + 1) * (J1 // 2))
                        act.activation(w2_high[:, u % 2, rows, :], w2_sb[u][:, rows, :], ACT.Copy).then_inc(w2_rounded, 1)

            loop(act, NE1 // RING1, experts_d)

        @block.vector
        def _(dve):
            dve.wait_ge(const_p, 20)
            dve.memset(ones_b[:, :], 1.0)
            dve.tensor_scalar(row_id[:, 1:2], row_id[:, 0:1], HD.bit_length() - 1, 1, ALU.logical_shift_right,
                              ALU.bitwise_and).then_inc(const_d, 1)
            dve.wait_ge(const_d, 1)
            dve.tensor_copy(row_f[:, :], row_id[:, 1:2]).then_inc(const_d, 1)
            dve.wait_ge(const_d, 2)
            dve.tensor_scalar(parity[:, 0:1], row_f[:, :], -SCALE, SCALE, ALU.mult, ALU.add)
            dve.tensor_scalar(parity[:, 1:2], row_f[:, :], SCALE, None, ALU.mult).then_inc(const_d, 1)
            places = [conv_wT[:, 2 * k:2 * k + 2, :] for k in range(2)] + [wT0[:, w, :, :] for w in range(4)] + [b1T[:, :, :]]
            for n, place in enumerate(places):
                dve.wait_ge(prep_full, n + 1)
                dve.tensor_copy(place, front_bank[n % 2][:, :].rearrange("p (a b) -> p a b", a=place.shape[1])).then_inc(prep_free, 1)

            def ln_stats(L, w, i, src):
                settle(dve, i)
                for t in range(2):
                    last = dve.bn_stats(stats[:, w, t, :], src(t))
                last.then_inc(L.stat_steps[w], 1)
                wait(dve, L.stat_steps[w], i + 1)
                settle(dve, i)
                for t in range(2):
                    last = dve.bn_aggr(moments[:, w, t, :], stats[:, w, t, :])
                last.then_inc(L.moments_ready[w], 1)

            def ln_apply(L, w, i, src, dst, done):
                wait(dve, L.rstd_ready[w], i + 1)
                wait(dve, L.moments_ready[w], i + 1)
                for t in range(2):
                    last = dve.tensor_scalar(dst(t), src(t), moments[:, w, t, 0:1], rstd[:, w, t:t + 1],
                                             ALU.subtract, ALU.mult)
                last.then_inc(done, 1)

            def h_tile(i):
                return lambda t: h[:, bass.ds(2 * i + t, 1), :].rearrange("p a d -> p (a d)")

            def mix_tokens(i, first):
                wait(dve, L0.x_summed, i + 1)
                if first:
                    dve.wait_ge(dense_in, 48)
                for t in range(2):
                    b, n = front(L0, i, 2 + t)
                    wait(dve, L0.front_full[b], n + 1)
                    dve.scalar_tensor_tensor(out=tok[:, t, :], in0=x_sum[:, t, :], scalar=0.5, in1=front_bank[b][:, 0:D],
                                             op0=ALU.mult, op1=ALU.add).then_inc(L0.front_free[b], 1)
                for t in range(2):
                    b, n = front(L0, i, 2 + t)
                    wait(dve, L0.front_free[b], n + 1)
                    dve.tensor_tensor(tok[:, t, :], tok[:, t, :], conv_b[:, :], ALU.add).then_inc(L0.tok_biased, 1)
                wait(dve, L0.tok_biased, 2 * i + 2)
                ln_stats(L0, 2, i, lambda t: tok[:, t, :])

            def front_a(L, i, first):
                if L is L0:
                    mix_tokens(i, first)
                else:
                    ln_stats(L1, 0, i, h_tile(i))

            def front_b(i):
                ln_apply(L0, 2, i, lambda t: tok[:, t, :], lambda t: tok[:, t, :], L0.tok_normed)

            def front_c(i):
                wait(dve, L0.h_ready, i + 1)
                ln_stats(L0, 0, i, h_tile(i))

            def front_d(L, i):
                b, n = front(L, i - 1, L.KF)
                wait(dve, L.front_full[b], n + 1)
                ln_apply(L, 0, i, h_tile(i), lambda t: normed[:, t, :], L.normed_ready)

            def greatest(L, i, t, b):
                if b == 0:
                    wait(dve, L.turn_full, 8 * i + 4 * t - 4)
                wait(dve, L.score_full, 8 * i + 4 * t + b + 1)
                settle(dve, i)
                for j in range(HEADS_PER_BANK):
                    hd = head(b, j)
                    last = dve.tensor_tensor_reduce(probs[:, t, hd, :], score_bank[b % 2][:, j * P:(j + 1) * P],
                                                    L.mask[:, :], -1.0, 3e38, ALU.add, ALU.min,
                                                    neg_max[:, t, hd:hd + 1])
                last.then_inc(L.max_done, 1)

            def invert(L, i, t):
                wait(dve, L.exp_done, 8 * i + 4 * t + 4)
                wait(dve, L.back_full, (i - 1) * L.NB + 1)
                dve.reciprocal(exp_inv[:, t, :], exp_sum[:, t, :]).then_inc(L.inv_done, 1)

            def normalise(L, i):
                wait(dve, L.pv_done, 8 * i + 8)
                wait(dve, L.back_free, i * L.NB + 2)
                dve.tensor_tensor(mixedT[:, :, :], mix_bank[:, :].rearrange("p (c n) -> p c n", c=DC),
                                  inv_rows[:, :, :], ALU.mult).then_inc(L.mix_done, 1)

            def residual(L, i):
                wait(dve, L.back_full, i * L.NB + 3)
                hp = h[:, bass.ts(i, 2), :]
                dve.tensor_tensor(hp, hp, back_bank[:, :].rearrange("p (t d) -> p t d", t=2), ALU.add).then_inc(L.back_free, 1)

            def residual_stats(L, i):
                wait(dve, L.back_free, i * L.NB + 3)
                ln_stats(L, 1, i, h_tile(i))

            def expert_input(L, i):
                wait(dve, L.scattered, 16 * 2 * L.K * i)
                if L is L0:
                    wait(dve, L.input_added, i)
                ln_apply(L, 1, i, h_tile(i), lambda t: ffn_in[:, t, 0:D], L.ffn_ready)

            def choose(L, i):
                E, K = L.E, L.K
                chain = Chain(dve, L.route_steps, i, ROUTE_STEPS[L.n])
                wait(dve, L.back_full, i * L.NB + 5)
                wait(dve, L.scatter_ready, i)
                lg = logits[:, :, 0:E]
                dve.tensor_tensor(lg, back_bank[:, 0:2 * E].rearrange("p (t e) -> p t e", t=2),
                                  over(L.rb[:, 0:E], 1, [P, 2, E]), ALU.add).then_inc(L.back_free, 1)
                wait(dve, L.back_free, i * L.NB + 5)
                if L is L0:
                    chain.link(dve.tensor_reduce(rsmall[:, 0, :], lg, AX.X, ALU.max))
                    dve.tensor_tensor(shifted[:, :, 0:E], lg, over(rsmall[:, 0, :], 2, [P, 2, E]), ALU.subtract).then_inc(L.to_exp, 1)
                    wait(dve, L.from_exp, i + 1)
                    chain.link(dve.tensor_reduce(rsmall[:, 1, :], gate_p[:, :, 0:E], AX.X, ALU.add))
                    chain.link(dve.reciprocal(rsmall[:, 2, :], rsmall[:, 1, :]))
                    chain.link(dve.tensor_tensor(lg, gate_p[:, :, 0:E], over(rsmall[:, 2, :], 2, [P, 2, E]), ALU.mult))
                settle(dve, i)
                for t in range(2):
                    last = dve.max(top_v[:, t, :], logits[:, t, 0:E])
                chain.link(last)
                settle(dve, i)
                for t in range(2):
                    last = dve.max_index(top_i[:, t, :], top_v[:, t, :], logits[:, t, 0:E])
                chain.link(last)
                chain.link(dve.tensor_copy(top_f[:, :, :], top_i[:, :, :]))
                for k in range(K):
                    last = dve.tensor_tensor(onehot[:, k, :, 0:E], over(iota_e[:, 0:E], 1, [P, 2, E]),
                                             top_f[:, :, k:k + 1].to_broadcast([P, 2, E]), ALU.is_equal)
                chain.link(last)
                ch = chosen[:, :, 0:E]
                if K == 2:
                    chain.link(dve.tensor_tensor(ch, onehot[:, 0, :, 0:E], onehot[:, 1, :, 0:E], ALU.add))
                else:
                    chain.link(dve.tensor_tensor(product[:, 0, :, 0:E], onehot[:, 0, :, 0:E], onehot[:, 1, :, 0:E], ALU.add))
                    chain.link(dve.tensor_tensor(ch, product[:, 0, :, 0:E], onehot[:, 2, :, 0:E], ALU.add))
                dve.tensor_copy(earlier[:, 0, 0:E], running[:, 0:E])
                chain.link(dve.tensor_tensor(earlier[:, 1, 0:E], running[:, 0:E], chosen[:, 0, 0:E], ALU.add))
                dve.tensor_tensor(running[:, 0:E], earlier[:, 1, 0:E], chosen[:, 1, 0:E], ALU.add).then_inc(L.chosen_ready, 1)
                wait(dve, L.chosen_ready, i + 1)
                vals = top_v[:, :, 0:K]
                if L is L0:
                    chain.link(dve.tensor_tensor(rsmall[:, 3, :], top_v[:, :, 0], top_v[:, :, 1], ALU.add))
                    chain.link(dve.tensor_scalar(rsmall[:, 4, :], rsmall[:, 3, :], GATE_SUM_EPS, None, ALU.add))
                else:
                    dve.tensor_tensor(shifted[:, :, 0:K], vals, top_v[:, :, 0:1].to_broadcast([P, 2, K]), ALU.subtract).then_inc(L.to_exp, 1)
                    wait(dve, L.from_exp, i + 1)
                    vals = gate_p[:, :, 0:K]
                    chain.link(dve.tensor_reduce(rsmall[:, 4, :], vals, AX.X, ALU.add))
                chain.link(dve.reciprocal(rsmall[:, 5, :], rsmall[:, 4, :]))
                chain.link(dve.tensor_tensor(weight[:, 0:K, :], vals.rearrange("p t k -> p k t"),
                                             over(rsmall[:, 5, :], 1, [P, K, 2]), ALU.mult))
                chain.end()

            def place(L, i):
                E, K, C = L.E, L.K, L.C
                chain = Chain(dve, L.slot_steps, i, SLOT_STEPS[L.n])
                wait(dve, L.back_full, i * L.NB + 6)
                dve.tensor_copy(count_sb[:, :, 0:E], back_bank[:, 0:2 * E].rearrange("p (t e) -> p t e", t=2)).then_inc(L.back_free, 1)
                wait(dve, L.back_free, i * L.NB + 6)
                for k in range(K):
                    last = dve.tensor_tensor(product[:, k, :, 0:E], onehot[:, k, :, 0:E], count_sb[:, :, 0:E], ALU.mult)
                chain.link(last)
                chain.link(dve.tensor_reduce(posf[:, 0:K, :], product[:, 0:K, :, 0:E], AX.X, ALU.add))
                dve.tensor_scalar(validf[:, 0:K, :], posf[:, 0:K, :], float(C), None, ALU.is_lt)
                chain.link(dve.tensor_scalar(tmpf[:, 0:K, :], posf[:, 0:K, :], float(C - 1), None, ALU.min))
                chain.link(dve.scalar_tensor_tensor(out=slotf[:, 0:K, :], in0=top_f[:, :, 0:K].rearrange("p t k -> p k t"),
                                                    scalar=float(C), in1=tmpf[:, 0:K, :], op0=ALU.mult, op1=ALU.add))
                chain.link(dve.tensor_scalar(tmpf[:, 0:K, :], validf[:, 0:K, :], -float(SKIP), float(SKIP), ALU.mult, ALU.add))
                dve.tensor_copy(ffn_in[:, :, CODE], code[:, bass.ts(i, 2)])
                dve.tensor_copy(ffn_in[:, :, EXPERT:EXPERT + K], top_f[:, :, 0:K])
                dve.tensor_copy(ffn_in[:, :, WEIGHT:WEIGHT + K].rearrange("p t k -> p k t"), weight[:, 0:K, :])
                dve.tensor_tensor(scatter_i[:, 0:K, :], slotf[:, 0:K, :], tmpf[:, 0:K, :], ALU.add).then_inc(L.scatter_ready, 1)
                chain.end()

            def pairs(L):
                def body(i):
                    now, before_, next_ = there(i, PAIRS), there(i - 1, PAIRS), there(i + 1, PAIRS)
                    if before_:
                        invert(L, i - 1, 1)
                    if now:
                        greatest(L, i, 0, 0)
                        greatest(L, i, 0, 1)
                    if next_ and L is L1:
                        front_a(L1, i + 1, False)
                    if now:
                        greatest(L, i, 0, 2)
                        greatest(L, i, 0, 3)
                    if next_ and L is L1:
                        front_d(L1, i + 1)
                    if there(i - 2, PAIRS):
                        place(L, i - 2)
                    if before_:
                        normalise(L, i - 1)
                    if next_ and L is L0:
                        front_a(L0, i + 1, False)
                    if before_:
                        residual(L, i - 1)
                    if now:
                        invert(L, i, 0)
                        greatest(L, i, 1, 0)
                    if before_:
                        residual_stats(L, i - 1)
                    if next_ and L is L0:
                        front_b(i + 1)
                    if now:
                        greatest(L, i, 1, 1)
                        greatest(L, i, 1, 2)
                    if before_:
                        expert_input(L, i - 1)
                    if next_ and L is L0:
                        front_c(i + 1)
                    if now:
                        greatest(L, i, 1, 3)
                    if next_ and L is L0:
                        front_d(L0, i + 1)
                    if before_:
                        choose(L, i - 1)

                dve.memset(running[:, :], 0.0).then_inc(L.running_zero, 1)
                dve.wait_ge(L.running_zero, 1)
                if L is L1:
                    dve.wait_ge(h_loaded, 16)
                    dve.wait_ge(h_loaded_rest, 16)
                front_a(L, 0, True)
                if L is L0:
                    front_b(0)
                    front_c(0)
                front_d(L, 0)
                skewed_loop(dve, PAIRS, 2, body)

            dve.wait_ge(router_in, 16 * ROUTER_LOADS)
            pairs(L0)

            dve.wait_ge(L0.input_added, PAIRS)

            def shared_mlp(q, first, last):
                for j, (f, m) in enumerate(FT):
                    wait(dve, sh_silu, 3 * q + j + 1)
                    wait(dve, sh_y, 2 * q)
                    dve.tensor_tensor(shT[0:m, j, :], silu[j][0:m, :], bank[GU[j] + 1][0:m, :], ALU.mult).then_inc(sh_hid, 1)
                for half in range(2):
                    wait(dve, sh_y, 2 * q + half + 1)
                    hp = h[:, bass.ds(4 * q + 2 * half, 2), :]
                    dve.tensor_tensor(hp, hp, bank[6 + half][:, :].rearrange("p (t d) -> p t d", t=2), ALU.add).then_inc(sh_add, 1)

            loop(dve, N // BANK, shared_mlp)

            def slots(rows, buf, e, steps, added, done):
                ns = rows.shape[1]
                chain = Chain(dve, steps, e, 2)
                wait(dve, added[0], added[1])
                match, empty = slot_match[:, buf, 0:ns, :], slot_empty[:, buf, 0:ns]
                dve.tensor_scalar(match, rows[:, :, EXPERT:EXPERT + K1], iota_e[:, bass.ds(e, 1)], None, ALU.is_equal)
                chain.link(dve.scalar_tensor_tensor(out=empty, in0=rows[:, :, CODE], scalar=0.0, in1=empty_row[:, 0:ns],
                                                    op0=ALU.is_equal, op1=ALU.mult))
                dve.scalar_tensor_tensor(out=slot_token[:, buf, 0:ns], in0=rows[:, :, CODE], scalar=-1.0, in1=empty,
                                         op0=ALU.add, op1=ALU.add)
                chain.link(dve.tensor_tensor(match, match, rows[:, :, WEIGHT:WEIGHT + K1], ALU.mult))
                dve.tensor_reduce(slot_gate[:, buf, 0:ns], match, AX.X, ALU.add).then_inc(done, 1)
                chain.end()

            def slots_b(i, u):
                e = 2 * i + u
                wait(dve, er_in[u], 32 * (i + 1))
                slots(erows[:, u, :, :], u, e, slot_steps, (e_added, 16 * NCT * (e - 1)), e_slots)

            def keep_rows_b(i, u):
                e = 2 * i + u
                wait(dve, ex_full, e + 1)
                wait(dve, e_gu, NFT * (e - 1))
                for c in range(DC):
                    last = dve.tensor_copy(erowsT[u][:, c, :], bank[c][:, 0:C0])
                last.then_inc(ex_free, 1)

            def hidden_b(i, u, before_last):
                e = 2 * i + u
                for j, (f, m) in enumerate(FT):
                    s = (NFT * u + j) % 2
                    if j == NFT - 1:
                        before_last()
                    wait(dve, e_silu, NFT * e + j + 1)
                    wait(dve, e_y, NCT * (e - 1))
                    dve.tensor_tensor(hidT[u][0:m, j, :], silu[s][0:m, 0:C0], bank[3 + 2 * s][0:m, 0:C0], ALU.mult).then_inc(e_hid, 1)

            def result_b(i, u):
                e = 2 * i + u
                wait(dve, e_added, 16 * NCT * (e - 1))
                wait(dve, e_slots, e + 1)
                for s, (r, m) in enumerate(CT):
                    wait(dve, e_y, NCT * e + s + 1)
                    dve.tensor_scalar(yrows[u][0:m, s, :], bank[6 + (NCT * u + s) % 2][0:m, 0:D],
                                      slot_gate[0:m, u, s:s + 1], None, ALU.mult).then_inc(e_yfree, 1)

            def experts_b(i, first, last):
                for u in range(2):
                    if not last:
                        keep_rows_b(i + 1, u)
                    if u == 0:
                        hidden_b(i, 1, lambda: slots_b(i, 1))
                    elif not last:
                        hidden_b(i + 1, 0, lambda: slots_b(i + 1, 0))
                    result_b(i, u)

            keep_rows_b(0, 0)
            keep_rows_b(0, 1)
            hidden_b(0, 0, lambda: slots_b(0, 0))
            loop(dve, NE0 // 2, experts_b)

            pairs(L1)
            def keep_rows_d(i, v_):
                i, u = later(i, v_)
                e = RING1 * i + u
                wait(dve, dx_full, e + 1)
                wait(dve, dh_full, 2 * e - 2)
                dve.tensor_copy(drowsT[:, u % 2, :, :], bank[u % 2][:, 0:D].rearrange("p (c n) -> p c n", c=DC)).then_inc(dx_free, 1)

            def slots_d(i, v_):
                i, u = later(i, v_)
                e = RING1 * i + u
                wait(dve, dr_in[u], 16 * (i + 1))
                slots(drows[:, u:u + 1, :], u, e, d_steps, (d_added, 16 * (e - RING1 + 1)), d_slots)

            def split_w2(i, v_, half):
                i, u = later(i, v_)
                e = RING1 * i + u
                wait(dve, w2_rounded, 2 * e + half + 1)
                rows = slice(half * (J1 // 2), min((half + 1) * (J1 // 2), W2_DVE))
                split(dve, w2_high[:, u % 2, rows, :], w2_low[:, u % 2, rows, :], w2_sb[u][:, rows, :]).then_inc(w2_split_dve, 1)

            def split_hidden(i, v_, half):
                i, u = later(i, v_)
                e = RING1 * i + u
                wait(dve, dh_done, 2 * e + half + 1)
                rows = slice(half * (J1 // 2), (half + 1) * (J1 // 2))
                dve.tensor_copy(hidden_high[:, u % 2, rows, :], dhidT[:, u % 2, rows, :]).then_inc(hid_rounded, 1)
                wait(dve, hid_rounded, 2 * e + half + 1)
                split(dve, hidden_high[:, u % 2, rows, :], hidden_low[:, u % 2, rows, :], dhidT[:, u % 2, rows, :]).then_inc(hid_split, 1)

            def choose_b2(i, v_):
                i, u = later(i, v_)
                e = RING1 * i + u
                wait(dve, dy_full, e - 1)
                dve.tensor_copy(chooser[:, u % 2, :], ident[0:NE1, bass.ds(e, 1)].to_broadcast([NE1, P])).then_inc(chooser_ready, 1)

            def result_d(i, u):
                e = RING1 * i + u
                wait(dve, d_slots, e + 1)
                wait(dve, dy_full, e + 1)
                wait(dve, d_added, 16 * (e - 1))
                dve.tensor_scalar(dy[:, u % 2, :], bank[6 + u % 2][:, 0:D], slot_gate[:, u, 0:1], None,
                                  ALU.mult).then_inc(dy_free, 1)

            def experts_d(i, first, last):
                for u in range(RING1):
                    split_hidden(i, u, 1)
                    split_w2(i, u, 1)
                    if not (last and u + 2 >= RING1):
                        keep_rows_d(i, u + 2)
                    if not (last and u + 1 >= RING1):
                        split_hidden(i, u + 1, 0)
                        split_w2(i, u + 1, 0)
                        choose_b2(i, u + 1)
                        slots_d(i, u + 1)
                    result_d(i, u)

            keep_rows_d(0, 0)
            keep_rows_d(0, 1)
            dve.wait_ge(b2_in, 16)
            dve.wait_ge(h_final, 16)
            dve.tensor_copy(b2_high[:, :], b2_raw).then_inc(b2_rounded, 1)
            dve.wait_ge(b2_rounded, 1)
            split(dve, b2_high[:, :], b2_low[:, :], b2_raw).then_inc(b2_split, 1)
            split_hidden(0, 0, 0)
            split_w2(0, 0, 0)
            choose_b2(0, 0)
            slots_d(0, 0)
            loop(dve, NE1 // RING1, experts_d)


NAMES = ["x", "L0_tok_conv_w", "L0_tok_conv_b", "L0_tok_ln_gamma", "L0_tok_ln_beta", "L0_attn_Wq", "L0_attn_Wk",
         "L0_attn_Wv", "L0_attn_Wo", "L0_ffn_router_w", "L0_ffn_router_b", "L0_ffn_w_gate", "L0_ffn_w_up",
         "L0_ffn_w_down", "L0_ffn_sw_gate", "L0_ffn_sw_up", "L0_ffn_sw_down", "L1_attn_w_qkv", "L1_attn_w_out",
         "L1_ffn_gate_w", "L1_ffn_gate_b", "L1_ffn_w1", "L1_ffn_b1", "L1_ffn_w2", "L1_ffn_b2"]


def kernel(**inputs):
    import numpy as np
    from concourse import bacc
    from concourse.bass_utils import run_bass_kernel_spmd

    nc = bacc.Bacc("TRN2", target_bir_lowering=False, num_devices=1)
    arrays = {name: np.ascontiguousarray(inputs[name]) for name in NAMES}
    a = {name: nc.dram_tensor(name, arrays[name].shape, F32, kind="ExternalInput").ap() for name in NAMES}
    b, tokens, d = arrays["x"].shape
    out = nc.dram_tensor("out", [b, tokens // 2, d], F32, kind="ExternalOutput").ap()
    build(nc, a, out)
    return run_bass_kernel_spmd(nc, [arrays], core_ids=[0]).results[0]["out"]
```

```python
from contextlib import ExitStack

import concourse.bass as bass
from concourse import mybir

F32 = mybir.dt.float32
F32R = mybir.dt.float32r
BF16 = mybir.dt.bfloat16
I32 = mybir.dt.int32
U32 = mybir.dt.uint32
ALU = mybir.AluOpType
ACT = mybir.ActivationFunctionType
AX = mybir.AxisListType

P = 128
D = 256
DC = D // P
HEADS = 16
HD = D // HEADS
WINDOW = 64
EPS = 1e-5
BANK = 512
SCALE = HD ** -0.5
HEADS_PER_BANK = BANK // P
SBANKS = HEADS // HEADS_PER_BANK
MASKED = -1e30
SKIP = 1 << 20
GATE_SUM_EPS = 1e-9


def wait(eng, sem, count):
    if not isinstance(count, int) or count > 0:
        eng.wait_ge(sem, count)


def settle(eng, i):
    if not isinstance(i, int):
        eng.nop(nofuse=True)


class Chain:

    def __init__(self, eng, sem, call, steps):
        self.eng, self.sem, self.base, self.steps, self.n = eng, sem, call * steps, steps, 0

    def link(self, instruction):
        instruction.then_inc(self.sem, 1)
        self.n += 1
        self.eng.wait_ge(self.sem, self.base + self.n)

    def end(self):
        assert self.n == self.steps, (self.n, self.steps)


def loop(eng, count, body):
    body(0, True, count == 1)
    if count > 2:
        with eng.Fori(1, count - 1) as i:
            body(i, False, False)
    if count > 1:
        body(count - 1, False, True)


def skewed_loop(eng, count, lead, body):
    for i in range(lead):
        body(i)
    with eng.Fori(lead, count - 1) as i:
        body(i)
    for i in range(count - 1, count + lead):
        body(i)


def there(j, count):
    return not isinstance(j, int) or 0 <= j < count


def split(eng, high, low, value):
    return eng.tensor_tensor(low, value, high.bitcast(F32), ALU.subtract)


def over(ap, axis, shape):
    return ap.unsqueeze(axis).to_broadcast(shape)


class Layer:

    def __init__(self, sem, n):
        self.n = n
        self.score_full = sem(f"score_full_{n}")
        self.max_done = sem(f"max_done_{n}")
        self.exp_done = sem(f"exp_done_{n}")
        self.turn_full = sem(f"turn_full_{n}")
        self.turned = sem(f"turned_{n}")
        self.pv_done = sem(f"pv_done_{n}")
        self.inv_done = sem(f"inv_done_{n}")
        self.mix_done = sem(f"mix_done_{n}")
        self.back_full = sem(f"back_full_{n}")
        self.back_free = sem(f"back_free_{n}")
        self.scattered = sem(f"scattered_{n}")
        self.normed_ready = sem(f"normed_ready_{n}")
        self.ffn_ready = sem(f"ffn_ready_{n}")
        self.to_exp = sem(f"to_exp_{n}")
        self.from_exp = sem(f"from_exp_{n}")
        self.route_steps = sem(f"route_steps_{n}")
        self.weight_steps = sem(f"weight_steps_{n}")
        self.chosen_ready = sem(f"chosen_ready_{n}")
        self.slot_steps = sem(f"slot_steps_{n}")
        self.scatter_ready = sem(f"scatter_ready_{n}")
        self.running_zero = sem(f"running_zero_{n}")
        if n == 0:
            self.x_loaded = sem("x_loaded")
            self.x_summed = sem("x_summed")
            self.tok_biased = sem("tok_biased")
            self.tok_normed = sem("tok_normed")
            self.tok_scaled = sem("tok_scaled")
            self.h_ready = sem("h_ready")
            self.input_added = sem("input_added")
        norms = range(3 if n == 0 else 2)
        self.stat_steps = [sem(f"stat_steps_{n}{w}") for w in norms]
        self.moments_ready = [sem(f"moments_ready_{n}{w}") for w in norms]
        self.eps_added = [sem(f"eps_added_{n}{w}") for w in norms]
        self.rstd_ready = [sem(f"rstd_ready_{n}{w}") for w in norms]
        self.front_full = [sem(f"front_full_{n}{b}") for b in range(2)]
        self.front_free = [sem(f"front_free_{n}{b}") for b in range(2)]


def build(nc, a, out):
    B, TOK, _ = a["x"].shape
    S = TOK // 2
    PAIRS = B // 2
    NE0, _, F0 = a["L0_ffn_w_gate"].shape
    NE1, _, F1 = a["L1_ffn_w1"].shape
    K0, K1 = 2, 3
    N = B * S
    C0 = -(-5 * N * K0 // (4 * NE0))
    C1 = 128
    FT = [(j * P, min(P, F0 - j * P)) for j in range(-(-F0 // P))]
    CT = [(j * P, min(P, C0 - j * P)) for j in range(-(-C0 // P))]
    NFT, NCT = len(FT), len(CT)
    GROUPS = N // BANK
    GROUPS_BEFORE = GROUPS // 2
    J1 = F1 // P
    RING1 = 4
    assert S == P and C1 == P and B % 2 == 0 and NFT == 3 and NCT == 3

    ctx = ExitStack()
    with ctx:
        def sb(name, shape, dt=F32):
            return ctx.enter_context(nc.sbuf_tensor(name, shape, dt))

        def sem(name):
            return ctx.enter_context(nc.semaphore(name))

        CODE, EXPERT, WEIGHT, ROW = D, D + 1, D + 1 + K1, D + 8
        rows0 = nc.dram_tensor("rows0", [NE0 * C0, ROW], F32, kind="Internal").ap()
        rows1 = nc.dram_tensor("rows1", [NE1 * C1, ROW], F32, kind="Internal").ap()
        stream = nc.dram_tensor("stream", [N + NCT * P, D], F32, kind="Internal").ap()

        bank = [ctx.enter_context(nc.psum_tensor(f"bank{n}", [P, BANK], F32)) for n in range(8)]
        score_bank, turn_bank, mix_bank = bank[0:2], bank[2:4], bank[4]
        front_bank, back_bank = bank[5:7], bank[7]
        prep_bank = bank[0:4]

        ident = sb("ident", [P, P])
        ones_f = sb("ones_f", [P, P])
        zeros = sb("zeros", [P, BANK])
        mask0 = sb("mask0", [P, P])
        mask1 = sb("mask1", [P, P])
        before = sb("before", [P, P], BF16)
        ones_b = sb("ones_b", [P, P], BF16)
        parity = sb("parity", [P, 2])
        row_id = sb("row_id", [P, 2], I32)
        row_f = sb("row_f", [P, 1])
        half_neg = sb("half_neg", [P, 2])
        iota_e = sb("iota_e", [P, NE1])
        router0 = sb("router0", [P, DC, NE0])
        router1 = sb("router1", [P, DC, NE1])
        rb0 = sb("rb0", [P, NE0])
        rb1 = sb("rb1", [P, NE1])
        b1T = sb("b1T", [P, J1, NE1])
        normed = sb("normed", [P, 2, D])
        normedT = sb("normedT", [P, DC, 2 * P])
        qT = sb("qT", [P, DC, 2, P])
        kT = sb("kT", [P, DC, 2, 2, P])
        HALF = (P // HD) * (P + HD)
        v_wide = sb("v_wide", [P, 2 * DC, HALF])
        probsT = sb("probsT", [P, SBANKS, BANK])
        neg_max = sb("neg_max", [P, 2, HEADS])
        exp_sum = sb("exp_sum", [P, 2, HEADS])
        exp_inv = sb("exp_inv", [P, 2, HEADS])
        own_rows = sb("own_rows", [HEADS, D])
        exp_invT = sb("exp_invT", [HEADS, 2 * P])
        inv_rows = sb("inv_rows", [P, DC, 2 * P])
        mixedT = sb("mixedT", [P, DC, 2 * P])
        ffn_in = sb("ffn_in", [P, 2, ROW])
        ffn_inT = sb("ffn_inT", [P, DC, 2 * P])
        slot_match = sb("slot_match", [P, RING1, NCT, K1])
        slot_gate = sb("slot_gate", [P, RING1, NCT])
        slot_empty = sb("slot_empty", [P, RING1, NCT])
        slot_token = sb("slot_token", [P, RING1, NCT], I32)
        empty_row = sb("empty_row", [P, NCT])
        stats = sb("stats", [P, 3, 2, 6])
        moments = sb("moments", [P, 3, 2, 2])
        rstd = sb("rstd", [P, 3, 2])
        var_eps = sb("var_eps", [P, 3, 2])
        logits = sb("logits", [P, 2, NE1])
        shifted = sb("shifted", [P, 2, NE1])
        gate_p = sb("gate_p", [P, 2, NE1])
        top_v = sb("top_v", [P, 2, 8])
        top_i = sb("top_i", [P, 2, 8], U32)
        top_f = sb("top_f", [P, 2, 8])
        rsmall = sb("rsmall", [P, 8, 2])
        onehot = sb("onehot", [P, K1, 2, NE1])
        chosen = sb("chosen", [P, 2, NE1], BF16)
        earlier = sb("earlier", [P, 2, NE1], BF16)
        running = sb("running", [P, NE1], BF16)
        count_sb = sb("count_sb", [P, 2, NE1])
        product = sb("product", [P, K1, 2, NE1])
        posf = sb("posf", [P, K1, 2])
        slotf = sb("slotf", [P, K1, 2])
        tmpf = sb("tmpf", [P, K1, 2])
        validf = sb("validf", [P, K1, 2])
        weight = sb("weight", [P, K1, 2])
        scatter_i = sb("scatter_i", [P, K1, 2], I32)
        code = sb("code", [P, B])
        SLOT1 = 2 * F1 * DC
        arena = sb("arena", [P, RING1 * SLOT1])
        at = [0]

        def part(n):
            at[0] += n
            assert at[0] <= RING1 * SLOT1
            return arena[:, at[0] - n:at[0]]

        all_inT = part(DC * N).rearrange("p (c n) -> p c n", c=DC)
        gate_w = [part(DC * F0).rearrange("p (c f) -> p c f", c=DC) for _ in range(2)]
        up_w = [part(DC * F0).rearrange("p (c f) -> p c f", c=DC) for _ in range(2)]
        down_w = [part(NFT * D).rearrange("p (j d) -> p j d", j=NFT) for _ in range(2)]
        hidden = part(2 * NFT * C0)
        hidT = [hidden[:, u * NFT * C0:(u + 1) * NFT * C0].rearrange("p (j n) -> p j n", j=NFT) for u in range(2)]
        silu = [part(BANK) for _ in range(3)]
        shT = hidden[:, 0:NFT * BANK].rearrange("p (j n) -> p j n", j=NFT)
        yrows = [part(NCT * D).rearrange("p (s d) -> p s d", s=NCT) for _ in range(2)]
        w1_sb = [arena[:, s * SLOT1:s * SLOT1 + DC * F1].rearrange("p (c f) -> p c f", c=DC) for s in range(RING1)]
        w2_sb = [arena[:, s * SLOT1 + DC * F1:(s + 1) * SLOT1].rearrange("p (j d) -> p j d", j=J1) for s in range(RING1)]
        flat = probsT[:, :, :].rearrange("p b n -> p (b n)")
        drows = sb("drows", [P, RING1, ROW])
        drowsT = flat[:, 0:2 * D].rearrange("p (u c n) -> p u c n", u=2, c=DC)
        dy = flat[:, 2 * D:4 * D].rearrange("p (u d) -> p u d", u=2)
        b2_raw = flat[0:NE1, 4 * D:5 * D]
        ctx_abc = ExitStack()

        def sb_abc(name, shape):
            return ctx_abc.enter_context(nc.sbuf_tensor(name, shape, F32))

        probs = sb_abc("probs", [P, 2, HEADS, P])
        w_qkv = sb_abc("w_qkv", [P, DC, 3 * D])
        w_out = sb_abc("w_out", [P, DC, D])
        sw_gate = sb_abc("sw_gate", [P, DC, F0])
        sw_up = sb_abc("sw_up", [P, DC, F0])
        sw_down = sb_abc("sw_down", [P, NFT, D])
        early = sb_abc("early", [P, 12 * D])
        h = sb_abc("h", [P, B, D])
        with ExitStack() as ctx_a:
            conv_wT = ctx_a.enter_context(nc.sbuf_tensor("conv_wT", [P, 2 * DC, D], F32))
            wT0 = ctx_a.enter_context(nc.sbuf_tensor("wT0", [P, 4, DC, D], F32))
            conv_b = ctx_a.enter_context(nc.sbuf_tensor("conv_b", [P, D], F32))
            gamma = ctx_a.enter_context(nc.sbuf_tensor("gamma", [P, D], F32))
            beta = ctx_a.enter_context(nc.sbuf_tensor("beta", [P, D], F32))
        with ExitStack() as ctx_b:
            gate_up_high = ctx_b.enter_context(nc.sbuf_tensor("gate_up_high", [P, 2, DC, F0], F32R))
            gate_up_low = ctx_b.enter_context(nc.sbuf_tensor("gate_up_low", [P, 2, DC, F0], F32R))
            rows_high = ctx_b.enter_context(nc.sbuf_tensor("rows_high", [P, DC, C0], F32R))
            rows_low = ctx_b.enter_context(nc.sbuf_tensor("rows_low", [P, DC, C0], F32R))
        x_in = early[:, 0:4 * D].rearrange("p (t d) -> p t d", t=2)
        x_sum = early[:, 4 * D:6 * D].rearrange("p (t d) -> p t d", t=2)
        tok = early[:, 6 * D:8 * D].rearrange("p (t d) -> p t d", t=2)
        xT = early[:, 8 * D:12 * D].rearrange("p (t c n) -> p t c n", t=2, c=2 * DC)
        erows = early[:, 0:2 * NCT * ROW].rearrange("p (u s d) -> p u s d", u=2, s=NCT)
        stage = probs[:, :, :, :].rearrange("p a b c -> p (a b c)")
        conv_raw = stage[:, 0:2 * 2 * D].rearrange("p (m f) -> p m f", m=2)
        w_raw = stage[:, 4 * D:12 * D].rearrange("p (w m d) -> p w m d", w=4, m=2)
        b1_raw = stage[0:NE1, 12 * D:12 * D + F1]
        ctx_abc.close()
        hidden_high = sb("hidden_high", [P, 2, J1, P], F32R)
        hidden_low = sb("hidden_low", [P, 2, J1, P], F32R)
        w2_high = sb("w2_high", [P, 2, J1, D], F32R)
        w2_low = sb("w2_low", [P, 2, J1, D], F32R)
        dhidT = sb("dhidT", [P, 2, J1, P])
        b2_high = sb("b2_high", [NE1, D], F32R)
        b2_low = sb("b2_low", [NE1, D], F32R)
        chooser = sb("chooser", [NE1, 2, P], F32R)

        conv_in = sem("conv_in")
        raw_in, dense_in, router_in, fill0, fill1, fill_stream = (
            sem("raw_in"), sem("dense_in"), sem("router_in"), sem("fill0"), sem("fill1"), sem("fill_stream"))
        const_p, const_d, prep_full, prep_free = sem("const_p"), sem("const_d"), sem("prep_full"), sem("prep_free")

        layers = []
        for n in range(2):
            L = Layer(sem, n)
            L.NF = 8 if n == 0 else 4
            L.KF = L.NF - 4
            L.NB = 6
            L.E, L.K, L.C = (NE0, K0, C0) if n == 0 else (NE1, K1, C1)
            L.mask = mask0 if n == 0 else mask1
            L.rows = rows0 if n == 0 else rows1
            L.rw, L.rb = (router0, rb0) if n == 0 else (router1, rb1)
            if n == 0:
                L.w = [lambda c, o, w=w: wT0[:, w, c, o] for w in range(4)]
            else:
                L.w = [lambda c, o, w=w: w_qkv[:, c, w * D + o.start:w * D + o.stop] for w in range(3)]
                L.w.append(lambda c, o: w_out[:, c, o])
            layers.append(L)
        L0, L1 = layers

        sh_gu, sh_silu, sh_hid, sh_y, sh_add = (sem(s) for s in ("sh_gu", "sh_silu", "sh_hid", "sh_y", "sh_add"))
        ew_in = [sem(f"ew_in{s}") for s in range(2)]
        ed_in = [sem(f"ed_in{s}") for s in range(2)]
        er_in = [sem(f"er_in{s}") for s in range(2)]
        slot_steps = sem("slot_steps")
        e_slots, e_added, h_stored, h_loaded, h_loaded_rest = (
            sem(s) for s in ("e_slots", "e_added", "h_stored", "h_loaded", "h_loaded_rest"))
        rows_rounded, gate_up_rounded, gate_split, up_split = (
            sem(s) for s in ("rows_rounded", "gate_up_rounded", "gate_split", "up_split"))
        ex_full, ex_free, e_gu, e_silu, e_hid, e_y, e_yfree = (
            sem(s) for s in ("ex_full", "ex_free", "e_gu", "e_silu", "e_hid", "e_y", "e_yfree"))
        dw1_in = [sem(f"dw1_in{s}") for s in range(RING1)]
        dw2_in = [sem(f"dw2_in{s}") for s in range(RING1)]
        dr_in = [sem(f"dr_in{s}") for s in range(RING1)]
        d_slots, d_steps, d_added, h_final = (sem(s) for s in ("d_slots", "d_steps", "d_added", "h_final"))
        dx_full, dx_free, dh_full, dh_done, dy_full, dy_free = (
            sem(s) for s in ("dx_full", "dx_free", "dh_full", "dh_done", "dy_full", "dy_free"))
        out_done, b2_in, b2_rounded, b2_split, chooser_ready = (
            sem(s) for s in ("out_done", "b2_in", "b2_rounded", "b2_split", "chooser_ready"))
        w2_rounded, hid_rounded, hid_split, w2_split_dve, w2_split_pool = (
            sem(s) for s in ("w2_rounded", "hid_rounded", "hid_split", "w2_split_dve", "w2_split_pool"))
        FILL = 4 * BANK
        FILLS = [-(-r.shape[0] * r.shape[1] // (P * FILL)) for r in (rows0, rows1)]

        def front(L, i, k):
            return k % 2, i * (L.NF // 2) + k // 2

        L0.fill, L1.fill = fill0, fill1
        GU = (2, 4, 0)
        ROUTER_LOADS = 8 + NFT
        ROUTE_STEPS, WEIGHT_STEPS, SLOT_STEPS = (10, 7), (4, 3), (5, 5)

        def head(b, j):
            return 8 * (j // 2) + 2 * b + j % 2

        W2_DVE = J1 - 2

        def later(i, u):
            return (i + 1, u - RING1) if u >= RING1 else (i, u)

        block = ctx.enter_context(nc.Block())

        @block.sync
        def _(sp):
            x_rows = a["x"].rearrange("b (t k) d -> b t (k d)", k=2)

            def load_x(i, first):
                if not first:
                    for k in range(2):
                        b, n = front(L0, i - 1, k)
                        wait(sp, L0.front_full[b], n + 1)
                    wait(sp, L0.x_summed, i)
                sp.dma_start(x_in[:, :, :], x_rows[bass.ts(i, 2)].rearrange("b t f -> t b f")).then_inc(L0.x_loaded, 16)

            sp.dma_start(conv_raw, a["L0_tok_conv_w"].rearrange("(m o) i k -> o m (i k)", m=2)).then_inc(conv_in, 16)
            load_x(0, True)
            for w, name in enumerate(("Wq", "Wk", "Wv", "Wo")):
                sp.dma_start(w_raw[:, w], a[f"L0_attn_{name}"].rearrange("(m o) d -> o m d", m=2)).then_inc(raw_in, 16)
            sp.dma_start(b1_raw, a["L1_ffn_b1"]).then_inc(raw_in, 16)

            def shared_row(dst, src):
                sp.dma_start(dst, src.rearrange("(a n) -> a n", a=1).to_broadcast([P, src.shape[0]])).then_inc(dense_in, 16)

            shared_row(conv_b[:, :], a["L0_tok_conv_b"])
            shared_row(gamma[:, :], a["L0_tok_ln_gamma"])
            shared_row(beta[:, :], a["L0_tok_ln_beta"])
            def whole(dst, src):
                sp.dma_start(dst, src).then_inc(router_in, 16)

            whole(router0[:, :, :], a["L0_ffn_router_w"].rearrange("(c p) e -> p c e", p=P))
            whole(rb0[:, :], a["L0_ffn_router_b"].rearrange("(a n) -> a n", a=1).to_broadcast([P, NE0]))
            whole(router1[:, :, :], a["L1_ffn_gate_w"].rearrange("(c p) e -> p c e", p=P))
            whole(rb1[:, :], a["L1_ffn_gate_b"].rearrange("(a n) -> a n", a=1).to_broadcast([P, NE1]))
            whole(w_qkv[:, :, :], a["L1_attn_w_qkv"].rearrange("(c p) e -> p c e", p=P))
            whole(w_out[:, :, :], a["L1_attn_w_out"].rearrange("(c p) e -> p c e", p=P))
            whole(sw_gate[:, :, :], a["L0_ffn_sw_gate"].rearrange("(c p) e -> p c e", p=P))
            whole(sw_up[:, :, :], a["L0_ffn_sw_up"].rearrange("(c p) e -> p c e", p=P))
            for j, (f, m) in enumerate(FT):
                whole(sw_down[0:m, j, :], a["L0_ffn_sw_down"][f:f + m, :])

            def load_gate_up(e, u, first):
                if not first:
                    wait(sp, gate_split, e - 1)
                    wait(sp, up_split, e - 1)
                s = ew_in[u % 2]
                sp.dma_start(gate_w[u % 2], a["L0_ffn_w_gate"][bass.ds(e, 1)].rearrange("a (p c) f -> p (a c) f", c=DC)).then_inc(s, 16)
                sp.dma_start(up_w[u % 2], a["L0_ffn_w_up"][bass.ds(e, 1)].rearrange("a (p c) f -> p (a c) f", c=DC)).then_inc(s, 16)

            def load_down(e, u, first):
                if not first:
                    wait(sp, e_y, (e - 1) * NCT)
                s = ed_in[u % 2]
                full = sum(m == P for _, m in FT)
                sp.dma_start(down_w[u % 2][:, 0:full, :],
                             a["L0_ffn_w_down"][bass.ds(e, 1), 0:full * P].rearrange("a (j p) d -> p (a j) d", p=P)).then_inc(s, 16)
                sp.dma_start(down_w[u % 2][0:F0 - full * P, full:full + 1, :],
                             a["L0_ffn_w_down"][bass.ds(e, 1), full * P:F0].rearrange("a p d -> p a d")).then_inc(s, 16)

            full = sum(m == P for _, m in CT)

            def load_rows(e, u, first):
                if not first:
                    wait(sp, ex_full, e - 1)
                    wait(sp, e_slots, e - 1)
                s = er_in[u % 2]
                sp.dma_start(erows[:, u % 2, 0:full, :], rows0[bass.ds(e * C0, full * P)].rearrange("(s p) d -> p s d", p=P)).then_inc(s, 16)
                sp.dma_start(erows[0:C0 - full * P, u % 2, full, :], rows0[bass.ds(e * C0 + full * P, C0 - full * P)]).then_inc(s, 16)

            for u in range(2):
                load_gate_up(u, u, True)
                load_down(u, u, True)
            def fill_zeros():
                for rows, fill in ((rows0, fill0), (rows1, fill1)):
                    flat = rows.rearrange("r d -> (r d)")
                    for at in range(0, flat.shape[0], P * FILL):
                        n = min(P * FILL, flat.shape[0] - at) // P
                        w = min(n, BANK)
                        sp.dma_start(flat[at:at + n * P].rearrange("(p r n) -> p r n", p=P, n=w),
                                      over(zeros[:, 0:w], 1, [P, n // w, w])).then_inc(fill, 16)
                sp.dma_start(stream[N:].rearrange("(s p) d -> p s d", p=P), over(zeros[:, 0:D], 1, [P, NCT, D])).then_inc(fill_stream, 16)

            load_x(1, False)
            sp.wait_ge(const_p, 3)
            fill_zeros()
            with sp.Fori(2, PAIRS) as i:
                load_x(i, False)

            sp.wait_ge(L0.scattered, 16 * 2 * K0 * PAIRS)
            load_rows(0, 0, True)
            load_rows(1, 1, True)

            def experts_b(i):
                for u in range(2):
                    e = 2 * i + u
                    if not (isinstance(i, int) and e + 3 >= NE0):
                        load_rows(e + 3, u + 3, False)
                        load_gate_up(e + 3, u + 3, False)
                    load_down(e + 2, u, False)

            stream_rows = stream[0:N].rearrange("(b p) d -> p b d", p=P)
            sp.wait_ge(sh_add, 2 * GROUPS_BEFORE)
            sp.dma_start(stream_rows, h[:, :, :]).then_inc(h_stored, 16)
            load_rows(2, 2, False)
            load_gate_up(2, 2, False)
            experts_b(0)
            with sp.Fori(1, NE0 // 2 - 2) as i:
                experts_b(i)
            experts_b(NE0 // 2 - 2)
            sp.wait_ge(e_added, 16 * NCT * NE0)
            sp.dma_start(h[:, 0:2, :], stream_rows[:, 0:2, :]).then_inc(h_loaded, 16)
            sp.dma_start(h[:, 2:B, :], stream_rows[:, 2:B, :]).then_inc(h_loaded_rest, 16)

            sp.wait_ge(sh_y, 2 * GROUPS)
            def load_w1(e, u, first):
                if not first:
                    wait(sp, dh_full, 2 * (e - RING1) + 2)
                sp.dma_start(w1_sb[u], a["L1_ffn_w1"][bass.ds(e, 1)].rearrange("a (p c) f -> p (a c) f", c=DC)).then_inc(dw1_in[u], 16)

            def load_w2(e, u, first):
                if not first:
                    wait(sp, w2_split_dve, 2 * (e - RING1) + 2)
                    wait(sp, w2_split_pool, e - RING1 + 1)
                sp.dma_start(w2_sb[u], a["L1_ffn_w2"][bass.ds(e, 1)].rearrange("a (p j) d -> p (a j) d", j=J1)).then_inc(dw2_in[u], 16)

            def load_dr(e, u, first):
                if not first:
                    wait(sp, dx_full, e - RING1 + 1)
                    wait(sp, d_slots, e - RING1 + 1)
                sp.dma_start(drows[:, u, :], rows1[bass.ds(e * C1, C1)]).then_inc(dr_in[u], 16)

            for u in range(RING1):
                load_w1(u, u, True)
                load_w2(u, u, True)
            sp.wait_ge(L1.back_free, (PAIRS - 1) * L1.NB + 3)
            sp.dma_start(stream_rows, h[:, :, :]).then_inc(h_final, 16)
            sp.wait_ge(L1.scattered, 16 * 2 * K1 * PAIRS)
            for u in range(RING1):
                load_dr(u, u, True)
            sp.dma_start(b2_raw, a["L1_ffn_b2"]).then_inc(b2_in, 16)

            def experts_d(i, first, last):
                for u in range(RING1):
                    e = RING1 * i + u
                    load_w1(e + RING1, u, False)
                    load_dr(e + RING1, u, False)
                    load_w2(e + RING1, u, False)

            loop(sp, NE1 // RING1 - 1, experts_d)

            sp.wait_ge(d_added, 16 * NE1)
            sp.dma_start(out.rearrange("b p d -> (b p) d"), stream[0:N]).then_inc(out_done, 16)
            sp.wait_ge(out_done, 16)

        @block.gpsimd
        def _(pool):
            g = nc.gpsimd
            g.memset(ident[:, :], 0.0).then_inc(const_p, 1)
            pool.wait_ge(const_p, 1)
            g.affine_select(out=ident[:, :], in_=ident[:, :], compare_op=ALU.not_equal, fill=1.0, base=0,
                            pattern=[[-1, P]], channel_multiplier=1).then_inc(const_p, 1)
            g.memset(zeros[:, :], 0.0).then_inc(const_p, 1)
            g.memset(ones_f[:, :], 1.0).then_inc(const_p, 1)
            g.memset(half_neg[:, :], -0.5).then_inc(const_p, 1)
            g.memset(mask0[:, :], 0.0).then_inc(const_p, 1)
            g.memset(mask1[:, :], 0.0).then_inc(const_p, 1)
            g.iota(code[:, :], [[P, B]], base=1, channel_multiplier=1, allow_small_or_imprecise_dtypes=True).then_inc(const_p, 1)
            g.iota(empty_row[:, :], [[P, NCT]], base=N + 1, channel_multiplier=1, allow_small_or_imprecise_dtypes=True).then_inc(const_p, 1)
            g.memset(ffn_in[:, :, D:ROW], 0.0).then_inc(const_p, 1)
            g.memset(own_rows[:, :], 1.0).then_inc(const_p, 1)
            g.iota(row_id[:, 0:1], [[0, 1]], base=0, channel_multiplier=1).then_inc(const_p, 1)
            g.iota(iota_e[:, :], [[1, NE1]], base=0, channel_multiplier=0, allow_small_or_imprecise_dtypes=True).then_inc(const_p, 1)
            pool.wait_ge(const_p, 13)
            g.affine_select(out=mask0[:, :], in_=mask0[:, :], compare_op=ALU.is_ge, fill=MASKED, base=0,
                            pattern=[[-1, P]], channel_multiplier=1).then_inc(const_p, 1)
            g.affine_select(out=mask1[:, :], in_=mask1[:, :], compare_op=ALU.is_ge, fill=MASKED, base=0,
                            pattern=[[-1, P]], channel_multiplier=1).then_inc(const_p, 1)
            g.affine_select(out=before[:, :], in_=ones_f[:, :], compare_op=ALU.is_gt, fill=0.0, base=0,
                            pattern=[[1, P]], channel_multiplier=-1).then_inc(const_p, 1)
            g.affine_select(out=own_rows[:, :], in_=own_rows[:, :], compare_op=ALU.is_ge, fill=0.0, base=0,
                            pattern=[[1, D]], channel_multiplier=-HD).then_inc(const_p, 1)
            pool.wait_ge(const_p, 17)
            g.affine_select(out=own_rows[:, :], in_=own_rows[:, :], compare_op=ALU.is_ge, fill=0.0, base=HD - 1,
                            pattern=[[-1, D]], channel_multiplier=HD).then_inc(const_p, 1)
            g.affine_select(out=mask0[:, :], in_=mask0[:, :], compare_op=ALU.is_gt, fill=MASKED, base=WINDOW,
                            pattern=[[1, P]], channel_multiplier=-1).then_inc(const_p, 1)
            pool.wait_ge(const_p, 19)

            def ln_scale(L, w, i):
                wait(pool, L.moments_ready[w], i + 1)
                settle(pool, i)
                g.tensor_scalar(var_eps[:, w, :], moments[:, w, :, 1], EPS, None, ALU.add).then_inc(L.eps_added[w], 1)
                pool.wait_ge(L.eps_added[w], i + 1)
                g.tensor_tensor(rstd[:, w, :], var_eps[:, w, :], half_neg[:, :], ALU.pow).then_inc(L.rstd_ready[w], 1)

            def sum_x(i):
                wait(pool, L0.x_loaded, 16 * (i + 1))
                wait(pool, L0.tok_biased, 2 * i)
                g.tensor_tensor(x_sum[:, :, :], x_in[:, :, 0:D], x_in[:, :, D:2 * D], ALU.add).then_inc(L0.x_summed, 1)

            def affine(i, first):
                wait(pool, L0.tok_normed, i + 1)
                if first:
                    pool.wait_ge(dense_in, 48)
                g.tensor_tensor(tok[:, :, :], tok[:, :, :], over(gamma[:, :], 1, [P, 2, D]), ALU.mult).then_inc(L0.tok_scaled, 1)
                wait(pool, L0.tok_scaled, i + 1)
                settle(pool, i)
                g.tensor_tensor(h[:, bass.ts(i, 2), :], tok[:, :, :], over(beta[:, :], 1, [P, 2, D]), ALU.add).then_inc(L0.h_ready, 1)

            def scatter(L, i):
                wait(pool, L.scatter_ready, i + 1)
                settle(pool, i)
                for t in range(2):
                    for k in range(L.K):
                        g.indirect_dma_start(L.rows, bass.IndirectOffsetOnAxis(ap=scatter_i[:, k, t:t + 1], axis=0),
                                             ffn_in[:, t, :], None, bounds_check=L.E * L.C - 1,
                                             oob_is_err=False).then_inc(L.scattered, 16)

            def add_input(i):
                wait(pool, L0.ffn_ready, i + 1)
                hp = h[:, bass.ts(i, 2), :]
                g.tensor_tensor(hp, hp, ffn_in[:, :, 0:D], ALU.add).then_inc(L0.input_added, 1)

            sum_x(0)
            ln_scale(L0, 2, 0)
            affine(0, True)
            ln_scale(L0, 0, 0)

            def phase_a(i):
                before_, next_ = there(i - 1, PAIRS), there(i + 1, PAIRS)
                if next_:
                    sum_x(i + 1)
                if there(i - 2, PAIRS):
                    scatter(L0, i - 2)
                if next_:
                    ln_scale(L0, 2, i + 1)
                if before_:
                    ln_scale(L0, 1, i - 1)
                if next_:
                    affine(i + 1, False)
                if before_:
                    add_input(i - 1)
                if next_:
                    ln_scale(L0, 0, i + 1)
                if isinstance(i, int) and i == 1:
                    pool.wait_ge(L0.fill, 16 * FILLS[0])

            skewed_loop(pool, PAIRS, 2, phase_a)

            def split_up_b(i, u):
                e = 2 * i + u
                wait(pool, gate_up_rounded, 2 * e + 2)
                split(g, gate_up_high[:, 1, :, :], gate_up_low[:, 1, :, :], up_w[u]).then_inc(up_split, 1)

            split_up_b(0, 0)
            split_up_b(0, 1)

            def add_b(i, first, last):
                for u in range(2):
                    e = 2 * i + u
                    if not last:
                        split_up_b(i + 1, u)
                    wait(pool, e_added, 16 * NCT * e)
                    wait(pool, e_yfree, NCT * (e + 1))
                    settle(pool, i)
                    for s, (r, m) in enumerate(CT):
                        g.indirect_dma_start(stream, bass.IndirectOffsetOnAxis(ap=slot_token[0:m, u, s:s + 1], axis=0),
                                             yrows[u][0:m, s, :], None, bounds_check=N + NCT * P - 1,
                                             compute_op=ALU.add).then_inc(e_added, 16)

            pool.wait_ge(h_stored, 16)
            pool.wait_ge(fill_stream, 16)
            loop(pool, NE0 // 2, add_b)

            pool.wait_ge(L1.fill, 16 * FILLS[1])
            ln_scale(L1, 0, 0)

            def phase_c(i):
                if there(i + 1, PAIRS):
                    ln_scale(L1, 0, i + 1)
                if there(i - 2, PAIRS):
                    scatter(L1, i - 2)
                if there(i - 1, PAIRS):
                    ln_scale(L1, 1, i - 1)

            skewed_loop(pool, PAIRS, 2, phase_c)

            def split_w2_pool(i, u):
                e = RING1 * i + u
                wait(pool, w2_rounded, 2 * e + 2)
                split(g, w2_high[:, u % 2, W2_DVE:J1, :], w2_low[:, u % 2, W2_DVE:J1, :], w2_sb[u][:, W2_DVE:J1, :]).then_inc(w2_split_pool, 1)

            def add_d(i, first, last):
                for u in range(RING1):
                    e = RING1 * i + u
                    split_w2_pool(i, u)
                    wait(pool, d_added, 16 * e)
                    wait(pool, dy_free, e + 1)
                    settle(pool, i)
                    g.indirect_dma_start(stream, bass.IndirectOffsetOnAxis(ap=slot_token[:, u, 0:1], axis=0),
                                         dy[:, u % 2, :], None, bounds_check=N + NCT * P - 1,
                                         compute_op=ALU.add).then_inc(d_added, 16)

            pool.wait_ge(h_final, 16)
            loop(pool, NE1 // RING1, add_d)

        @block.tensor
        def _(pe):
            pe.wait_ge(const_p, 2)
            pe.wait_ge(conv_in, 16)
            prep = [0]

            def prep_job(turns):
                n = prep[0]
                wait(pe, prep_free, n - len(prep_bank) + 1)
                for col, in_ap, k in turns:
                    last = pe.transpose(prep_bank[n % len(prep_bank)][:, col:col + k], in_ap, ident[0:k, 0:k])
                last.then_inc(prep_full, 1)
                prep[0] += 1

            def turn_conv_weights():
                for k in range(2):
                    prep_job([((c * 2 + m) * P, conv_raw[:, m, c * 2 * P + k:(c + 1) * 2 * P:2], P)
                              for c in range(DC) for m in range(2)])

            def turn_weights():
                pe.wait_ge(raw_in, 16 * 5)
                for w in range(4):
                    prep_job([((c * 2 + m) * P, w_raw[:, w, m, c * P:(c + 1) * P], P)
                              for c in range(DC) for m in range(2)])
                prep_job([(j * NE1, b1_raw[:, j:F1:J1], NE1) for j in range(J1)])

            def front_job(L, i, k):
                b, n = front(L, i, k)
                wait(pe, L.front_free[b], n)
                return front_bank[b], L.front_full[b]

            def turn_x(i):
                wait(pe, L0.x_loaded, 16 * (i + 1))
                for t in range(2):
                    bk, full = front_job(L0, i, t)
                    for c in range(2 * DC):
                        last = pe.transpose(bk[:, c * P:(c + 1) * P], x_in[:, t, c * P:(c + 1) * P], ident[:, :])
                    last.then_inc(full, 1)

            def conv(i):
                for t in range(2):
                    wait(pe, L0.front_free[t], i * (L0.NF // 2) + 1)
                    bk, full = front_job(L0, i, 2 + t)
                    for c in range(2 * DC):
                        last = pe.matmul(bk[:, 0:D], xT[:, t, c, :], conv_wT[:, c, :], start=c == 0, stop=c == 2 * DC - 1)
                    last.then_inc(full, 1)

            def turn_normed(L, i):
                wait(pe, L.normed_ready, i + 1)
                bk, full = front_job(L, i, L.KF)
                for c in range(DC):
                    for t in range(2):
                        last = pe.transpose(bk[:, (2 * c + t) * P:(2 * c + t + 1) * P], normed[:, t, c * P:(c + 1) * P], ident[:, :])
                last.then_inc(full, 1)

            def project_qk(L, i, w):
                b, n = front(L, i, L.KF)
                wait(pe, L.front_free[b], n + 1)
                bk, full = front_job(L, i, L.KF + 1 + w)
                for m in range(DC):
                    for c in range(DC):
                        last = pe.matmul(bk[:, m * D:(m + 1) * D], L.w[w](c, slice(m * P, (m + 1) * P)),
                                         normedT[:, c, :], start=c == 0, stop=c == DC - 1)
                last.then_inc(full, 1)

            def project_v(L, i):
                bk, full = front_job(L, i, L.KF + 3)
                for t in range(2):
                    for c in range(DC):
                        last = pe.matmul(bk[:, t * D:(t + 1) * D], normedT[:, c, t * P:(t + 1) * P],
                                         L.w[2](c, slice(0, D)), start=c == 0, stop=c == DC - 1)
                last.then_inc(full, 1)

            def scores(L, i, t, b):
                if t == 0 and b == 0:
                    for k in (1, 2):
                        fb, n = front(L, i, L.KF + k)
                        wait(pe, L.front_free[fb], n + 1)
                wait(pe, L.max_done, 8 * i + 4 * t + b - 1)
                row = 32 * b
                for m in range(DC):
                    last = pe.matmul(score_bank[b % 2][:, 2 * m * P:2 * (m + 1) * P], qT[row:row + 32, m, t, :],
                                     kT[row:row + 32, m, t, :, :], start=True, stop=True)
                last.then_inc(L.score_full, 1)

            def turn_probs(L, i, t, b):
                n = 8 * i + 4 * t + b
                wait(pe, L.exp_done, n + 1)
                wait(pe, L.turned, n - 1)
                for j in range(HEADS_PER_BANK):
                    last = pe.transpose(turn_bank[b % 2][:, j * P:(j + 1) * P], probs[:, t, head(b, j), :], ident[:, :])
                last.then_inc(L.turn_full, 1)

            def values(L, i, t, b):
                wait(pe, L.turned, 8 * i + 4 * t + b + 1)
                if b == 0:
                    fb, fn = front(L, i, L.KF + 3)
                    wait(pe, L.front_free[fb], fn + 1)
                    wait(pe, L.mix_done, i)
                for j in range(HEADS_PER_BANK):
                    m, own = divmod(head(b, j), P // HD)
                    col = (2 * m + t) * P
                    last = pe.matmul(mix_bank[:, col:col + P], v_wide[:, DC * t + m, own * P:(own + 1) * P],
                                     probsT[:, b, j * P:(j + 1) * P], start=b == 0 and j == 0,
                                     stop=b == SBANKS - 1 and j % 2 == 1, skip_group_check=True)
                last.then_inc(L.pv_done, 1)

            def step(L, s, a, beside):
                for b in range(SBANKS):
                    if s:
                        scores(L, *s, b)
                    if a:
                        turn_probs(L, *a, b)
                        if b >= 1:
                            values(L, *a, b - 1)
                    beside(b)
                if a:
                    values(L, *a, SBANKS - 1)

            def back_job(L, i, k):
                wait(pe, L.back_free, i * L.NB + k)

            def turn_inverse(L, i):
                wait(pe, L.inv_done, 2 * i + 2)
                back_job(L, i, 0)
                for t in range(2):
                    last = pe.transpose(back_bank[0:HEADS, t * P:(t + 1) * P], exp_inv[:, t, :], ident[:, :])
                last.then_inc(L.back_full, 1)

            def spread_inverse(L, i):
                back_job(L, i, 1)
                for m in range(DC):
                    last = pe.matmul(back_bank[:, m * D:(m + 1) * D], own_rows[:, m * P:(m + 1) * P], exp_invT[:, :],
                                     start=True, stop=True)
                last.then_inc(L.back_full, 1)

            def project_out(L, i):
                wait(pe, L.mix_done, i + 1)
                back_job(L, i, 2)
                for t in range(2):
                    for c in range(DC):
                        last = pe.matmul(back_bank[:, t * D:(t + 1) * D], mixedT[:, c, t * P:(t + 1) * P],
                                         L.w[3](c, slice(0, D)), start=c == 0, stop=c == DC - 1)
                last.then_inc(L.back_full, 1)

            def turn_ffn_in(L, i):
                wait(pe, L.ffn_ready, i + 1)
                back_job(L, i, 3)
                for c in range(DC):
                    for t in range(2):
                        last = pe.transpose(back_bank[:, (2 * c + t) * P:(2 * c + t + 1) * P], ffn_in[:, t, c * P:(c + 1) * P], ident[:, :])
                last.then_inc(L.back_full, 1)

            def route(L, i):
                back_job(L, i, 4)
                for t in range(2):
                    for c in range(DC):
                        last = pe.matmul(back_bank[:, t * L.E:(t + 1) * L.E], ffn_inT[:, c, t * P:(t + 1) * P],
                                         L.rw[:, c, :], start=c == 0, stop=c == DC - 1)
                last.then_inc(L.back_full, 1)

            def count(L, i):
                wait(pe, L.chosen_ready, i + 1)
                back_job(L, i, 5)
                for t in range(2):
                    col = back_bank[:, t * L.E:(t + 1) * L.E]
                    pe.matmul(col, before[:, :], chosen[:, t, 0:L.E], start=True, stop=False)
                    last = pe.matmul(col, ones_b[:, :], earlier[:, t, 0:L.E], start=False, stop=True)
                last.then_inc(L.back_full, 1)

            def pairs(L):
                def body(i):
                    now, before_, next_ = there(i, PAIRS), there(i - 1, PAIRS), there(i + 1, PAIRS)
                    if isinstance(i, int) and i == 0 and L is L0:
                        pe.wait_ge(router_in, 16 * ROUTER_LOADS)

                    def beside_first(b):
                        if b == (SBANKS - 1 if now else 1) and there(i - 2, PAIRS):
                            count(L, i - 2)

                    def beside_second(b):
                        if b == SBANKS - 1 and before_:
                            turn_ffn_in(L, i - 1)

                    step(L, (i, 0) if now else None, (i - 1, 1) if before_ else None, beside_first)
                    if before_:
                        turn_inverse(L, i - 1)
                    if next_ and L is L0:
                        turn_x(i + 1)
                    if next_ and L is L1:
                        turn_normed(L1, i + 1)
                    if before_:
                        spread_inverse(L, i - 1)
                    if next_ and L is L0:
                        conv(i + 1)
                    if next_ and L is L1:
                        project_qk(L1, i + 1, 0)
                        project_qk(L1, i + 1, 1)
                    if before_:
                        project_out(L, i - 1)
                    if now:
                        step(L, (i, 1), (i, 0), beside_second)
                    else:
                        beside_second(SBANKS - 1)
                    if next_ and L is L0:
                        turn_normed(L0, i + 1)
                    if before_:
                        route(L, i - 1)
                    if next_ and L is L0:
                        project_qk(L0, i + 1, 0)
                        project_qk(L0, i + 1, 1)
                    if next_:
                        project_v(L, i + 1)

                if L is L0:
                    turn_conv_weights()
                    turn_x(0)
                    pe.wait_ge(prep_free, 2)
                    conv(0)
                    turn_weights()
                    pe.wait_ge(const_p, 19)
                turn_normed(L, 0)
                pe.wait_ge(prep_free, prep[0])
                project_qk(L, 0, 0)
                project_qk(L, 0, 1)
                project_v(L, 0)
                skewed_loop(pe, PAIRS, 2, body)

            def banks_empty(L):
                pe.wait_ge(L.max_done, SBANKS * B)
                pe.wait_ge(L.turned, SBANKS * B)
                for b in range(2):
                    pe.wait_ge(L.front_free[b], PAIRS * L.NF // 2)
                pe.wait_ge(L.back_free, PAIRS * L.NB)
                pe.wait_ge(L.mix_done, PAIRS)

            pairs(L0)
            banks_empty(L0)

            def shared_mlp(q):
                for j, (f, m) in enumerate(FT):
                    gate_bank, up_bank = bank[GU[j]], bank[GU[j] + 1]
                    wait(pe, sh_hid, 3 * q + j - 2)
                    for w, dst in ((sw_gate, gate_bank), (sw_up, up_bank)):
                        for c in range(DC):
                            mm = pe.matmul(dst[0:m, :], w[:, c, f:f + m], all_inT[:, c, bass.ts(q, BANK)],
                                           start=c == 0, stop=c == DC - 1)
                    mm.then_inc(sh_gu, 1)
                wait(pe, sh_hid, 3 * q + 3)
                for half in range(2):
                    wait(pe, sh_add, 2 * q - 1 + half)
                    for t in range(2):
                        col = (2 * half + t) * P
                        for j, (f, m) in enumerate(FT):
                            mm = pe.matmul(bank[6 + half][:, t * D:(t + 1) * D], shT[0:m, j, col:col + P],
                                           sw_down[0:m, j, :], start=j == 0, stop=j == NFT - 1)
                    mm.then_inc(sh_y, 1)

            def shared_groups(first, end):
                for q in range(first, end):
                    shared_mlp(q)
                pe.wait_ge(sh_hid, NFT * end)
                pe.wait_ge(sh_add, 2 * end)

            shared_groups(0, GROUPS_BEFORE)

            def turn_rows_b(i, u):
                e = 2 * i + u
                wait(pe, er_in[u], 32 * (i + 1))
                wait(pe, ex_free, e)
                for c in range(DC):
                    for s, (r, m) in enumerate(CT):
                        mm = pe.transpose(bank[c][:, r:r + m], erows[0:m, u, s, c:D:DC], ident[0:m, 0:m])
                mm.then_inc(ex_full, 1)

            def gate_up(i, u):
                e = 2 * i + u
                wait(pe, ex_free, e + 1)
                wait(pe, gate_split, e + 1)
                wait(pe, up_split, e + 1)
                for j, (f, m) in enumerate(FT):
                    s = (NFT * u + j) % 2
                    wait(pe, e_hid, NFT * e + j - 1)
                    for w, dst in enumerate((bank[2 + 2 * s], bank[3 + 2 * s])):
                        for c in range(DC):
                            w_high, w_low = gate_up_high[:, w, c, f:f + m], gate_up_low[:, w, c, f:f + m]
                            for n, (wp, xp) in enumerate(((w_high, rows_high), (w_high, rows_low), (w_low, rows_high))):
                                mm = pe.matmul(dst[0:m, 0:C0], wp, xp[:, c, :], start=c == 0 and n == 0,
                                               stop=c == DC - 1 and n == 2)
                    mm.then_inc(e_gu, 1)

            def down(i, u):
                e = 2 * i + u
                wait(pe, e_hid, NFT * (e + 1))
                wait(pe, ed_in[u], 32 * (i + 1))
                for s, (r, m) in enumerate(CT):
                    wait(pe, e_yfree, NCT * e + s - 1)
                    for j, (f, fm) in enumerate(FT):
                        mm = pe.matmul(bank[6 + (NCT * u + s) % 2][0:m, 0:D], hidT[u][0:fm, j, r:r + m],
                                       down_w[u][0:fm, j, :], start=j == 0, stop=j == NFT - 1)
                    mm.then_inc(e_y, 1)

            def experts_b(i, first, last):
                for u in range(2):
                    if not last:
                        turn_rows_b(i + 1, u)
                    if u == 0:
                        gate_up(i, 1)
                    elif not last:
                        gate_up(i + 1, 0)
                    down(i, u)

            turn_rows_b(0, 0)
            turn_rows_b(0, 1)
            gate_up(0, 0)
            loop(pe, NE0 // 2, experts_b)
            pe.wait_ge(e_hid, NFT * NE0)
            pe.wait_ge(e_yfree, NCT * NE0)
            shared_groups(GROUPS_BEFORE, GROUPS)

            pairs(L1)
            banks_empty(L1)

            def turn_rows_d(i, v_):
                i, u = later(i, v_)
                e = RING1 * i + u
                wait(pe, dr_in[u], 16 * (i + 1))
                wait(pe, dx_free, e - 1)
                for c in range(DC):
                    mm = pe.transpose(bank[u % 2][:, c * P:(c + 1) * P], drows[:, u, c:D:DC], ident[:, :])
                mm.then_inc(dx_full, 1)

            def first_product(i, v_):
                i, u = later(i, v_)
                e = RING1 * i + u
                wait(pe, dx_free, e + 1)
                wait(pe, dw1_in[u], 16 * (i + 1))
                for half in range(2):
                    wait(pe, dh_done, 2 * e - 3 + half)
                    for jj in range(J1 // 2):
                        j = half * (J1 // 2) + jj
                        for c in range(DC):
                            mm = pe.matmul(bank[2 + 2 * (u % 2) + half][:, jj * P:(jj + 1) * P], w1_sb[u][:, c, j:F1:J1],
                                           drowsT[:, u % 2, c, :], start=c == 0, stop=c == DC - 1)
                    mm.then_inc(dh_full, 1)

            def second_product(i, u):
                e = RING1 * i + u
                wait(pe, hid_split, 2 * e + 2)
                wait(pe, w2_split_dve, 2 * e + 2)
                wait(pe, w2_split_pool, e + 1)
                wait(pe, dy_free, e - 1)
                for j in range(J1):
                    high, low = hidden_high[:, u % 2, j, :], hidden_low[:, u % 2, j, :]
                    w_high, w_low = w2_high[:, u % 2, j, :], w2_low[:, u % 2, j, :]
                    for n, (hid, w) in enumerate(((high, w_high), (high, w_low), (low, w_high))):
                        pe.matmul(bank[6 + u % 2][:, 0:D], hid, w, start=j == 0 and n == 0, stop=False)
                wait(pe, chooser_ready, e + 1)
                for n, b2 in enumerate((b2_high, b2_low)):
                    mm = pe.matmul(bank[6 + u % 2][:, 0:D], chooser[:, u % 2, :], b2[:, :], start=False, stop=n == 1)
                mm.then_inc(dy_full, 1)

            def experts_d(i, first, last):
                for u in range(RING1):
                    if not (last and u + 2 >= RING1):
                        turn_rows_d(i, u + 2)
                    if not (last and u + 1 >= RING1):
                        first_product(i, u + 1)
                    second_product(i, u)

            turn_rows_d(0, 0)
            turn_rows_d(0, 1)
            first_product(0, 0)
            pe.wait_ge(b2_split, 1)
            loop(pe, NE1 // RING1, experts_d)

        @block.scalar
        def _(act):
            def from_front(L, i, k):
                b, n = front(L, i, k)
                wait(act, L.front_full[b], n + 1)
                return front_bank[b], L.front_free[b]

            def keep_xT(i):
                for t in range(2):
                    wait(act, L0.front_full[t], (i - 1) * (L0.NF // 2) + 2)
                for t in range(2):
                    bk, free = from_front(L0, i, t)
                    act.activation(xT[:, t, :, :], bk[:, :].rearrange("p (c n) -> p c n", n=P), ACT.Copy).then_inc(free, 1)

            def keep_normedT(L, i):
                b, n = front(L, i - 1, L.KF + 3)
                wait(act, L.front_full[b], n + 1)
                bk, free = from_front(L, i, L.KF)
                act.activation(normedT[:, :, :], bk[:, :].rearrange("p (c n) -> p c n", c=DC), ACT.Copy).then_inc(free, 1)

            def keep_q(L, i):
                wait(act, L.score_full, 8 * i)
                bk, free = from_front(L, i, L.KF + 1)
                act.activation(qT[:, :, :, :], bk[:, :].rearrange("p (m t n) -> p m t n", m=DC, t=2), ACT.Copy).then_inc(free, 1)

            def keep_k(L, i):
                wait(act, L.score_full, 8 * i)
                bk, free = from_front(L, i, L.KF + 2)
                for r in range(2):
                    last = act.activation(kT[:, :, :, r, :], bk[:, :].rearrange("p (m t n) -> p m t n", m=DC, t=2),
                                          ACT.Copy, scale=parity[:, r:r + 1])
                last.then_inc(free, 1)

            def keep_v(L, i):
                wait(act, L.pv_done, 8 * i)
                bk, free = from_front(L, i, L.KF + 3)
                act.activation(v_wide[:, :, :].rearrange("p g (j n) -> p g j n", n=P + HD)[:, :, :, 0:HD],
                               bk[:, :].rearrange("p (g j d) -> p g j d", g=2 * DC, d=HD), ACT.Copy).then_inc(free, 1)

            def exponentials(L, i, t, b):
                if b == 0:
                    wait(act, L.inv_done, 2 * i + t - 1)
                wait(act, L.max_done, 8 * i + 4 * t + b + 1)
                for j in range(HEADS_PER_BANK):
                    hd = head(b, j)
                    last = act.activation(probs[:, t, hd, :], probs[:, t, hd, :], ACT.Exp, scale=-1.0,
                                          bias=neg_max[:, t, hd:hd + 1], accum_out=exp_sum[:, t, hd:hd + 1])
                last.then_inc(L.exp_done, 1)

            def keep_turned(L, i, t, b):
                n = 8 * i + 4 * t + b
                wait(act, L.turn_full, n + 1)
                wait(act, L.pv_done, n - 3)
                act.activation(probsT[:, b, :], turn_bank[b % 2][:, :], ACT.Copy).then_inc(L.turned, 1)

            def step(L, s, a, beside):
                for b in range(SBANKS):
                    if a:
                        keep_turned(L, *a, b)
                    beside(b)
                    if s:
                        exponentials(L, *s, b)

            def from_back(L, i, k):
                wait(act, L.back_full, i * L.NB + k + 1)

            def keep_inverse(L, i):
                from_back(L, i, 0)
                act.activation(exp_invT[:, :], back_bank[0:HEADS, 0:2 * P], ACT.Copy).then_inc(L.back_free, 1)

            def keep_spread(L, i):
                from_back(L, i, 1)
                wait(act, L.mix_done, i)
                act.activation(inv_rows[:, :, :], back_bank[:, :].rearrange("p (c n) -> p c n", c=DC), ACT.Copy).then_inc(L.back_free, 1)

            def keep_ffn_inT(L, i):
                from_back(L, i, 3)
                src = back_bank[:, :].rearrange("p (c n) -> p c n", c=DC)
                act.activation(ffn_inT[:, :, :], src, ACT.Copy).then_inc(L.back_free, 1)

            def keep_for_shared(i):
                wait(act, L0.back_free, i * L0.NB + 4)
                act.activation(all_inT[:, :, bass.ts(i, 2 * P)], ffn_inT[:, :, :], ACT.Copy)

            def router_exp(L, i):
                wait(act, L.to_exp, i + 1)
                n = L.E if L is L0 else L.K
                act.activation(gate_p[:, :, 0:n], shifted[:, :, 0:n], ACT.Exp).then_inc(L.from_exp, 1)

            def pairs(L):
                def body(i):
                    now, before_, next_ = there(i, PAIRS), there(i - 1, PAIRS), there(i + 1, PAIRS)

                    def beside_first(b):
                        if b == 1 and there(i - 2, PAIRS) and L is L1:
                            router_exp(L1, i - 2)

                    def beside_second(b):
                        if b == SBANKS - 1:
                            if before_:
                                keep_ffn_inT(L, i - 1)
                            if next_ and L is L1:
                                keep_q(L1, i + 1)

                    step(L, (i, 0) if now else None, (i - 1, 1) if before_ else None, beside_first)
                    if now and L is L0:
                        keep_v(L0, i)
                    if before_:
                        keep_inverse(L, i - 1)
                    if next_ and L is L0:
                        keep_xT(i + 1)
                    if next_ and L is L1:
                        keep_normedT(L1, i + 1)
                    if now and L is L1:
                        keep_v(L1, i)
                    if before_:
                        keep_spread(L, i - 1)
                    if now:
                        step(L, (i, 1), (i, 0), beside_second)
                    else:
                        beside_second(SBANKS - 1)
                    if next_ and L is L0:
                        keep_normedT(L0, i + 1)
                    if before_ and L is L0:
                        router_exp(L0, i - 1)
                        keep_for_shared(i - 1)
                    if next_ and L is L0:
                        keep_q(L0, i + 1)
                    if next_:
                        keep_k(L, i + 1)

                if L is L0:
                    keep_xT(0)
                    act.wait_ge(const_d, 4)
                keep_normedT(L, 0)
                keep_q(L, 0)
                keep_k(L, 0)
                skewed_loop(act, PAIRS, 2, body)

            pairs(L0)

            def shared_silu(q):
                for j, (f, m) in enumerate(FT):
                    wait(act, sh_gu, 3 * q + j + 1)
                    wait(act, sh_hid, 3 * q + j - 2)
                    act.activation(silu[j][0:m, :], bank[GU[j]][0:m, :], ACT.Silu).then_inc(sh_silu, 1)

            for q in range(GROUPS_BEFORE):
                shared_silu(q)

            def round_b(i, u):
                e = 2 * i + u
                wait(act, e_gu, NFT * e)
                wait(act, ex_full, e + 1)
                for c in range(DC):
                    last = act.activation(rows_high[:, c, :], bank[c][:, 0:C0], ACT.Copy)
                last.then_inc(rows_rounded, 1)
                wait(act, ew_in[u], 32 * (i + 1))
                for w, src in enumerate((gate_w[u], up_w[u])):
                    act.activation(gate_up_high[:, w, :, :], src, ACT.Copy).then_inc(gate_up_rounded, 1)

            def experts_b(i, first, last):
                for u in range(2):
                    e = 2 * i + u
                    for j, (f, m) in enumerate(FT):
                        s = (NFT * u + j) % 2
                        wait(act, e_gu, NFT * e + j + 1)
                        wait(act, e_hid, NFT * e + j - 1)
                        act.activation(silu[s][0:m, 0:C0], bank[2 + 2 * s][0:m, 0:C0], ACT.Silu).then_inc(e_silu, 1)
                    if u == 0:
                        round_b(i, 1)
                    elif not last:
                        round_b(i + 1, 0)

            round_b(0, 0)
            loop(act, NE0 // 2, experts_b)
            for q in range(GROUPS_BEFORE, GROUPS):
                shared_silu(q)

            pairs(L1)
            act.wait_ge(h_final, 16)

            def experts_d(i, first, last):
                for u in range(RING1):
                    e = RING1 * i + u
                    wait(act, dy_full, e - 1)
                    wait(act, dw2_in[u], 16 * (i + 1))
                    for half in range(2):
                        wait(act, dh_full, 2 * e + half + 1)
                        for jj in range(J1 // 2):
                            j = half * (J1 // 2) + jj
                            last_ = act.activation(dhidT[:, u % 2, j, :], bank[2 + 2 * (u % 2) + half][:, jj * P:(jj + 1) * P],
                                                   ACT.Gelu, bias=b1T[:, j, bass.ds(e, 1)])
                        last_.then_inc(dh_done, 1)
                        rows = slice(half * (J1 // 2), (half + 1) * (J1 // 2))
                        act.activation(w2_high[:, u % 2, rows, :], w2_sb[u][:, rows, :], ACT.Copy).then_inc(w2_rounded, 1)

            loop(act, NE1 // RING1, experts_d)

        @block.vector
        def _(dve):
            places = [conv_wT[:, 2 * k:2 * k + 2, :] for k in range(2)] + [wT0[:, w, :, :] for w in range(4)] + [b1T[:, :, :]]

            def keep_weights(first, end):
                for n in range(first, end):
                    dve.wait_ge(prep_full, n + 1)
                    dve.tensor_copy(places[n], prep_bank[n % len(prep_bank)][:, :].rearrange("p (a b) -> p a b", a=places[n].shape[1])).then_inc(prep_free, 1)

            keep_weights(0, 2)

            dve.memset(v_wide[:, :, :], 0.0).then_inc(const_d, 1)
            dve.memset(ones_b[:, :], 1.0)
            dve.wait_ge(const_p, 19)
            dve.tensor_scalar(row_id[:, 1:2], row_id[:, 0:1], HD.bit_length() - 1, 1, ALU.logical_shift_right,
                              ALU.bitwise_and).then_inc(const_d, 1)
            dve.wait_ge(const_d, 2)
            dve.tensor_copy(row_f[:, :], row_id[:, 1:2]).then_inc(const_d, 1)
            dve.wait_ge(const_d, 3)
            dve.tensor_scalar(parity[:, 0:1], row_f[:, :], -SCALE, SCALE, ALU.mult, ALU.add)
            dve.tensor_scalar(parity[:, 1:2], row_f[:, :], SCALE, None, ALU.mult).then_inc(const_d, 1)

            def ln_stats(L, w, i, src):
                settle(dve, i)
                for t in range(2):
                    last = dve.bn_stats(stats[:, w, t, :], src(t))
                last.then_inc(L.stat_steps[w], 1)
                wait(dve, L.stat_steps[w], i + 1)
                settle(dve, i)
                for t in range(2):
                    last = dve.bn_aggr(moments[:, w, t, :], stats[:, w, t, :])
                last.then_inc(L.moments_ready[w], 1)

            def ln_apply(L, w, i, src, dst, done):
                wait(dve, L.rstd_ready[w], i + 1)
                wait(dve, L.moments_ready[w], i + 1)
                for t in range(2):
                    last = dve.tensor_scalar(dst(t), src(t), moments[:, w, t, 0:1], rstd[:, w, t:t + 1],
                                             ALU.subtract, ALU.mult)
                last.then_inc(done, 1)

            def h_tile(i):
                return lambda t: h[:, bass.ds(2 * i + t, 1), :].rearrange("p a d -> p (a d)")

            def mix_tokens(i, first):
                wait(dve, L0.x_summed, i + 1)
                if first:
                    dve.wait_ge(dense_in, 48)
                for t in range(2):
                    b, n = front(L0, i, 2 + t)
                    wait(dve, L0.front_full[b], n + 1)
                    dve.scalar_tensor_tensor(out=tok[:, t, :], in0=x_sum[:, t, :], scalar=0.5, in1=front_bank[b][:, 0:D],
                                             op0=ALU.mult, op1=ALU.add).then_inc(L0.front_free[b], 1)
                for t in range(2):
                    b, n = front(L0, i, 2 + t)
                    wait(dve, L0.front_free[b], n + 1)
                    dve.tensor_tensor(tok[:, t, :], tok[:, t, :], conv_b[:, :], ALU.add).then_inc(L0.tok_biased, 1)
                wait(dve, L0.tok_biased, 2 * i + 2)
                ln_stats(L0, 2, i, lambda t: tok[:, t, :])

            def front_a(L, i, first):
                if L is L0:
                    mix_tokens(i, first)
                else:
                    ln_stats(L1, 0, i, h_tile(i))

            def front_b(i):
                ln_apply(L0, 2, i, lambda t: tok[:, t, :], lambda t: tok[:, t, :], L0.tok_normed)

            def front_c(i):
                wait(dve, L0.h_ready, i + 1)
                ln_stats(L0, 0, i, h_tile(i))

            def front_d(L, i):
                b, n = front(L, i - 1, L.KF)
                wait(dve, L.front_full[b], n + 1)
                ln_apply(L, 0, i, h_tile(i), lambda t: normed[:, t, :], L.normed_ready)

            def greatest(L, i, t, b):
                if b == 0:
                    wait(dve, L.turn_full, 8 * i + 4 * t - 4)
                wait(dve, L.score_full, 8 * i + 4 * t + b + 1)
                settle(dve, i)
                for j in range(HEADS_PER_BANK):
                    hd = head(b, j)
                    last = dve.tensor_tensor_reduce(probs[:, t, hd, :], score_bank[b % 2][:, j * P:(j + 1) * P],
                                                    L.mask[:, :], -1.0, 3e38, ALU.add, ALU.min,
                                                    neg_max[:, t, hd:hd + 1])
                last.then_inc(L.max_done, 1)

            def invert(L, i, t):
                wait(dve, L.exp_done, 8 * i + 4 * t + 4)
                wait(dve, L.back_full, (i - 1) * L.NB + 1)
                dve.reciprocal(exp_inv[:, t, :], exp_sum[:, t, :]).then_inc(L.inv_done, 1)

            def normalise(L, i):
                wait(dve, L.pv_done, 8 * i + 8)
                wait(dve, L.back_free, i * L.NB + 2)
                dve.tensor_tensor(mixedT[:, :, :], mix_bank[:, :].rearrange("p (c n) -> p c n", c=DC),
                                  inv_rows[:, :, :], ALU.mult).then_inc(L.mix_done, 1)

            def residual(L, i):
                wait(dve, L.back_full, i * L.NB + 3)
                hp = h[:, bass.ts(i, 2), :]
                dve.tensor_tensor(hp, hp, back_bank[:, :].rearrange("p (t d) -> p t d", t=2), ALU.add).then_inc(L.back_free, 1)

            def residual_stats(L, i):
                wait(dve, L.back_free, i * L.NB + 3)
                ln_stats(L, 1, i, h_tile(i))

            def expert_input(L, i):
                wait(dve, L.scattered, 16 * 2 * L.K * i)
                if L is L0:
                    wait(dve, L.input_added, i)
                ln_apply(L, 1, i, h_tile(i), lambda t: ffn_in[:, t, 0:D], L.ffn_ready)

            def choose(L, i):
                E, K = L.E, L.K
                chain = Chain(dve, L.route_steps, i, ROUTE_STEPS[L.n])
                wait(dve, L.back_full, i * L.NB + 5)
                wait(dve, L.scatter_ready, i)
                lg = logits[:, :, 0:E]
                dve.tensor_tensor(lg, back_bank[:, 0:2 * E].rearrange("p (t e) -> p t e", t=2),
                                  over(L.rb[:, 0:E], 1, [P, 2, E]), ALU.add).then_inc(L.back_free, 1)
                wait(dve, L.back_free, i * L.NB + 5)
                if L is L0:
                    chain.link(dve.tensor_reduce(rsmall[:, 0, :], lg, AX.X, ALU.max))
                    dve.tensor_tensor(shifted[:, :, 0:E], lg, over(rsmall[:, 0, :], 2, [P, 2, E]), ALU.subtract).then_inc(L.to_exp, 1)
                    wait(dve, L.from_exp, i + 1)
                    chain.link(dve.tensor_reduce(rsmall[:, 1, :], gate_p[:, :, 0:E], AX.X, ALU.add))
                    chain.link(dve.reciprocal(rsmall[:, 2, :], rsmall[:, 1, :]))
                    chain.link(dve.tensor_tensor(lg, gate_p[:, :, 0:E], over(rsmall[:, 2, :], 2, [P, 2, E]), ALU.mult))
                settle(dve, i)
                for t in range(2):
                    last = dve.max(top_v[:, t, :], logits[:, t, 0:E])
                chain.link(last)
                settle(dve, i)
                for t in range(2):
                    last = dve.max_index(top_i[:, t, :], top_v[:, t, :], logits[:, t, 0:E])
                chain.link(last)
                chain.link(dve.tensor_copy(top_f[:, :, :], top_i[:, :, :]))
                for k in range(K):
                    last = dve.tensor_tensor(onehot[:, k, :, 0:E], over(iota_e[:, 0:E], 1, [P, 2, E]),
                                             top_f[:, :, k:k + 1].to_broadcast([P, 2, E]), ALU.is_equal)
                chain.link(last)
                ch = chosen[:, :, 0:E]
                if K == 2:
                    chain.link(dve.tensor_tensor(ch, onehot[:, 0, :, 0:E], onehot[:, 1, :, 0:E], ALU.add))
                else:
                    chain.link(dve.tensor_tensor(product[:, 0, :, 0:E], onehot[:, 0, :, 0:E], onehot[:, 1, :, 0:E], ALU.add))
                    chain.link(dve.tensor_tensor(ch, product[:, 0, :, 0:E], onehot[:, 2, :, 0:E], ALU.add))
                dve.tensor_copy(earlier[:, 0, 0:E], running[:, 0:E])
                chain.link(dve.tensor_tensor(earlier[:, 1, 0:E], running[:, 0:E], chosen[:, 0, 0:E], ALU.add))
                dve.tensor_tensor(running[:, 0:E], earlier[:, 1, 0:E], chosen[:, 1, 0:E], ALU.add).then_inc(L.chosen_ready, 1)
                chain.end()

            def less_greatest(i):
                wait(dve, L1.chosen_ready, i + 1)
                dve.tensor_tensor(shifted[:, :, 0:K1], top_v[:, :, 0:K1], top_v[:, :, 0:1].to_broadcast([P, 2, K1]),
                                  ALU.subtract).then_inc(L1.to_exp, 1)

            def weigh(L, i):
                K = L.K
                chain = Chain(dve, L.weight_steps, i, WEIGHT_STEPS[L.n])
                if L is L0:
                    vals = top_v[:, :, 0:K]
                    chain.link(dve.tensor_tensor(rsmall[:, 3, :], top_v[:, :, 0], top_v[:, :, 1], ALU.add))
                    chain.link(dve.tensor_scalar(rsmall[:, 4, :], rsmall[:, 3, :], GATE_SUM_EPS, None, ALU.add))
                else:
                    wait(dve, L.from_exp, i + 1)
                    vals = gate_p[:, :, 0:K]
                    chain.link(dve.tensor_reduce(rsmall[:, 4, :], vals, AX.X, ALU.add))
                chain.link(dve.reciprocal(rsmall[:, 5, :], rsmall[:, 4, :]))
                chain.link(dve.tensor_tensor(weight[:, 0:K, :], vals.rearrange("p t k -> p k t"),
                                             over(rsmall[:, 5, :], 1, [P, K, 2]), ALU.mult))
                chain.end()

            def place(L, i):
                E, K, C = L.E, L.K, L.C
                chain = Chain(dve, L.slot_steps, i, SLOT_STEPS[L.n])
                wait(dve, L.back_full, i * L.NB + 6)
                dve.tensor_copy(count_sb[:, :, 0:E], back_bank[:, 0:2 * E].rearrange("p (t e) -> p t e", t=2)).then_inc(L.back_free, 1)
                wait(dve, L.back_free, i * L.NB + 6)
                for k in range(K):
                    last = dve.tensor_tensor(product[:, k, :, 0:E], onehot[:, k, :, 0:E], count_sb[:, :, 0:E], ALU.mult)
                chain.link(last)
                chain.link(dve.tensor_reduce(posf[:, 0:K, :], product[:, 0:K, :, 0:E], AX.X, ALU.add))
                dve.tensor_scalar(validf[:, 0:K, :], posf[:, 0:K, :], float(C), None, ALU.is_lt)
                chain.link(dve.tensor_scalar(tmpf[:, 0:K, :], posf[:, 0:K, :], float(C - 1), None, ALU.min))
                chain.link(dve.scalar_tensor_tensor(out=slotf[:, 0:K, :], in0=top_f[:, :, 0:K].rearrange("p t k -> p k t"),
                                                    scalar=float(C), in1=tmpf[:, 0:K, :], op0=ALU.mult, op1=ALU.add))
                chain.link(dve.tensor_scalar(tmpf[:, 0:K, :], validf[:, 0:K, :], -float(SKIP), float(SKIP), ALU.mult, ALU.add))
                dve.tensor_copy(ffn_in[:, :, CODE], code[:, bass.ts(i, 2)])
                dve.tensor_copy(ffn_in[:, :, EXPERT:EXPERT + K], top_f[:, :, 0:K])
                dve.tensor_copy(ffn_in[:, :, WEIGHT:WEIGHT + K].rearrange("p t k -> p k t"), weight[:, 0:K, :])
                dve.tensor_tensor(scatter_i[:, 0:K, :], slotf[:, 0:K, :], tmpf[:, 0:K, :], ALU.add).then_inc(L.scatter_ready, 1)
                chain.end()

            def first_pair(L):
                dve.memset(running[:, :], 0.0).then_inc(L.running_zero, 1)
                dve.wait_ge(L.running_zero, 1)
                front_a(L, 0, True)
                if L is L0:
                    keep_weights(2, 4)
                    front_b(0)
                    keep_weights(4, len(places))
                    front_c(0)
                front_d(L, 0)

            def pairs(L):
                def body(i):
                    now, before_, next_ = there(i, PAIRS), there(i - 1, PAIRS), there(i + 1, PAIRS)
                    if now:
                        if before_:
                            invert(L, i - 1, 1)
                        greatest(L, i, 0, 0)
                    if there(i - 2, PAIRS) and L is L1:
                        less_greatest(i - 2)
                    if now:
                        greatest(L, i, 0, 1)
                    if now and next_ and L is L1:
                        front_a(L1, i + 1, False)
                    if there(i - 2, PAIRS) and L is L1:
                        weigh(L1, i - 2)
                    if not now and there(i - 2, PAIRS):
                        place(L, i - 2)
                    if not now and before_:
                        invert(L, i - 1, 1)
                    if now:
                        greatest(L, i, 0, 2)
                        greatest(L, i, 0, 3)
                    if next_ and L is L1:
                        front_d(L1, i + 1)
                    if now and there(i - 2, PAIRS):
                        place(L, i - 2)
                    if before_:
                        normalise(L, i - 1)
                    if next_ and L is L0:
                        front_a(L0, i + 1, False)
                    if before_:
                        residual(L, i - 1)
                    if now:
                        invert(L, i, 0)
                        greatest(L, i, 1, 0)
                    if before_:
                        residual_stats(L, i - 1)
                    if next_ and L is L0:
                        front_b(i + 1)
                    if now:
                        greatest(L, i, 1, 1)
                        greatest(L, i, 1, 2)
                    if before_:
                        expert_input(L, i - 1)
                    if next_ and L is L0:
                        front_c(i + 1)
                    if now:
                        greatest(L, i, 1, 3)
                    if next_ and L is L0:
                        front_d(L0, i + 1)
                    if before_:
                        choose(L, i - 1)
                    if before_ and L is L0:
                        weigh(L0, i - 1)

                skewed_loop(dve, PAIRS, 2, body)

            first_pair(L0)
            dve.wait_ge(router_in, 16 * ROUTER_LOADS)
            pairs(L0)

            dve.wait_ge(L0.input_added, PAIRS)

            def shared_mlp(q):
                for j, (f, m) in enumerate(FT):
                    wait(dve, sh_silu, 3 * q + j + 1)
                    wait(dve, sh_y, 2 * q)
                    dve.tensor_tensor(shT[0:m, j, :], silu[j][0:m, :], bank[GU[j] + 1][0:m, :], ALU.mult).then_inc(sh_hid, 1)
                if q == GROUPS_BEFORE:
                    dve.wait_ge(h_loaded, 16)
                    dve.wait_ge(h_loaded_rest, 16)
                for half in range(2):
                    wait(dve, sh_y, 2 * q + half + 1)
                    hp = h[:, bass.ds(4 * q + 2 * half, 2), :]
                    dve.tensor_tensor(hp, hp, bank[6 + half][:, :].rearrange("p (t d) -> p t d", t=2), ALU.add).then_inc(sh_add, 1)

            for q in range(GROUPS_BEFORE):
                shared_mlp(q)

            def slots(rows, buf, e, steps, added, done):
                ns = rows.shape[1]
                chain = Chain(dve, steps, e, 2)
                wait(dve, added[0], added[1])
                match, empty = slot_match[:, buf, 0:ns, :], slot_empty[:, buf, 0:ns]
                dve.tensor_scalar(match, rows[:, :, EXPERT:EXPERT + K1], iota_e[:, bass.ds(e, 1)], None, ALU.is_equal)
                chain.link(dve.scalar_tensor_tensor(out=empty, in0=rows[:, :, CODE], scalar=0.0, in1=empty_row[:, 0:ns],
                                                    op0=ALU.is_equal, op1=ALU.mult))
                dve.scalar_tensor_tensor(out=slot_token[:, buf, 0:ns], in0=rows[:, :, CODE], scalar=-1.0, in1=empty,
                                         op0=ALU.add, op1=ALU.add)
                chain.link(dve.tensor_tensor(match, match, rows[:, :, WEIGHT:WEIGHT + K1], ALU.mult))
                dve.tensor_reduce(slot_gate[:, buf, 0:ns], match, AX.X, ALU.add).then_inc(done, 1)
                chain.end()

            def slots_b(i, u):
                e = 2 * i + u
                wait(dve, er_in[u], 32 * (i + 1))
                slots(erows[:, u, :, :], u, e, slot_steps, (e_added, 16 * NCT * (e - 1)), e_slots)

            def split_rows_b(i, u):
                e = 2 * i + u
                wait(dve, rows_rounded, e + 1)
                wait(dve, e_gu, NFT * e)
                for c in range(DC):
                    last = split(dve, rows_high[:, c, :], rows_low[:, c, :], bank[c][:, 0:C0])
                last.then_inc(ex_free, 1)

            def split_gate_b(i, u):
                e = 2 * i + u
                wait(dve, gate_up_rounded, 2 * e + 1)
                split(dve, gate_up_high[:, 0, :, :], gate_up_low[:, 0, :, :], gate_w[u]).then_inc(gate_split, 1)

            def hidden_b(i, u, before_last):
                e = 2 * i + u
                for j, (f, m) in enumerate(FT):
                    s = (NFT * u + j) % 2
                    if j == NFT - 1:
                        before_last()
                    wait(dve, e_silu, NFT * e + j + 1)
                    wait(dve, e_y, NCT * (e - 1))
                    dve.tensor_tensor(hidT[u][0:m, j, :], silu[s][0:m, 0:C0], bank[3 + 2 * s][0:m, 0:C0], ALU.mult).then_inc(e_hid, 1)

            def result_b(i, u, s):
                e = 2 * i + u
                r, m = CT[s]
                wait(dve, e_added, 16 * NCT * (e - 1))
                wait(dve, e_slots, e + 1)
                wait(dve, e_y, NCT * e + s + 1)
                dve.tensor_scalar(yrows[u][0:m, s, :], bank[6 + (NCT * u + s) % 2][0:m, 0:D],
                                  slot_gate[0:m, u, s:s + 1], None, ALU.mult).then_inc(e_yfree, 1)

            def experts_b(i, first, last):
                for u in range(2):
                    if u == 0:
                        hidden_b(i, 1, lambda: slots_b(i, 1))
                    elif not last:
                        hidden_b(i + 1, 0, lambda: slots_b(i + 1, 0))
                    result_b(i, u, 0)
                    if not last:
                        split_rows_b(i + 1, u)
                    result_b(i, u, 1)
                    if not last:
                        split_gate_b(i + 1, u)
                    result_b(i, u, 2)

            for u in range(2):
                split_rows_b(0, u)
                split_gate_b(0, u)
                if u == 0:
                    hidden_b(0, 0, lambda: slots_b(0, 0))
            loop(dve, NE0 // 2, experts_b)
            for q in range(GROUPS_BEFORE, GROUPS):
                shared_mlp(q)
                if q == GROUPS_BEFORE:
                    first_pair(L1)

            pairs(L1)
            def keep_rows_d(i, v_):
                i, u = later(i, v_)
                e = RING1 * i + u
                wait(dve, dx_full, e + 1)
                wait(dve, dh_full, 2 * e - 2)
                dve.tensor_copy(drowsT[:, u % 2, :, :], bank[u % 2][:, 0:D].rearrange("p (c n) -> p c n", c=DC)).then_inc(dx_free, 1)

            def slots_d(i, v_):
                i, u = later(i, v_)
                e = RING1 * i + u
                wait(dve, dr_in[u], 16 * (i + 1))
                slots(drows[:, u:u + 1, :], u, e, d_steps, (d_added, 16 * (e - RING1 + 1)), d_slots)

            def split_w2(i, v_, half):
                i, u = later(i, v_)
                e = RING1 * i + u
                wait(dve, w2_rounded, 2 * e + half + 1)
                rows = slice(half * (J1 // 2), min((half + 1) * (J1 // 2), W2_DVE))
                split(dve, w2_high[:, u % 2, rows, :], w2_low[:, u % 2, rows, :], w2_sb[u][:, rows, :]).then_inc(w2_split_dve, 1)

            def split_hidden(i, v_, half):
                i, u = later(i, v_)
                e = RING1 * i + u
                wait(dve, dh_done, 2 * e + half + 1)
                rows = slice(half * (J1 // 2), (half + 1) * (J1 // 2))
                dve.tensor_copy(hidden_high[:, u % 2, rows, :], dhidT[:, u % 2, rows, :]).then_inc(hid_rounded, 1)
                wait(dve, hid_rounded, 2 * e + half + 1)
                split(dve, hidden_high[:, u % 2, rows, :], hidden_low[:, u % 2, rows, :], dhidT[:, u % 2, rows, :]).then_inc(hid_split, 1)

            def choose_b2(i, v_):
                i, u = later(i, v_)
                e = RING1 * i + u
                wait(dve, dy_full, e - 1)
                dve.tensor_copy(chooser[:, u % 2, :], ident[0:NE1, bass.ds(e, 1)].to_broadcast([NE1, P])).then_inc(chooser_ready, 1)

            def result_d(i, u):
                e = RING1 * i + u
                wait(dve, d_slots, e + 1)
                wait(dve, dy_full, e + 1)
                wait(dve, d_added, 16 * (e - 1))
                dve.tensor_scalar(dy[:, u % 2, :], bank[6 + u % 2][:, 0:D], slot_gate[:, u, 0:1], None,
                                  ALU.mult).then_inc(dy_free, 1)

            def experts_d(i, first, last):
                for u in range(RING1):
                    split_hidden(i, u, 1)
                    split_w2(i, u, 1)
                    if not (last and u + 2 >= RING1):
                        keep_rows_d(i, u + 2)
                    if not (last and u + 1 >= RING1):
                        split_hidden(i, u + 1, 0)
                        split_w2(i, u + 1, 0)
                        choose_b2(i, u + 1)
                        slots_d(i, u + 1)
                    result_d(i, u)

            keep_rows_d(0, 0)
            keep_rows_d(0, 1)
            dve.wait_ge(b2_in, 16)
            dve.wait_ge(h_final, 16)
            dve.tensor_copy(b2_high[:, :], b2_raw).then_inc(b2_rounded, 1)
            dve.wait_ge(b2_rounded, 1)
            split(dve, b2_high[:, :], b2_low[:, :], b2_raw).then_inc(b2_split, 1)
            split_hidden(0, 0, 0)
            split_w2(0, 0, 0)
            choose_b2(0, 0)
            slots_d(0, 0)
            loop(dve, NE1 // RING1, experts_d)


NAMES = ["x", "L0_tok_conv_w", "L0_tok_conv_b", "L0_tok_ln_gamma", "L0_tok_ln_beta", "L0_attn_Wq", "L0_attn_Wk",
         "L0_attn_Wv", "L0_attn_Wo", "L0_ffn_router_w", "L0_ffn_router_b", "L0_ffn_w_gate", "L0_ffn_w_up",
         "L0_ffn_w_down", "L0_ffn_sw_gate", "L0_ffn_sw_up", "L0_ffn_sw_down", "L1_attn_w_qkv", "L1_attn_w_out",
         "L1_ffn_gate_w", "L1_ffn_gate_b", "L1_ffn_w1", "L1_ffn_b1", "L1_ffn_w2", "L1_ffn_b2"]


def kernel(**inputs):
    import numpy as np
    from concourse import bacc
    from concourse.bass_utils import run_bass_kernel_spmd

    nc = bacc.Bacc("TRN2", target_bir_lowering=False, num_devices=1)
    arrays = {name: np.ascontiguousarray(inputs[name]) for name in NAMES}
    a = {name: nc.dram_tensor(name, arrays[name].shape, F32, kind="ExternalInput").ap() for name in NAMES}
    b, tokens, d = arrays["x"].shape
    out = nc.dram_tensor("out", [b, tokens // 2, d], F32, kind="ExternalOutput").ap()
    build(nc, a, out)
    return run_bass_kernel_spmd(nc, [arrays], core_ids=[0]).results[0]["out"]
```
